# Optimizing a Trainium2 kernel written in Bass

```python
import numpy as np
import jax
import jax.numpy as jnp

def _softmax(x, axis=-1):
    return jax.nn.softmax(x, axis=axis)
def _gelu(x):
    return jax.nn.gelu(x, approximate=True)
def _silu(x):
    return jax.nn.silu(x)
def _sigmoid(x):
    return jax.nn.sigmoid(x)
def _layernorm(x, axis=-1, eps=1e-5):
    m = jnp.mean(x, axis=axis, keepdims=True)
    v = jnp.var(x, axis=axis, keepdims=True)
    return (x - m) / jnp.sqrt(v + eps)
def _scatter_add(tgt, idx, src, axis=0):
    return tgt.at[idx].add(src)
def _segment_sum(src, seg, n):
    return jax.ops.segment_sum(src, seg, n)

kernel_name = 'mk_conv_attn_hybrid_d2_conv_nhwc256_76ab5a'

def setup_inputs(seed: int = 0):
    np.random.seed(seed)
    _w = jnp.asarray
    def _rec_inputs():
        import jax
        import jax.numpy as jnp
        _gk = jax.random.key(seed)
        x = -0.0005207 + 1.001 * jax.random.normal(jax.random.fold_in(_gk, 1), (2, 64, 64, 256), jnp.float32)
        return x
    x = _rec_inputs()
    def _L0_conv_setup():
        import jax, jax.numpy as jnp
        import numpy as np
        B, N, D, H = (2, 64, 256, 8)
        DK = D // H
        EPS = 1e-05

        def layer_norm(x, g, b):
            mu = jnp.mean(x, axis=-1, keepdims=True)
            var = jnp.var(x, axis=-1, keepdims=True)
            return (x - mu) * jax.lax.rsqrt(var + EPS) * g + b
        key = jax.random.key(seed)
        ks = jax.random.split(key, 12)
        s = 1.0 / np.sqrt(D)
        inp = {'x': jax.random.normal(ks[0], (B, N, N, D), jnp.float32), 'W_lk': jax.random.uniform(ks[1], (D, D), jnp.float32, -s, s), 'W_rk': jax.random.uniform(ks[2], (D, D), jnp.float32, -s, s), 'W_lv': jax.random.uniform(ks[3], (D, D), jnp.float32, -s, s), 'W_rv': jax.random.uniform(ks[4], (D, D), jnp.float32, -s, s), 'W_out': jax.random.uniform(ks[5], (D, D), jnp.float32, -s, s), 'ln_agg_g': jnp.ones((D,), jnp.float32), 'ln_agg_b': jnp.zeros((D,), jnp.float32), 'W1': jax.random.uniform(ks[6], (D, 2 * D), jnp.float32, -s, s), 'b1': jnp.zeros((2 * D,), jnp.float32), 'W2': jax.random.uniform(ks[7], (2 * D, D), jnp.float32, -1.0 / np.sqrt(2 * D), 1.0 / np.sqrt(2 * D)), 'b2': jnp.zeros((D,), jnp.float32), 'ln2_g': jnp.ones((D,), jnp.float32), 'ln2_b': jnp.zeros((D,), jnp.float32)}
        return inp
    _L0_conv_all = _L0_conv_setup()
    _L0_conv_in = {k: v for k, v in _L0_conv_all.items() if k in ('W_lk', 'W_rk', 'W_lv', 'W_rv', 'W_out', 'ln_agg_g', 'ln_agg_b', 'W1', 'b1', 'W2', 'b2', 'ln2_g', 'ln2_b', )}
    del _L0_conv_all

    def _L1_attn_setup():
        import jax, jax.numpy as jnp
        import numpy as np
        B, S, D = (4, 4096, 256)
        key = jax.random.key(seed)
        ks = jax.random.split(key, 7)
        scale = 1.0 / np.sqrt(D)
        return {'x': jax.random.normal(ks[0], (B, S, D), dtype=jnp.float32), 'Wq': jax.random.normal(ks[1], (D, D), dtype=jnp.float32) * scale, 'bq': jax.random.normal(ks[2], (D,), dtype=jnp.float32) * scale, 'Wk': jax.random.normal(ks[3], (D, D), dtype=jnp.float32) * scale, 'bk': jax.random.normal(ks[4], (D,), dtype=jnp.float32) * scale, 'Wv': jax.random.normal(ks[5], (D, D), dtype=jnp.float32) * scale, 'bv': jax.random.normal(ks[6], (D,), dtype=jnp.float32) * scale}
    _L1_attn_all = _L1_attn_setup()
    _L1_attn_in = {k: v for k, v in _L1_attn_all.items() if k in ('Wq', 'bq', 'Wk', 'bk', 'Wv', 'bv', )}
    del _L1_attn_all

    def _L1_ffn_setup():
        import jax, jax.numpy as jnp
        import numpy as np
        from jax import lax
        key = jax.random.key(seed)
        B, T, I, H = (64, 2048, 256, 256)
        ks = jax.random.split(key, 13)
        s = 1.0 / np.sqrt(H)

        def w(k, shape):
            return jax.random.uniform(k, shape, jnp.float32, -s, s)
        return {'x': jax.random.normal(ks[0], (B, T, I), jnp.float32), 'U_i': w(ks[1], (I, H)), 'V_i': w(ks[2], (H, H)), 'b_i': w(ks[3], (H,)), 'U_f': w(ks[4], (I, H)), 'V_f': w(ks[5], (H, H)), 'b_f': w(ks[6], (H,)), 'U_c': w(ks[7], (I, H)), 'V_c': w(ks[8], (H, H)), 'b_c': w(ks[9], (H,)), 'U_o': w(ks[10], (I, H)), 'V_o': w(ks[11], (H, H)), 'b_o': w(ks[12], (H,))}
    _L1_ffn_all = _L1_ffn_setup()
    _L1_ffn_in = {k: v for k, v in _L1_ffn_all.items() if k in ('U_i', 'V_i', 'b_i', 'U_f', 'V_f', 'b_f', 'U_c', 'V_c', 'b_c', 'U_o', 'V_o', 'b_o', )}
    del _L1_ffn_all

    return {
        "x": x,
        "L0_conv_W_lk": _L0_conv_in["W_lk"],
        "L0_conv_W_rk": _L0_conv_in["W_rk"],
        "L0_conv_W_lv": _L0_conv_in["W_lv"],
        "L0_conv_W_rv": _L0_conv_in["W_rv"],
        "L0_conv_W_out": _L0_conv_in["W_out"],
        "L0_conv_ln_agg_g": _L0_conv_in["ln_agg_g"],
        "L0_conv_ln_agg_b": _L0_conv_in["ln_agg_b"],
        "L0_conv_W1": _L0_conv_in["W1"],
        "L0_conv_b1": _L0_conv_in["b1"],
        "L0_conv_W2": _L0_conv_in["W2"],
        "L0_conv_b2": _L0_conv_in["b2"],
        "L0_conv_ln2_g": _L0_conv_in["ln2_g"],
        "L0_conv_ln2_b": _L0_conv_in["ln2_b"],
        "L1_attn_Wq": _L1_attn_in["Wq"],
        "L1_attn_bq": _L1_attn_in["bq"],
        "L1_attn_Wk": _L1_attn_in["Wk"],
        "L1_attn_bk": _L1_attn_in["bk"],
        "L1_attn_Wv": _L1_attn_in["Wv"],
        "L1_attn_bv": _L1_attn_in["bv"],
        "L1_ffn_U_i": _L1_ffn_in["U_i"],
        "L1_ffn_V_i": _L1_ffn_in["V_i"],
        "L1_ffn_b_i": _L1_ffn_in["b_i"],
        "L1_ffn_U_f": _L1_ffn_in["U_f"],
        "L1_ffn_V_f": _L1_ffn_in["V_f"],
        "L1_ffn_b_f": _L1_ffn_in["b_f"],
        "L1_ffn_U_c": _L1_ffn_in["U_c"],
        "L1_ffn_V_c": _L1_ffn_in["V_c"],
        "L1_ffn_b_c": _L1_ffn_in["b_c"],
        "L1_ffn_U_o": _L1_ffn_in["U_o"],
        "L1_ffn_V_o": _L1_ffn_in["V_o"],
        "L1_ffn_b_o": _L1_ffn_in["b_o"],
    }

def reference(x, L0_conv_W_lk, L0_conv_W_rk, L0_conv_W_lv, L0_conv_W_rv, L0_conv_W_out, L0_conv_ln_agg_g, L0_conv_ln_agg_b, L0_conv_W1, L0_conv_b1, L0_conv_W2, L0_conv_b2, L0_conv_ln2_g, L0_conv_ln2_b, L1_attn_Wq, L1_attn_bq, L1_attn_Wk, L1_attn_bk, L1_attn_Wv, L1_attn_bv, L1_ffn_U_i, L1_ffn_V_i, L1_ffn_b_i, L1_ffn_U_f, L1_ffn_V_f, L1_ffn_b_f, L1_ffn_U_c, L1_ffn_V_c, L1_ffn_b_c, L1_ffn_U_o, L1_ffn_V_o, L1_ffn_b_o):
    import jax
    import jax.numpy as jnp
    def _L0_conv_ref(x, W_lk, W_rk, W_lv, W_rv, W_out, ln_agg_g, ln_agg_b, W1, b1, W2, b2, ln2_g, ln2_b):
        import jax, jax.numpy as jnp
        import numpy as np
        B, N, D, H = (2, 64, 256, 8)
        DK = D // H
        EPS = 1e-05

        def layer_norm(x, g, b):
            mu = jnp.mean(x, axis=-1, keepdims=True)
            var = jnp.var(x, axis=-1, keepdims=True)
            return (x - mu) * jax.lax.rsqrt(var + EPS) * g + b
        b, n = (x.shape[0], x.shape[1])
        lk = (x @ W_lk).reshape(b, n, n, H, DK)
        rk = (x @ W_rk).reshape(b, n, n, H, DK)
        lv = (x @ W_lv).reshape(b, n, n, H, DK)
        rv = (x @ W_rv).reshape(b, n, n, H, DK)
        scores = jnp.einsum('bxahd,bayhd->bxayh', lk, rk) / np.sqrt(DK)
        att = jax.nn.softmax(scores, axis=2)
        o = jnp.einsum('bxayh,bxahd,bayhd->bxyhd', att, lv, rv)
        o = o.reshape(b, n, n, D) @ W_out
        h = layer_norm(x + o, ln_agg_g, ln_agg_b)
        m = jax.nn.relu(h @ W1 + b1) @ W2 + b2
        return layer_norm(m + h, ln2_g, ln2_b)

    def _L1_attn_ref(x, Wq, bq, Wk, bk, Wv, bv):
        import jax, jax.numpy as jnp
        import numpy as np
        B, S, D = (4, 4096, 256)
        q = jnp.einsum('bsd,ed->bse', x, Wq) + bq
        k = jnp.einsum('bsd,ed->bse', x, Wk) + bk
        v = jnp.einsum('bsd,ed->bse', x, Wv) + bv
        d = q.shape[-1]
        scores = jnp.einsum('bqd,bkd->bqk', q, k) / jnp.sqrt(jnp.asarray(d, q.dtype))
        w = jax.nn.softmax(scores, axis=2)
        out = jnp.einsum('bqk,bkd->bqd', w, v)
        return out

    def _L1_ffn_ref(x, U_i, V_i, b_i, U_f, V_f, b_f, U_c, V_c, b_c, U_o, V_o, b_o):
        import jax, jax.numpy as jnp
        import numpy as np
        from jax import lax
        B, T, _ = x.shape
        H = U_i.shape[1]
        xt = jnp.swapaxes(x, 0, 1)
        xi = xt @ U_i + b_i
        xf = xt @ U_f + b_f
        xg = xt @ U_c + b_c
        xo = xt @ U_o + b_o
        h0 = jnp.zeros((B, H), x.dtype)
        c0 = jnp.zeros((B, H), x.dtype)

        def step(carry, xs):
            h, c = carry
            xi_t, xf_t, xg_t, xo_t = xs
            i_t = jax.nn.sigmoid(xi_t + h @ V_i)
            f_t = jax.nn.sigmoid(xf_t + h @ V_f)
            g_t = jnp.tanh(xg_t + h @ V_c)
            o_t = jax.nn.sigmoid(xo_t + h @ V_o)
            c_new = h * c + i_t * g_t
            h_new = o_t * jnp.tanh(c_new)
            return ((h_new, c_new), h_new)
        (_, _), hs = lax.scan(step, (h0, c0), (xi, xf, xg, xo))
        return jnp.swapaxes(hs, 0, 1)

    def _gn(v, G=32, eps=1e-5):
        B_, H_, W_, C_ = v.shape
        g = v.reshape(B_, H_, W_, G, C_ // G)
        m = jnp.mean(g, axis=(1, 2, 4), keepdims=True)
        s = jnp.var(g, axis=(1, 2, 4), keepdims=True)
        return ((g - m) / jnp.sqrt(s + eps)).reshape(v.shape)

    def _ln_c(v, eps=1e-6):
        m = jnp.mean(v, axis=-1, keepdims=True)
        s = jnp.var(v, axis=-1, keepdims=True)
        return (v - m) / jnp.sqrt(s + eps)

    def _ln_t(v, eps=1e-5):
        m = jnp.mean(v, axis=-1, keepdims=True)
        s = jnp.var(v, axis=-1, keepdims=True)
        return (v - m) / jnp.sqrt(s + eps)

    def _to_tokens(v):
        B_, H_, W_, C_ = v.shape
        return v.reshape(B_, H_ * W_, C_)
    def _from_tokens(t, like):
        return t.reshape(like.shape)

    x = _L0_conv_ref(x, L0_conv_W_lk, L0_conv_W_rk, L0_conv_W_lv, L0_conv_W_rv, L0_conv_W_out, L0_conv_ln_agg_g, L0_conv_ln_agg_b, L0_conv_W1, L0_conv_b1, L0_conv_W2, L0_conv_b2, L0_conv_ln2_g, L0_conv_ln2_b)
    t = _to_tokens(x)
    t = t + _L1_attn_ref(_ln_t(t), L1_attn_Wq, L1_attn_bq, L1_attn_Wk, L1_attn_bk, L1_attn_Wv, L1_attn_bv)
    t = t + _L1_ffn_ref(_ln_t(t), L1_ffn_U_i, L1_ffn_V_i, L1_ffn_b_i, L1_ffn_U_f, L1_ffn_V_f, L1_ffn_b_f, L1_ffn_U_c, L1_ffn_V_c, L1_ffn_b_c, L1_ffn_U_o, L1_ffn_V_o, L1_ffn_b_o)
    x = _from_tokens(t, x)
    return x


_drawn_inputs = setup_inputs


def setup_inputs(seed=0):
    import zlib

    import numpy as np

    out = dict(_drawn_inputs(seed))
    spreads = {'L0_conv_ln_agg_g': (1.0, 0.2),
     'L0_conv_ln_agg_b': (0.0, 0.1),
     'L0_conv_b1': (0.0, 0.1),
     'L0_conv_b2': (0.0, 0.1),
     'L0_conv_ln2_g': (1.0, 0.2),
     'L0_conv_ln2_b': (0.0, 0.1)}
    factors = {'L0_conv_W_lk': 7.022,
     'L0_conv_W_rk': 6.983,
     'L1_attn_bq': 8.0,
     'L1_attn_bk': 64.0,
     'L1_ffn_V_i': 8.0,
     'L1_ffn_b_i': 23.175,
     'L1_ffn_V_c': 4.154,
     'L1_ffn_b_c': 7.472,
     'L1_ffn_V_o': 8.0,
     'L1_ffn_b_o': 21.738}
    for name, (base, spread) in spreads.items():
        noise = np.random.default_rng([zlib.crc32(name.encode()), seed]).standard_normal(out[name].shape)
        drawn = base * np.exp(spread * noise) if base else spread * noise
        out[name] = jnp.asarray(drawn.astype(out[name].dtype))
    for name, factor in factors.items():
        out[name] = (out[name] * factor).astype(out[name].dtype)
    return out
```

```python
from contextlib import ExitStack

import numpy as np

import concourse.bass as bass
from concourse import mybir

F32 = mybir.dt.float32
I32 = mybir.dt.int32
ALU = mybir.AluOpType
ACT = mybir.ActivationFunctionType
AX_X = mybir.AxisListType.X

P = 128
B, N, D = 2, 64, 256
H = 8
DK = D // H
G = 2
HG = H // G
T = N * N
KT = D // P
LN_EPS = 1e-5


class Phase:

    def __init__(self, nc, stack, name):
        self.nc, self.stack, self.name, self.sems = nc, stack, name, []
        stack.callback(self.clear)

    def clear(self):
        with self.nc.Block() as block:
            @block.sync
            def _(sp):
                for sem in self.sems:
                    sp.sem_clear(sem)

    def sb(self, name, shape, dtype=F32):
        return self.stack.enter_context(self.nc.sbuf_tensor(f"{self.name}_{name}", shape, dtype))

    def ps(self, name, shape):
        return self.stack.enter_context(self.nc.psum_tensor(f"{self.name}_{name}", shape, F32))

    def sem(self, name):
        self.sems.append(self.stack.enter_context(self.nc.semaphore(f"{self.name}_{name}")))
        return self.sems[-1]


HEAD = 32


def start_at_head(nc, sems):
    with nc.Block() as block:
        @block.sync
        def _(sp):
            for sem in sems:
                sp.sem_inc(sem, HEAD)


def k_rows(w):
    return w.rearrange("(k p) n -> p k n", p=P)


def scores_phase(nc, b, x, w_lk, w_rk, ident_d, att):
    with ExitStack() as stack:
        ph = Phase(nc, stack, f"sc{b}")
        ident = ph.sb("ident", [P, P])
        wlk = ph.sb("wlk", [P, KT, D])
        wrk = ph.sb("wrk", [P, KT, D])
        lkT = ph.sb("lkT", [P, G, T])
        rkT = ph.sb("rkT", [P, G, T])
        BLK = 512
        NBLK = T // BLK

        with ExitStack() as inner:
            pj = Phase(nc, inner, f"pj{b}")
            xin = pj.sb("xin", [P, 2, BLK // P, D])
            xT = pj.sb("xT", [P, 2, KT, BLK])
            psT = pj.ps("psT", [P, KT, BLK])
            psP = pj.ps("psP", [P, 2 * G, BLK])
            w_in = pj.sem("w_in")
            x_in = [pj.sem(f"x_in{s}") for s in range(2)]
            turned = pj.sem("turned")
            xT_done = pj.sem("xT_done")
            projected = pj.sem("projected")
            stored = pj.sem("stored")
            start_at_head(nc, [turned, xT_done, projected, stored])
            with nc.Block() as block:
                @block.sync
                def _(sp):
                    sp.dma_start(ident[:, :], ident_d).then_inc(w_in, 16)
                    sp.dma_start(wlk[:, :, :], k_rows(w_lk)).then_inc(w_in, 16)
                    sp.dma_start(wrk[:, :, :], k_rows(w_rk)).then_inc(w_in, 16)
                    xb = x[b].rearrange("x a d -> (x a) d")
                    with sp.Fori(0, NBLK // 2) as i:
                        for s in range(2):
                            n = i * 2 + s
                            sp.wait_ge(turned, HEAD + n - 1)
                            sp.dma_start(xin[:, s], xb[bass.ds(n * BLK, BLK), :].rearrange("(t p) d -> p t d", p=P)).then_inc(x_in[s], 16)

                @block.tensor
                def _(pe):
                    pe.wait_ge(w_in, 48)
                    with pe.Fori(0, NBLK // 2) as i:
                        for s in range(2):
                            n = i * 2 + s
                            pe.wait_ge(x_in[s], i * 16 + 16)
                            pe.wait_ge(xT_done, HEAD + n)
                            for k in range(KT):
                                for t in range(BLK // P):
                                    mm = pe.transpose(psT[:, k, t * P:(t + 1) * P], xin[:, s, t, k * P:(k + 1) * P], ident[:, :])
                            mm.then_inc(turned, 1)
                            pe.wait_ge(xT_done, HEAD + n + 1)
                            for j in range(2 * G):
                                w, g = (wlk, wrk)[j // G], j % G
                                pe.wait_ge(stored, HEAD + (n - 1) * (2 * G) + j + 1)
                                for k in range(KT):
                                    mm = pe.matmul(psP[:, j, :], w[:, k, g * P:(g + 1) * P], xT[:, s, k, :], start=(k == 0), stop=(k == KT - 1))
                                mm.then_inc(projected, 1)

                @block.scalar
                def _(act):
                    with act.Fori(0, NBLK // 2) as i:
                        for s in range(2):
                            n = i * 2 + s
                            act.wait_ge(turned, HEAD + n + 1)
                            act.wait_ge(projected, HEAD + (n - 1) * (2 * G))
                            nc.scalar.copy(xT[:, s], psT[:, :, :]).then_inc(xT_done, 1)

                @block.vector
                def _(dve):
                    with dve.Fori(0, NBLK // 2) as i:
                        for s in range(2):
                            n = i * 2 + s
                            for j in range(2 * G):
                                dst = (lkT, rkT)[j // G]
                                dve.wait_ge(projected, HEAD + n * (2 * G) + j + 1)
                                nc.vector.tensor_copy(dst[:, j % G, bass.ds(n * BLK, BLK)], psP[:, j, :]).then_inc(stored, 1)

        with ExitStack() as inner:
            sm = Phase(nc, inner, f"sm{b}")
            AB = 8
            NA = N // AB
            F = HG * N
            E = sm.sb("E", [P, N, F])
            lks = sm.sb("lks", [P, 2, G, AB, N])
            rks = sm.sb("rks", [P, 2, G, AB, N])
            part = sm.sb("part", [P, NA, F])
            top = sm.sb("top", [P, F])
            den = sm.sb("den", [P, F])
            rden = sm.sb("rden", [P, F])
            psS = sm.ps("psS", [P, 2, HG, AB * N])
            lk_cut = sm.sem("lk_cut")
            rk_cut = sm.sem("rk_cut")
            scored = sm.sem("scored")
            kept = sm.sem("kept")
            maxed = sm.sem("maxed")
            topped = sm.sem("topped")
            shifted = sm.sem("shifted")
            exped = sm.sem("exped")
            summed = sm.sem("summed")
            inverted = sm.sem("inverted")
            normed = sm.sem("normed")
            saved = sm.sem("saved")
            CH = 4
            CA = N // CH
            start_at_head(nc, [lk_cut, rk_cut, scored, kept, maxed])
            lk_v = lkT[:, :, :].rearrange("p g (x a) -> p g a x", a=N)
            rk_v = rkT[:, :, :].rearrange("p g (a y) -> p g a y", y=N)
            with nc.Block() as block:
                @block.gpsimd
                def _(pool):
                    with pool.Fori(0, NA // 2) as i:
                        for s in range(2):
                            n = i * 2 + s
                            pool.wait_ge(scored, HEAD + n - 1)
                            for g in range(G):
                                nc.gpsimd.tensor_copy(lks[:, s, g], lk_v[:, g, bass.ds(n * AB, AB), :]).then_inc(lk_cut, 1)

                @block.tensor
                def _(pe):
                    with pe.Fori(0, NA // 2) as i:
                        for s in range(2):
                            n = i * 2 + s
                            pe.wait_ge(lk_cut, HEAD + n * 2 + 2)
                            pe.wait_ge(rk_cut, HEAD + n * 2 + 2)
                            pe.wait_ge(kept, HEAD + n - 1)
                            for a in range(AB):
                                for g in range(G):
                                    for h in range(HG):
                                        r = slice(h * DK, (h + 1) * DK)
                                        mm = pe.matmul(psS[g * N:(g + 1) * N, s, h, a * N:(a + 1) * N], lks[r, s, g, a, :], rks[r, s, g, a, :],
                                                       start=True, stop=True, tile_position=(h * DK, g * N))
                            mm.then_inc(scored, 1)

                @block.scalar
                def _(act):
                    with act.Fori(0, NA // 2) as i:
                        for s in range(2):
                            n = i * 2 + s
                            act.wait_ge(scored, HEAD + n + 1)
                            nc.scalar.copy(E[:, bass.ds(n * AB, AB), :].rearrange("p a (h y) -> p h a y", h=HG),
                                           psS[:, s].rearrange("p h (a y) -> p h a y", a=AB)).then_inc(kept, 1)
                    for c in range(CH):
                        act.wait_ge(shifted, c + 1)
                        nc.scalar.activation(E[:, c * CA:(c + 1) * CA, :], E[:, c * CA:(c + 1) * CA, :], ACT.Exp,
                                             scale=float(DK) ** -0.5).then_inc(exped, 1)

                @block.vector
                def _(dve):
                    def cut(n, s):
                        dve.wait_ge(scored, HEAD + n - 1)
                        for g in range(G):
                            nc.vector.tensor_copy(rks[:, s, g], rk_v[:, g, bass.ds(n * AB, AB), :]).then_inc(rk_cut, 1)

                    def step_max(n):
                        dve.wait_ge(kept, HEAD + n + 1)
                        nc.vector.tensor_reduce(part[:, bass.ds(n, 1), :], E[:, bass.ds(n * AB, AB), :].rearrange("p a f -> p f a"),
                                                AX_X, ALU.max).then_inc(maxed, 1)

                    cut(0, 0)
                    with dve.Fori(0, NA // 2 - 1) as i:
                        cut(i * 2 + 1, 1)
                        step_max(i * 2)
                        cut(i * 2 + 2, 0)
                        step_max(i * 2 + 1)
                    cut(NA - 1, 1)
                    step_max(NA - 2)
                    step_max(NA - 1)
                    dve.wait_ge(maxed, HEAD + NA)
                    nc.vector.tensor_reduce(top[:, :], part[:, :, :].rearrange("p n f -> p f n"), AX_X, ALU.max).then_inc(topped, 1)
                    dve.wait_ge(topped, 1)
                    for c in range(CH):
                        nc.vector.tensor_tensor(E[:, c * CA:(c + 1) * CA, :], E[:, c * CA:(c + 1) * CA, :],
                                                top[:, :].unsqueeze(1).broadcast_to([P, CA, F]), ALU.subtract).then_inc(shifted, 1)
                    dve.wait_ge(exped, CH)
                    nc.vector.tensor_reduce(den[:, :], E[:, :, :].rearrange("p a f -> p f a"), AX_X, ALU.add).then_inc(summed, 1)
                    dve.wait_ge(summed, 1)
                    nc.vector.reciprocal(rden[:, :], den[:, :]).then_inc(inverted, 1)
                    dve.wait_ge(inverted, 1)
                    for c in range(CH):
                        nc.vector.tensor_tensor(E[:, c * CA:(c + 1) * CA, :], E[:, c * CA:(c + 1) * CA, :],
                                                rden[:, :].unsqueeze(1).broadcast_to([P, CA, F]), ALU.mult).then_inc(normed, 1)

                @block.sync
                def _(sp):
                    for c in range(CH):
                        sp.wait_ge(normed, c + 1)
                        for g in range(G):
                            sp.dma_start(att[b, :, c * CA:(c + 1) * CA, g * F:(g + 1) * F], E[g * N:(g + 1) * N, c * CA:(c + 1) * CA, :]).then_inc(saved, 16)
                    sp.wait_ge(saved, 16 * CH * G)


def mix_phase(nc, b, x, w_lv, w_rv, ident_d, sel_d, mask_d, att, o_d):
    with ExitStack() as stack:
        ph = Phase(nc, stack, f"mx{b}")
        ident = ph.sb("ident", [P, P])
        wlv = ph.sb("wlv", [P, KT, D])
        wrv = ph.sb("wrv", [P, KT, D])
        rv = ph.sb("rv", [P, N, D])
        xin = ph.sb("xin", [P, 2, D])
        xT = ph.sb("xT", [P, 2, KT, P])
        NXP = N // 2

        with ExitStack() as inner:
            rp = Phase(nc, inner, f"rp{b}")
            psT = rp.ps("psT", [P, 2, 512])
            psR = rp.ps("psR", [P, 2, 512])
            w_in = rp.sem("w_in")
            x_in = [rp.sem(f"x_in{s}") for s in range(2)]
            turned = rp.sem("turned")
            xT_done = rp.sem("xT_done")
            made = rp.sem("made")
            stored = rp.sem("stored")
            start_at_head(nc, [turned, xT_done, made, stored])
            with nc.Block() as block:
                @block.sync
                def _(sp):
                    sp.dma_start(ident[:, :], ident_d).then_inc(w_in, 16)
                    sp.dma_start(wrv[:, :, :], k_rows(w_rv)).then_inc(w_in, 16)
                    sp.dma_start(wlv[:, :, :], k_rows(w_lv)).then_inc(w_in, 16)
                    with sp.Fori(0, N // 2) as i:
                        for s in range(2):
                            n = i * 2 + s
                            sp.wait_ge(turned, HEAD + n - 1)
                            for c in range(2):
                                sp.dma_start(xin[c * N:(c + 1) * N, s, :], x[b, :, bass.ds(n, 1), :]).then_inc(x_in[s], 16)

                @block.tensor
                def _(pe):
                    def turn(n, s, i):
                        pe.wait_ge(x_in[s], i * 32 + 32)
                        pe.wait_ge(xT_done, HEAD + n - 1)
                        for k in range(KT):
                            mm = pe.transpose(psT[:, s, k * P:(k + 1) * P], xin[:, s, k * P:(k + 1) * P], ident[:, :])
                        mm.then_inc(turned, 1)

                    def make(n, s):
                        pe.wait_ge(xT_done, HEAD + n + 1)
                        pe.wait_ge(stored, HEAD + n - 1)
                        for k in range(KT):
                            mm = pe.matmul(psR[:, s, 0:D], xT[:, s, k, :], wrv[:, k, :], start=(k == 0), stop=(k == KT - 1))
                        mm.then_inc(made, 1)

                    pe.wait_ge(w_in, 48)
                    turn(0, 0, 0)
                    with pe.Fori(0, N // 2 - 1) as i:
                        turn(i * 2 + 1, 1, i)
                        make(i * 2, 0)
                        turn(i * 2 + 2, 0, i + 1)
                        make(i * 2 + 1, 1)
                    turn(N - 1, 1, N // 2 - 1)
                    make(N - 2, 0)
                    make(N - 1, 1)

                @block.scalar
                def _(act):
                    with act.Fori(0, N // 2) as i:
                        for s in range(2):
                            n = i * 2 + s
                            act.wait_ge(turned, HEAD + n + 1)
                            act.wait_ge(made, HEAD + n - 1)
                            nc.scalar.copy(xT[:, s], psT[:, s, 0:D].rearrange("p (k t) -> p k t", k=KT)).then_inc(xT_done, 1)

                @block.vector
                def _(dve):
                    with dve.Fori(0, N // 2) as i:
                        for s in range(2):
                            n = i * 2 + s
                            dve.wait_ge(made, HEAD + n + 1)
                            nc.vector.tensor_copy(rv[:, bass.ds(n, 1), :], psR[:, s, 0:D]).then_inc(stored, 1)

        with ExitStack() as inner:
            mp = Phase(nc, inner, f"mp{b}")
            YB = 8
            NYB = N // YB
            ZS = 4
            POOL_BLOCKS = (1, 4, 6)
            sel = mp.sb("sel", [P, 4, 32])
            mask = mp.sb("mask", [P, H])
            pair = mp.sb("pair", [P, 2, 2, H, N])
            lvs = mp.sb("lvs", [P, 2, D])
            Z = mp.sb("Z", [P, ZS, YB, D])
            cut = mp.sb("cut", [P, 2, 4, D])
            oS = mp.sb("oS", [P, 2, D])
            psT = mp.ps("psT", [P, 512])
            psL = mp.ps("psL", [P, 2, 512])
            psO = mp.ps("psO", [P, 2, 4, D])
            psN = mp.ps("psN", [P, 512])
            c_in = mp.sem("c_in")
            x_in = [mp.sem(f"x_in{s}") for s in range(2)]
            a_in = [mp.sem(f"a_in{s}") for s in range(2)]
            zeroed = mp.sem("zeroed")
            psO_clear = mp.sem("psO_clear")
            turned = mp.sem("turned")
            xT_done = mp.sem("xT_done")
            lv_made = mp.sem("lv_made")
            lv_kept = mp.sem("lv_kept")
            z_dve = mp.sem("z_dve")
            z_pool = mp.sem("z_pool")
            z_used = mp.sem("z_used")
            cut_done = mp.sem("cut_done")
            gathered = mp.sem("gathered")
            o_kept = mp.sem("o_kept")
            o_out = [mp.sem(f"o_out{s}") for s in range(2)]
            start_at_head(nc, [turned, xT_done, lv_made, lv_kept, z_dve, z_pool, z_used, cut_done, gathered, o_kept])
            dve_blocks = [k for k in range(NYB) if k not in POOL_BLOCKS]
            ND, NP = len(dve_blocks), len(POOL_BLOCKS)
            NQ = NYB // 2
            with nc.Block() as block:
                @block.sync
                def _(sp):
                    sp.dma_start(sel[:, :, :], sel_d).then_inc(c_in, 16)
                    sp.dma_start(mask[:, :], mask_d).then_inc(c_in, 16)
                    sp.wait_ge(zeroed, 2)

                    def load(n, s):
                        sp.wait_ge(turned, HEAD + n - 1)
                        sp.dma_start(xin[:, s, :], x[b, bass.ds(n * 2, 2)].rearrange("x a d -> (x a) d")).then_inc(x_in[s], 16)
                        sp.wait_ge(gathered, HEAD + (n - 1) * NQ)
                        for c in range(2):
                            sp.dma_start(pair[c * N:(c + 1) * N, s, c], att[b, bass.ds(n * 2 + c, 1)].rearrange("o a (h y) -> (o a) h y", y=N)).then_inc(a_in[s], 16)

                    def store(n, s):
                        sp.wait_ge(o_kept, HEAD + n + 1)
                        sp.dma_start(o_d[b, bass.ds(n, 1)].rearrange("o r d -> (o r) d"), oS[:, s, :]).then_inc(o_out[s], 16)

                    load(0, 0)
                    load(1, 1)
                    with sp.Fori(0, NXP // 2 - 1) as i:
                        for s in range(2):
                            store(i * 2 + s, s)
                            load(i * 2 + s + 2, s)
                    for s in range(2):
                        store(NXP - 2 + s, s)
                        sp.wait_ge(o_out[s], 16 * (NXP // 2))

                @block.tensor
                def _(pe):
                    def turn(n, s, r):
                        pe.wait_ge(x_in[s], r * 16 + 16)
                        pe.wait_ge(xT_done, HEAD + n)
                        for k in range(KT):
                            mm = pe.transpose(psT[:, k * P:(k + 1) * P], xin[:, s, k * P:(k + 1) * P], ident[:, :])
                        mm.then_inc(turned, 1)

                    def lv(n, s):
                        pe.wait_ge(xT_done, HEAD + n + 1)
                        pe.wait_ge(z_dve, HEAD + (n - 1) * ND)
                        for k in range(KT):
                            mm = pe.matmul(psL[:, s, 0:D], xT[:, s, k, :], wlv[:, k, :], start=(k == 0), stop=(k == KT - 1))
                        mm.then_inc(lv_made, 1)

                    def mix(n, s, c):
                        pe.wait_ge(cut_done, HEAD + n * NQ + c - 1)
                        for k in (2 * c, 2 * c + 1):
                            if k in POOL_BLOCKS:
                                pe.wait_ge(z_pool, HEAD + n * NP + POOL_BLOCKS.index(k) + 1)
                            else:
                                pe.wait_ge(z_dve, HEAD + n * ND + dve_blocks.index(k) + 1)
                            for y in range(YB):
                                j, q = y % 4, 2 * (k % 2) + y // 4
                                mm = pe.matmul(psO[32 * j:32 * j + 2 * H, c % 2, q, :], pair[:, s, :, :, k * YB + y], Z[:, k % ZS, y, :],
                                               start=True, stop=True, tile_position=(0, 32 * j))
                            mm.then_inc(z_used, 1)

                    def gather(n, c):
                        pe.wait_ge(cut_done, HEAD + n * NQ + c + 1)
                        if c == 0:
                            pe.wait_ge(o_kept, HEAD + n)
                        for q in range(4):
                            mm = pe.matmul(psN[32 * c:32 * c + 32, 0:D], sel[:, q, :], cut[:, c % 2, q, :], start=(q == 0), stop=(q == 3),
                                           tile_position=(0, 32 * c))
                        mm.then_inc(gathered, 1)

                    def step(n, s, r, first=False, last=False):
                        for c in range(NQ):
                            if c == 0:
                                pe.wait_ge(a_in[s], r * 32 + 32)
                            mix(n, s, c)
                            if c > 0:
                                gather(n, c - 1)
                            elif not first:
                                gather(n - 1, NQ - 1)
                            if c == 1 and not last:
                                turn(n + 1, 1 - s, r + s)
                            if c == 2 and not last:
                                lv(n + 1, 1 - s)
                        if last:
                            gather(n, NQ - 1)

                    pe.wait_ge(zeroed, 2)
                    pe.wait_ge(psO_clear, 1)
                    pe.wait_ge(c_in, 32)
                    turn(0, 0, 0)
                    lv(0, 0)
                    step(0, 0, 0, first=True)
                    step(1, 1, 0)
                    with pe.Fori(1, NXP // 2 - 1) as i:
                        for s in range(2):
                            step(i * 2 + s, s, i)
                    step(NXP - 2, 0, NXP // 2 - 1)
                    step(NXP - 1, 1, NXP // 2 - 1, last=True)

                @block.scalar
                def _(act):
                    def keep_xT(n, s):
                        act.wait_ge(turned, HEAD + n + 1)
                        nc.scalar.copy(xT[:, s], psT[:, 0:D].rearrange("p (k t) -> p k t", k=KT)).then_inc(xT_done, 1)

                    def keep_lv(n, s):
                        act.wait_ge(lv_made, HEAD + n + 1)
                        act.wait_ge(z_pool, HEAD + (n - 1) * NP)
                        nc.scalar.copy(lvs[:, s, :], psL[:, s, 0:D]).then_inc(lv_kept, 1)

                    def cut_heads(n, c):
                        act.wait_ge(z_used, HEAD + n * NYB + 2 * c + 2)
                        act.wait_ge(gathered, HEAD + n * NQ + c - 1)
                        for h in range(H):
                            ins = nc.scalar.activation(cut[:, c % 2, :, h * DK:(h + 1) * DK], psO[:, c % 2, :, h * DK:(h + 1) * DK], ACT.Copy,
                                                       scale=mask[:, h:h + 1])
                        ins.then_inc(cut_done, 1)

                    def keep_o(n, s, r):
                        act.wait_ge(gathered, HEAD + n * NQ + NQ)
                        if r is not None:
                            act.wait_ge(o_out[s], r * 16)
                        nc.scalar.copy(oS[:, s, :], psN[:, 0:D]).then_inc(o_kept, 1)

                    def step(n, s, r, first=False, last=False):
                        cut_heads(n, 0)
                        if not first:
                            keep_o(n - 1, 1 - s, r)
                        cut_heads(n, 1)
                        if not last:
                            keep_xT(n + 1, 1 - s)
                        cut_heads(n, 2)
                        if not last:
                            keep_lv(n + 1, 1 - s)
                        cut_heads(n, 3)

                    act.wait_ge(c_in, 32)
                    keep_xT(0, 0)
                    keep_lv(0, 0)
                    step(0, 0, None, first=True)
                    step(1, 1, None)
                    step(2, 0, None)
                    step(3, 1, 1)
                    with act.Fori(2, NXP // 2 - 1) as i:
                        step(i * 2, 0, i - 1)
                        step(i * 2 + 1, 1, i)
                    step(NXP - 2, 0, NXP // 2 - 2)
                    step(NXP - 1, 1, NXP // 2 - 1, last=True)
                    keep_o(NXP - 1, 1, NXP // 2 - 1)

                @block.vector
                def _(dve):
                    nc.vector.memset(psO[:, :, :, :], 0.0).then_inc(psO_clear, 1)
                    nc.vector.memset(pair[0:N, :, 1], 0.0).then_inc(zeroed, 1)
                    nc.vector.memset(pair[N:P, :, 0], 0.0).then_inc(zeroed, 1)
                    with dve.Fori(0, NXP // 2) as i:
                        for s in range(2):
                            n = i * 2 + s
                            dve.wait_ge(lv_kept, HEAD + n + 1)
                            for k in dve_blocks:
                                dve.wait_ge(z_used, HEAD + n * NYB + k + 1 - ZS)
                                nc.vector.tensor_tensor(Z[:, k % ZS], psL[:, s, 0:D].unsqueeze(1).broadcast_to([P, YB, D]), rv[:, k * YB:(k + 1) * YB, :],
                                                        ALU.mult).then_inc(z_dve, 1)

                @block.gpsimd
                def _(pool):
                    with pool.Fori(0, NXP // 2) as i:
                        for s in range(2):
                            n = i * 2 + s
                            pool.wait_ge(lv_kept, HEAD + n + 1)
                            for k in POOL_BLOCKS:
                                pool.wait_ge(z_used, HEAD + n * NYB + k + 1 - ZS)
                                nc.gpsimd.tensor_tensor(Z[:, k % ZS], lvs[:, s, :].unsqueeze(1).broadcast_to([P, YB, D]), rv[:, k * YB:(k + 1) * YB, :],
                                                        ALU.mult).then_inc(z_pool, 1)


def dense_phase(nc, x, o_d, w_out, g1, b1n, w1, b1, w2, b2, g2, b2n, ident_d, t_d, xlT_d):
    NT = B * T // P
    F1 = 2 * D
    MT = F1 // P
    with ExitStack() as stack:
        ph = Phase(nc, stack, "de")
        ident = ph.sb("ident", [P, P])
        wo = ph.sb("wo", [P, KT, D])
        wa = ph.sb("wa", [P, KT, F1])
        wb = ph.sb("wb", [P, MT, D])
        row = {name: ph.sb(name, [P, n]) for name, n in (("g1", D), ("b1n", D), ("b1", F1), ("b2", D), ("g2", D), ("b2n", D))}
        eps = ph.sb("eps", [P, 1])
        oin = ph.sb("oin", [P, 2, D])
        xres = ph.sb("xres", [P, 2, D])
        oT = ph.sb("oT", [P, 2, KT, P])
        hT = ph.sb("hT", [P, 2, KT, P])
        mT = ph.sb("mT", [P, 2, MT, P])
        xT = ph.sb("xT", [P, 2, KT, P])
        h0 = ph.sb("h0", [P, 2, D])
        hn = ph.sb("hn", [P, 2, D])
        hg = ph.sb("hg", [P, 2, D])
        hs = ph.sb("hs", [P, 2, D])
        hb2 = ph.sb("hb2", [P, NT, D])
        ma = ph.sb("ma", [P, 2, F1])
        m = ph.sb("m", [P, 2, F1])
        t0 = ph.sb("t0", [P, 2, D])
        tn = ph.sb("tn", [P, 2, D])
        tg = ph.sb("tg", [P, 2, D])
        ts = ph.sb("ts", [P, 2, D])
        xl = ph.sb("xl", [P, 2, D])
        stats = ph.sb("stats", [P, 3, 2, 6])
        mv = ph.sb("mv", [P, 3, 2, 2])
        std = ph.sb("std", [P, 3, 2, 1])
        rstd = ph.sb("rstd", [P, 3, 2, 1])
        ps_o, ps_h, ps_m, ps_x, ps_1, ps_2, ps_3 = (ph.ps(f"ps{j}", [P, 512]) for j in range(7))
        w_in = ph.sem("w_in")
        eps_set = ph.sem("eps_set")
        passed = ph.sem("passed")
        in_ = [ph.sem(f"in{s}") for s in range(2)]
        t_out = [ph.sem(f"t_out{s}") for s in range(2)]
        x_out = [ph.sem(f"x_out{s}") for s in range(2)]
        names = ("o_turned h_turned m_turned x_turned oT_kept hT_kept mT_kept xT_kept made1 made2 made3 "
                 "added1 biased relued added3 h_scaled h_done hb2_done t_scaled t_done").split()
        q = {n: ph.sem(n) for n in names}
        ln = [{n: ph.sem(f"{n}{j}") for n in ("stated", "aggregated", "rooted", "inverted", "normed")} for j in range(3)]
        start_at_head(nc, list(q.values()) + [v for d in ln for v in d.values()] + t_out + x_out)
        weights = [(ident[:, :], ident_d), (wo[:, :, :], k_rows(w_out)), (wa[:, :, :], k_rows(w1)), (wb[:, :, :], k_rows(w2))] + [
            (row[n][:, :], v.rearrange("(o n) -> o n", o=1).broadcast_to([P, row[n].shape[1]]))
            for n, v in (("g1", g1), ("b1n", b1n), ("b1", b1), ("b2", b2), ("g2", g2), ("b2n", b2n))]

        def iterations(eng, body):
            def fixed(i):
                body(i, i % 2, i // 2, lambda k: 0 <= i - 2 * k < NT)
            for i in range(8):
                fixed(i)
            with eng.Fori(4, NT // 2) as r:
                for s in range(2):
                    body(r * 2 + s, s, r, lambda k: True)
            for i in range(NT, NT + 8):
                fixed(i)

        with nc.Block() as block:
            @block.sync
            def _(sp):
                for dst, src in weights:
                    sp.dma_start(dst, src).then_inc(w_in, 16)

                def body(i, s, r, live):
                    if live(0):
                        sp.wait_ge(q["o_turned"], HEAD + i - 1)
                        sp.wait_ge(q["added1"], HEAD + i - 1)
                        ox = o_d.rearrange("b n (y x) d -> (b n) x y d", x=2)
                        for c in range(2):
                            sp.dma_start(oin[c * N:(c + 1) * N, s, :], ox[bass.ds(i, 1), c].rearrange("o y d -> (o y) d")).then_inc(in_[s], 16)
                        sp.dma_start(xres[:, s, :], x.rearrange("b x y d -> (b x y) d")[bass.ds(i * P, P), :]).then_inc(in_[s], 16)
                    if live(3):
                        n = i - 6
                        sp.wait_ge(q["t_done"], HEAD + n + 1)
                        sp.dma_start(t_d.rearrange("b t d -> (b t) d")[bass.ds(n * P, P), :], ts[:, s, :]).then_inc(t_out[s], 16)
                    if live(4):
                        n = i - 8
                        sp.wait_ge(q["xT_kept"], HEAD + n + 1)
                        sp.dma_start(xlT_d[:, :, bass.ds(n * P, P)].rearrange("k p t -> p k t"), xT[:, s]).then_inc(x_out[s], 16)

                iterations(sp, body)
                for s in range(2):
                    sp.wait_ge(t_out[s], HEAD + 16 * (NT // 2))
                    sp.wait_ge(x_out[s], HEAD + 16 * (NT // 2))

            @block.tensor
            def _(pe):
                def turn(dst, src, blocks, done):
                    for k in range(blocks):
                        mm = pe.transpose(dst[:, k * P:(k + 1) * P], src[:, k * P:(k + 1) * P], ident[:, :])
                    mm.then_inc(done, 1)

                def product(dst, lhsT, w, blocks, done):
                    for k in range(blocks):
                        mm = pe.matmul(dst, lhsT[:, k, :], w[:, k, :], start=(k == 0), stop=(k == blocks - 1))
                    mm.then_inc(done, 1)

                def body(i, s, r, live):
                    if live(0):
                        pe.wait_ge(in_[s], r * 48 + 48)
                        turn(ps_o, oin[:, s], KT, q["o_turned"])
                    if live(1):
                        pe.wait_ge(q["h_done"], HEAD + i - 2 + 1)
                        turn(ps_h, hs[:, s], KT, q["h_turned"])
                    if live(2):
                        pe.wait_ge(q["relued"], HEAD + i - 4 + 1)
                        turn(ps_m, m[:, s], MT, q["m_turned"])
                    if live(4):
                        pe.wait_ge(ln[2]["normed"], HEAD + i - 8 + 1)
                        pe.wait_ge(q["xT_kept"], HEAD + i - 8)
                        turn(ps_x, xl[:, s], KT, q["x_turned"])
                    if live(0):
                        pe.wait_ge(q["oT_kept"], HEAD + i + 1)
                        pe.wait_ge(q["added1"], HEAD + i)
                        product(ps_1[:, 0:D], oT[:, s], wo, KT, q["made1"])
                    if live(1):
                        pe.wait_ge(q["hT_kept"], HEAD + i - 2 + 1)
                        pe.wait_ge(q["biased"], HEAD + i - 2)
                        product(ps_2[:, :], hT[:, s], wa, KT, q["made2"])
                    if live(2):
                        pe.wait_ge(q["mT_kept"], HEAD + i - 4 + 1)
                        pe.wait_ge(q["added3"], HEAD + i - 4)
                        product(ps_3[:, 0:D], mT[:, s], wb, MT, q["made3"])

                pe.wait_ge(w_in, 16 * len(weights))
                iterations(pe, body)

            @block.scalar
            def _(act):
                def keep(dst, src, blocks, done):
                    nc.scalar.copy(dst, src[:, 0:blocks * P].rearrange("p (k t) -> p k t", k=blocks)).then_inc(done, 1)

                def root(j, n, s):
                    act.wait_ge(ln[j]["aggregated"], HEAD + n + 1)
                    nc.scalar.activation(std[:, j, s, :], mv[:, j, s, 1:2], ACT.Sqrt, bias=eps[:, :]).then_inc(ln[j]["rooted"], 1)

                def body(i, s, r, live):
                    if live(3):
                        root(2, i - 6, s)
                    if live(0):
                        act.wait_ge(q["o_turned"], HEAD + i + 1)
                        keep(oT[:, s], ps_o, KT, q["oT_kept"])
                    if live(1):
                        act.wait_ge(q["h_turned"], HEAD + i - 2 + 1)
                        keep(hT[:, s], ps_h, KT, q["hT_kept"])
                    if live(2):
                        act.wait_ge(q["m_turned"], HEAD + i - 4 + 1)
                        keep(mT[:, s], ps_m, MT, q["mT_kept"])
                    if live(4):
                        act.wait_ge(q["x_turned"], HEAD + i - 8 + 1)
                        act.wait_ge(x_out[s], HEAD + (r - 4) * 16)
                        keep(xT[:, s], ps_x, KT, q["xT_kept"])
                    if live(0):
                        root(0, i, s)
                    if live(1):
                        act.wait_ge(q["biased"], HEAD + i - 2 + 1)
                        nc.scalar.activation(m[:, s], ma[:, s], ACT.Relu).then_inc(q["relued"], 1)
                    if live(2):
                        root(1, i - 4, s)

                act.wait_ge(eps_set, 1)
                iterations(act, body)

            @block.vector
            def _(dve):
                def moments(j, n, s, src):
                    nc.vector.bn_stats(stats[:, j, s, :], src).then_inc(ln[j]["stated"], 1)
                    dve.wait_ge(ln[j]["stated"], HEAD + n + 1)
                    dve.sem_inc(passed, 1)
                    nc.vector.bn_aggr(mv[:, j, s, :], stats[:, j, s, :]).then_inc(ln[j]["aggregated"], 1)

                def normalise(j, n, s, dst, src):
                    dve.wait_ge(ln[j]["rooted"], HEAD + n + 1)
                    nc.vector.reciprocal(rstd[:, j, s, :], std[:, j, s, :]).then_inc(ln[j]["inverted"], 1)
                    dve.wait_ge(ln[j]["inverted"], HEAD + n + 1)
                    nc.vector.tensor_scalar(dst, src, mv[:, j, s, 0:1], rstd[:, j, s, :], ALU.subtract, ALU.mult).then_inc(ln[j]["normed"], 1)

                def body(i, s, r, live):
                    if live(3):
                        dve.wait_ge(q["t_done"], HEAD + i - 6 + 1)
                        moments(2, i - 6, s, ts[:, s])
                    if live(0):
                        dve.wait_ge(in_[s], r * 48 + 48)
                        dve.wait_ge(q["made1"], HEAD + i + 1)
                        nc.vector.tensor_tensor(h0[:, s], ps_1[:, 0:D], xres[:, s], ALU.add).then_inc(q["added1"], 1)
                        dve.wait_ge(q["added1"], HEAD + i + 1)
                        moments(0, i, s, h0[:, s])
                    if live(3):
                        dve.wait_ge(q["x_turned"], HEAD + i - 6 - 1)
                        normalise(2, i - 6, s, xl[:, s], ts[:, s])
                    if live(1):
                        dve.wait_ge(q["made2"], HEAD + i - 2 + 1)
                        dve.wait_ge(q["relued"], HEAD + i - 2 - 1)
                        nc.vector.tensor_tensor(ma[:, s], ps_2[:, :], row["b1"][:, :], ALU.add).then_inc(q["biased"], 1)
                    if live(0):
                        dve.wait_ge(q["h_scaled"], HEAD + i - 1)
                        normalise(0, i, s, hn[:, s], h0[:, s])
                    if live(2):
                        dve.wait_ge(q["made3"], HEAD + i - 4 + 1)
                        dve.wait_ge(q["hb2_done"], HEAD + i - 4 + 1)
                        nc.vector.tensor_tensor(t0[:, s], ps_3[:, 0:D], hb2[:, bass.ds(i - 4, 1), :].rearrange("p o d -> p (o d)"), ALU.add).then_inc(q["added3"], 1)
                        dve.wait_ge(q["added3"], HEAD + i - 4 + 1)
                        moments(1, i - 4, s, t0[:, s])
                        dve.wait_ge(q["t_scaled"], HEAD + i - 4 - 1)
                        normalise(1, i - 4, s, tn[:, s], t0[:, s])

                nc.vector.memset(eps[:, :], LN_EPS).then_inc(eps_set, 1)
                dve.wait_ge(w_in, 16 * len(weights))
                iterations(dve, body)

            @block.gpsimd
            def _(pool):
                def body(i, s, r, live):
                    if live(0):
                        pool.wait_ge(ln[0]["normed"], HEAD + i + 1)
                        nc.gpsimd.tensor_tensor(hg[:, s], hn[:, s], row["g1"][:, :], ALU.mult).then_inc(q["h_scaled"], 1)
                        pool.wait_ge(q["h_scaled"], HEAD + i + 1)
                        pool.wait_ge(q["h_turned"], HEAD + i - 1)
                        nc.gpsimd.tensor_tensor(hs[:, s], hg[:, s], row["b1n"][:, :], ALU.add).then_inc(q["h_done"], 1)
                        pool.wait_ge(q["h_done"], HEAD + i + 1)
                        nc.gpsimd.tensor_tensor(hb2[:, bass.ds(i, 1), :].rearrange("p o d -> p (o d)"), hs[:, s], row["b2"][:, :], ALU.add).then_inc(q["hb2_done"], 1)
                    if live(2):
                        n = i - 4
                        pool.wait_ge(ln[1]["normed"], HEAD + n + 1)
                        nc.gpsimd.tensor_tensor(tg[:, s], tn[:, s], row["g2"][:, :], ALU.mult).then_inc(q["t_scaled"], 1)
                        pool.wait_ge(q["t_scaled"], HEAD + n + 1)
                        pool.wait_ge(t_out[s], HEAD + (r - 2) * 16)
                        pool.wait_ge(ln[2]["normed"], HEAD + n - 1)
                        nc.gpsimd.tensor_tensor(ts[:, s], tg[:, s], row["b2n"][:, :], ALU.add).then_inc(q["t_done"], 1)

                pool.wait_ge(w_in, 16 * len(weights))
                iterations(pool, body)


def attention_phase(nc, b, t_d, xlT_d, wqT, bq, wkT, bk, wvT, bv, ident_d, t2_d):
    NT = T // P
    BLK = 512
    NBLK = T // BLK
    KB = BLK // P
    with ExitStack() as stack:
        ph = Phase(nc, stack, f"at{b}")
        ident = ph.sb("ident", [P, P])
        qT = ph.sb("qT", [P, KT, T])
        kT = ph.sb("kT", [P, KT, T])
        v = ph.sb("v", [P, T // P, D])

        with ExitStack() as inner:
            pj = Phase(nc, inner, f"qk{b}")
            w = [pj.sb(n, [P, KT, D]) for n in ("wq", "wk", "wv")]
            bias = [pj.sb(n, [P, KT]) for n in ("bq", "bk")]
            bvr = pj.sb("bvr", [P, D])
            xs = pj.sb("xs", [P, 2, KT, BLK])
            psP = pj.ps("psP", [P, 2 * KT, BLK])
            psV = pj.ps("psV", [P, KB, D])
            w_in = pj.sem("w_in")
            x_in = [pj.sem(f"x_in{s}") for s in range(2)]
            made = pj.sem("made")
            kept_qk = pj.sem("kept_qk")
            kept_v = pj.sem("kept_v")
            start_at_head(nc, [made, kept_qk, kept_v])
            loads = [(ident[:, :], ident_d), (w[0][:, :, :], k_rows(wqT)), (w[1][:, :, :], k_rows(wkT)), (w[2][:, :, :], k_rows(wvT)),
                     (bias[0][:, :], bq.rearrange("(k p) -> p k", p=P)), (bias[1][:, :], bk.rearrange("(k p) -> p k", p=P)),
                     (bvr[:, :], bv.rearrange("(o n) -> o n", o=1).broadcast_to([P, D]))]
            with nc.Block() as block:
                @block.sync
                def _(sp):
                    with nc.allow_non_contiguous_dma("two biases of 256 numbers, one to a partition"):
                        for dst, src in loads:
                            sp.dma_start(dst, src).then_inc(w_in, 16)
                    with sp.Fori(0, NBLK // 2) as r:
                        for s in range(2):
                            n = r * 2 + s
                            sp.wait_ge(made, HEAD + (n - 1) * 6)
                            sp.dma_start(xs[:, s], xlT_d[:, :, bass.ds(n * BLK + b * T, BLK)].rearrange("k p t -> p k t")).then_inc(x_in[s], 16)

                @block.tensor
                def _(pe):
                    pe.wait_ge(w_in, 16 * len(loads))
                    with pe.Fori(0, NBLK // 2) as r:
                        for s in range(2):
                            n = r * 2 + s
                            pe.wait_ge(x_in[s], r * 16 + 16)
                            for j in range(2 * KT):
                                pe.wait_ge(kept_qk, HEAD + (n - 1) * 4 + j + 1)
                                for k in range(KT):
                                    mm = pe.matmul(psP[:, j, :], w[j // KT][:, k, (j % KT) * P:(j % KT + 1) * P], xs[:, s, k, :], start=(k == 0), stop=(k == KT - 1))
                                mm.then_inc(made, 1)
                            for u in range(2):
                                pe.wait_ge(kept_v, HEAD + (n - 1) * 2 + u + 1)
                                for t in (2 * u, 2 * u + 1):
                                    for k in range(KT):
                                        mm = pe.matmul(psV[:, t, :], xs[:, s, k, t * P:(t + 1) * P], w[2][:, k, :], start=(k == 0), stop=(k == KT - 1))
                                mm.then_inc(made, 1)

                @block.scalar
                def _(act):
                    act.wait_ge(w_in, 16 * len(loads))
                    with act.Fori(0, NBLK // 2) as r:
                        for s in range(2):
                            n = r * 2 + s
                            for j in range(2 * KT):
                                act.wait_ge(made, HEAD + n * 6 + j + 1)
                                nc.scalar.activation((qT, kT)[j // KT][:, j % KT, bass.ds(n * BLK, BLK)], psP[:, j, :], ACT.Identity,
                                                     bias=bias[j // KT][:, j % KT:j % KT + 1]).then_inc(kept_qk, 1)

                @block.vector
                def _(dve):
                    dve.wait_ge(w_in, 16 * len(loads))
                    with dve.Fori(0, NBLK // 2) as r:
                        for s in range(2):
                            n = r * 2 + s
                            for u in range(2):
                                dve.wait_ge(made, HEAD + n * 6 + 4 + u + 1)
                                nc.vector.tensor_tensor(v[:, bass.ds(n * KB + 2 * u, 2), :], psV[:, 2 * u:2 * u + 2, :],
                                                        bvr[:, :].unsqueeze(1).broadcast_to([P, 2, D]), ALU.add).then_inc(kept_v, 1)

        with ExitStack() as inner:
            ap = Phase(nc, inner, f"sv{b}")
            SCALE = float(D) ** -0.5
            qs = ap.sb("qs", [P, 2, KT, P])
            S = ap.sb("S", [P, 2, NBLK, BLK])
            mx = ap.sb("mx", [P, 2, NBLK])
            top = ap.sb("top", [P, 2, 1])
            shift = ap.sb("shift", [P, 2, 1])
            part = ap.sb("part", [P, 2, NBLK])
            den = ap.sb("den", [P, 2, 1])
            rden = ap.sb("rden", [P, 2, 1])
            pT = ap.sb("pT", [P, 2, KB, P])
            tin = ap.sb("tin", [P, 2, D])
            t2 = ap.sb("t2", [P, 2, D])
            psS = ap.ps("psS", [P, 4, BLK])
            psT = ap.ps("psT", [P, 2, BLK])
            psO = ap.ps("psO", [P, 2, 512])
            t_in = [ap.sem(f"t_in{s}") for s in range(2)]
            t2_out = [ap.sem(f"t2_out{s}") for s in range(2)]
            q_cut = ap.sem("q_cut")
            scored = ap.sem("scored")
            kept = ap.sem("kept")
            maxed = ap.sem("maxed")
            topped = ap.sem("topped")
            shifted = ap.sem("shifted")
            exped = ap.sem("exped")
            turned = ap.sem("turned")
            pT_kept = ap.sem("pT_kept")
            weighed = ap.sem("weighed")
            summed = ap.sem("summed")
            inverted = ap.sem("inverted")
            added = ap.sem("added")
            start_at_head(nc, [q_cut, scored, kept, maxed, topped, shifted, exped, turned, pT_kept, weighed, summed, inverted, added] + t2_out)
            C = NBLK

            def tiles(eng, body):
                body(0, 0, 0, True)
                body(1, 1, 0, True)
                with eng.Fori(1, NT // 2 - 1) as r:
                    for s in range(2):
                        body(r * 2 + s, s, r, True)
                body(NT - 2, 0, NT // 2 - 1, True)
                body(NT - 1, 1, NT // 2 - 1, False)

            with nc.Block() as block:
                @block.sync
                def _(sp):
                    def load(n, s):
                        sp.wait_ge(added, HEAD + n - 1)
                        sp.dma_start(tin[:, s, :], t_d[b, bass.ds(n * P, P), :]).then_inc(t_in[s], 16)

                    def save(n, s):
                        sp.wait_ge(added, HEAD + n + 1)
                        sp.dma_start(t2_d[b, bass.ds(n * P, P), :], t2[:, s, :]).then_inc(t2_out[s], 16)

                    for s in range(2):
                        load(s, s)
                    with sp.Fori(0, NT // 2 - 1) as r:
                        for s in range(2):
                            save(r * 2 + s, s)
                            load(r * 2 + s + 2, s)
                    for s in range(2):
                        save(NT - 2 + s, s)
                    for s in range(2):
                        sp.wait_ge(t2_out[s], HEAD + 16 * (NT // 2))

                @block.gpsimd
                def _(pool):
                    with pool.Fori(0, NT // 2) as r:
                        for s in range(2):
                            n = r * 2 + s
                            pool.wait_ge(scored, HEAD + (n - 1) * C)
                            nc.gpsimd.tensor_copy(qs[:, s], qT[:, :, bass.ds(n * P, P)]).then_inc(q_cut, 1)

                @block.tensor
                def _(pe):
                    def score(n, s, c):
                        if c == 0:
                            pe.wait_ge(q_cut, HEAD + n + 1)
                        pe.wait_ge(kept, HEAD + n * C + c - 3)
                        for k in range(KT):
                            mm = pe.matmul(psS[:, c % 4, :], qs[:, s, k, :], kT[:, k, c * BLK:(c + 1) * BLK], start=(k == 0), stop=(k == KT - 1))
                        mm.then_inc(scored, 1)

                    def turn(n, s, c):
                        pe.wait_ge(exped, HEAD + n * C + c + 1)
                        pe.wait_ge(pT_kept, HEAD + n * C + c - 1)
                        for t in range(KB):
                            mm = pe.transpose(psT[:, c % 2, t * P:(t + 1) * P], S[:, s, c, t * P:(t + 1) * P], ident[:, :])
                        mm.then_inc(turned, 1)

                    def weigh(n, s, c):
                        pe.wait_ge(pT_kept, HEAD + n * C + c + 1)
                        if c == 0:
                            pe.wait_ge(added, HEAD + n - 1)
                        for t in range(KB):
                            mm = pe.matmul(psO[:, s, 0:D], pT[:, c % 2, t, :], v[:, c * KB + t, :],
                                           start=(c == 0 and t == 0), stop=(c == C - 1 and t == KB - 1))
                        mm.then_inc(weighed, 1)

                    def body(n, s, r, ahead):
                        for step in range(C + 4):
                            if ahead and step < C:
                                score(n + 1, 1 - s, step)
                            if 3 <= step < C + 3:
                                turn(n, s, step - 3)
                            if 4 <= step:
                                weigh(n, s, step - 4)

                    for c in range(C):
                        score(0, 0, c)
                    tiles(pe, body)

                @block.scalar
                def _(act):
                    def keep(n, s, c):
                        act.wait_ge(scored, HEAD + n * C + c + 1)
                        nc.scalar.copy(S[:, s, c, :], psS[:, c % 4, :]).then_inc(kept, 1)

                    def exponent(n, s, c):
                        if c == 0:
                            act.wait_ge(shifted, HEAD + n + 1)
                        nc.scalar.activation(S[:, s, c, :], S[:, s, c, :], ACT.Exp, bias=shift[:, s, :], scale=SCALE,
                                             accum_out=part[:, s, c:c + 1]).then_inc(exped, 1)

                    def body(n, s, r, ahead):
                        exponent(n, s, 0)
                        for c in range(C):
                            if c + 1 < C:
                                exponent(n, s, c + 1)
                            if ahead:
                                keep(n + 1, 1 - s, c)

                    for c in range(C):
                        keep(0, 0, c)
                    tiles(act, body)

                @block.vector
                def _(dve):
                    def most(n, s, c):
                        dve.wait_ge(kept, HEAD + n * C + c + 1)
                        nc.vector.tensor_reduce(mx[:, s, c:c + 1], S[:, s, c, :], AX_X, ALU.max).then_inc(maxed, 1)

                    def bias(n, s):
                        dve.wait_ge(maxed, HEAD + n * C + C)
                        nc.vector.tensor_reduce(top[:, s, :], mx[:, s, :], AX_X, ALU.max).then_inc(topped, 1)
                        dve.wait_ge(topped, HEAD + n + 1)
                        nc.vector.tensor_scalar(shift[:, s, :], top[:, s, :], -SCALE, None, ALU.mult).then_inc(shifted, 1)

                    def keep_pT(n, s, c):
                        dve.wait_ge(turned, HEAD + n * C + c + 1)
                        dve.wait_ge(weighed, HEAD + n * C + c - 1)
                        nc.vector.tensor_copy(pT[:, c % 2], psT[:, c % 2, :].rearrange("p (t q) -> p t q", t=KB)).then_inc(pT_kept, 1)

                    def finish(n, s, r):
                        nc.vector.tensor_reduce(den[:, s, :], part[:, s, :], AX_X, ALU.add).then_inc(summed, 1)
                        dve.wait_ge(summed, HEAD + n + 1)
                        nc.vector.reciprocal(rden[:, s, :], den[:, s, :]).then_inc(inverted, 1)
                        dve.wait_ge(weighed, HEAD + n * C + C)
                        dve.wait_ge(inverted, HEAD + n + 1)
                        dve.wait_ge(t_in[s], r * 16 + 16)
                        dve.wait_ge(t2_out[s], HEAD + r * 16)
                        nc.vector.scalar_tensor_tensor(out=t2[:, s, :], in0=psO[:, s, 0:D], scalar=rden[:, s, :], in1=tin[:, s, :],
                                                       op0=ALU.mult, op1=ALU.add).then_inc(added, 1)

                    def body(n, s, r, ahead):
                        for step in range(C + 3):
                            if ahead and step < C:
                                most(n + 1, 1 - s, step)
                                if step == C - 1:
                                    bias(n + 1, 1 - s)
                            if step >= 3:
                                keep_pT(n, s, step - 3)
                        finish(n, s, r)

                    for c in range(C):
                        most(0, 0, c)
                    bias(0, 0)
                    tiles(dve, body)


def gates_phase(nc, t2_d, u, bg, ident_d, xg_d):
    NT = B * T // P
    GW = 3 * D
    with ExitStack() as stack:
        ph = Phase(nc, stack, "ga")
        ident = ph.sb("ident", [P, P])
        w = ph.sb("w", [P, KT, GW])
        bias = ph.sb("bias", [P, GW])
        eps = ph.sb("eps", [P, 1])
        tin = ph.sb("tin", [P, 2, D])
        xl = ph.sb("xl", [P, 2, D])
        xT = ph.sb("xT", [P, 2, KT, P])
        xg = ph.sb("xg", [P, 2, GW])
        stats = ph.sb("stats", [P, 2, 6])
        mv = ph.sb("mv", [P, 2, 2])
        std = ph.sb("std", [P, 2, 1])
        rstd = ph.sb("rstd", [P, 2, 1])
        psT = ph.ps("psT", [P, 2, 512])
        psG = ph.ps("psG", [P, 2, 1024])
        w_in, eps_set, passed = ph.sem("w_in"), ph.sem("eps_set"), ph.sem("passed")
        t_in = [ph.sem(f"t_in{s}") for s in range(2)]
        g_out = [ph.sem(f"g_out{s}") for s in range(2)]
        stated, aggregated, rooted, inverted, normed, turned, xT_kept, made, biased = (
            ph.sem(n) for n in "stated aggregated rooted inverted normed turned xT_kept made biased".split())
        start_at_head(nc, [stated, aggregated, rooted, inverted, normed, turned, xT_kept, made, biased] + g_out)
        loads = [(ident[:, :], ident_d)] + [(w[:, :, j * D:(j + 1) * D], k_rows(u[j])) for j in range(3)] + [
            (bias[:, j * D:(j + 1) * D], bg[j].rearrange("(o n) -> o n", o=1).broadcast_to([P, D])) for j in range(3)]

        def iterations(eng, body):
            for i in range(4):
                body(i, i % 2, i // 2, lambda k, i=i: i - 2 * k >= 0)
            with eng.Fori(2, NT // 2) as r:
                for s in range(2):
                    body(r * 2 + s, s, r, lambda k: True)
            for i in range(NT, NT + 4):
                body(i, i % 2, i // 2, lambda k, i=i: i - 2 * k < NT)

        with nc.Block() as block:
            @block.sync
            def _(sp):
                for dst, src in loads:
                    sp.dma_start(dst, src).then_inc(w_in, 16)

                def body(i, s, r, live):
                    if live(0):
                        sp.wait_ge(normed, HEAD + i - 1)
                        sp.dma_start(tin[:, s, :], t2_d.rearrange("b t d -> (b t) d")[bass.ds(i * P, P), :]).then_inc(t_in[s], 16)
                    if live(2):
                        n = i - 4
                        sp.wait_ge(biased, HEAD + n + 1)
                        sp.dma_start(xg_d.rearrange("b t d -> (b t) d")[bass.ds(n * P, P), :], xg[:, s, :]).then_inc(g_out[s], 16)
                iterations(sp, body)
                for s in range(2):
                    sp.wait_ge(g_out[s], HEAD + 16 * (NT // 2))

            @block.tensor
            def _(pe):
                def body(i, s, r, live):
                    if live(1):
                        n = i - 2
                        pe.wait_ge(normed, HEAD + n + 1)
                        pe.wait_ge(xT_kept, HEAD + n - 1)
                        for k in range(KT):
                            mm = pe.transpose(psT[:, s, k * P:(k + 1) * P], xl[:, s, k * P:(k + 1) * P], ident[:, :])
                        mm.then_inc(turned, 1)
                    if live(2):
                        n = i - 4
                        pe.wait_ge(xT_kept, HEAD + n + 1)
                        pe.wait_ge(biased, HEAD + n - 1)
                        for lo, hi in ((0, 512), (512, GW)):
                            for k in range(KT):
                                mm = pe.matmul(psG[:, s, lo:hi], xT[:, s, k, :], w[:, k, lo:hi], start=(k == 0), stop=(k == KT - 1))
                        mm.then_inc(made, 1)
                pe.wait_ge(w_in, 16 * len(loads))
                iterations(pe, body)

            @block.scalar
            def _(act):
                def body(i, s, r, live):
                    if live(0):
                        act.wait_ge(aggregated, HEAD + i + 1)
                        nc.scalar.activation(std[:, s, :], mv[:, s, 1:2], ACT.Sqrt, bias=eps[:, :]).then_inc(rooted, 1)
                    if live(1):
                        n = i - 2
                        act.wait_ge(turned, HEAD + n + 1)
                        act.wait_ge(made, HEAD + n - 1)
                        nc.scalar.copy(xT[:, s], psT[:, s, 0:D].rearrange("p (k t) -> p k t", k=KT)).then_inc(xT_kept, 1)
                act.wait_ge(eps_set, 1)
                iterations(act, body)

            @block.vector
            def _(dve):
                def body(i, s, r, live):
                    if live(0):
                        dve.wait_ge(t_in[s], r * 16 + 16)
                        nc.vector.bn_stats(stats[:, s, :], tin[:, s]).then_inc(stated, 1)
                        dve.wait_ge(stated, HEAD + i + 1)
                        dve.sem_inc(passed, 1)
                        nc.vector.bn_aggr(mv[:, s, :], stats[:, s, :]).then_inc(aggregated, 1)
                    if live(2):
                        n = i - 4
                        dve.wait_ge(made, HEAD + n + 1)
                        dve.wait_ge(g_out[s], HEAD + (r - 2) * 16)
                        nc.vector.tensor_tensor(xg[:, s, :], psG[:, s, 0:GW], bias[:, :], ALU.add).then_inc(biased, 1)
                    if live(0):
                        dve.wait_ge(rooted, HEAD + i + 1)
                        nc.vector.reciprocal(rstd[:, s, :], std[:, s, :]).then_inc(inverted, 1)
                        dve.wait_ge(inverted, HEAD + i + 1)
                        dve.wait_ge(turned, HEAD + i - 1)
                        nc.vector.tensor_scalar(xl[:, s, :], tin[:, s, :], mv[:, s, 0:1], rstd[:, s, :], ALU.subtract, ALU.mult).then_inc(normed, 1)
                nc.vector.memset(eps[:, :], LN_EPS).then_inc(eps_set, 1)
                dve.wait_ge(w_in, 16 * len(loads))
                iterations(dve, body)


def recurrent_phase(nc, xg_d, v_d, ident_d, t2_d, out):
    CHUNKS = P // B
    L = T // CHUNKS
    WARM = 48
    SAME = 2.0 ** -18
    GW = 3 * D
    with ExitStack() as stack:
        ph = Phase(nc, stack, "re")
        ident = ph.sb("ident", [P, P])
        w = ph.sb("w", [P, KT, GW])
        hT = ph.sb("hT", [P, 2, KT, P])
        h = ph.sb("h", [P, 2, D])
        c = ph.sb("c", [P, 2, D])
        hc = ph.sb("hc", [P, 2, D])
        ig = ph.sb("ig", [P, 2, D])
        tc = ph.sb("tc", [P, 2, D])
        z = ph.sb("z", [P, 2, GW])
        gate = ph.sb("gate", [P, 2, GW])
        xg = ph.sb("xg", [P, 2, GW])
        tin = ph.sb("tin", [P, 2, D])
        os = ph.sb("os", [P, 2, D])
        start = ph.sb("start", [P, 2, D])
        shifted = ph.sb("shifted", [P, 2, D])
        gap = ph.sb("gap", [P, 2 * D])
        most = ph.sb("most", [P, 1])
        most1 = ph.sb("most1", [1, 1])
        again = ph.sb("again", [1, 1], I32)
        psA = ph.ps("psA", [P, 512])
        psB = ph.ps("psB", [P, 512])
        psT = ph.ps("psT", [P, 512])
        psM = ph.ps("psM", [P, 512])
        sem = ph.sem
        w_in = sem("w_in")
        xg_in = [sem(f"xg_in{s}") for s in range(2)]
        t_in = [sem(f"t_in{s}") for s in range(2)]
        outed = [sem(f"outed{s}") for s in range(2)]
        ends_in = sem("ends_in")
        q = {n: sem(n) for n in ("ig_made o_made turned hT_kept ig_added o_added i_ready g_ready o_ready ig_ready c_ready "
                                 "tanh_ready h_ready hc_ready os_ready started cleared gapped gap_max gap_turned gap_most judged decided").split()}
        seen = {e: sem(f"seen_{e}") for e in ("sp", "pe", "act", "dve", "pool")}
        start_at_head(nc, list(q.values()) + list(seen.values()) + xg_in + t_in + outed + [ends_in])

        x_rows = xg_d.rearrange("b (n s) d -> (b n) s d", s=L)
        t_rows = t2_d.rearrange("b (n s) d -> (b n) s d", s=L)
        out_rows = out.rearrange("b x y d -> (b x y) d").rearrange("(r s) d -> r s d", s=L)

        def sweeps(eng, name, sweep):
            with eng.Fori(0, CHUNKS) as k:
                eng.wait_ge(q["decided"], HEAD + k + 1)
                eng.sem_inc(seen[name], 1)
                more = eng.value_load(again[0:1, 0:1], min_val=0, max_val=1)
                with eng.If(more > 0):
                    sweep(k)
                if name == "dve":
                    eng.sem_inc(q["decided"], 1)

        with nc.Block() as block:
            @block.sync
            def _(sp):

                def load(count, s, step, full, r):
                    sp.wait_ge(q["o_added"], HEAD + count - 1)
                    sp.dma_start(xg[:, s, :], x_rows[:, bass.ds(step, 1), :].rearrange("r o d -> r (o d)")).then_inc(xg_in[s], 16)
                    if full:
                        sp.wait_ge(q["os_ready"], HEAD + count - WARM - 1)
                        sp.dma_start(tin[:, s, :], t_rows[:, bass.ds(step, 1), :].rearrange("r o d -> r (o d)")).then_inc(t_in[s], 16)

                def save(count, s, step):
                    sp.wait_ge(q["os_ready"], HEAD + count - WARM + 1)
                    sp.dma_start(out_rows[:, bass.ds(step, 1), :].rearrange("r o d -> r (o d)"), os[:, s, :]).then_inc(outed[s], 16)

                def move_ends(steps):
                    sp.wait_ge(q["h_ready"], HEAD + steps)
                    sp.wait_ge(q["cleared"], HEAD + 1)
                    last = 1
                    for j, buf in enumerate((h, c)):
                        for b in range(B):
                            lo, hi = b * CHUNKS, (b + 1) * CHUNKS
                            sp.dma_start(shifted[lo + 1:hi, j, :], buf[lo:hi - 1, last, :]).then_inc(ends_in, 16)

                def prepare():
                    sp.dma_start(ident[:, :], ident_d).then_inc(w_in, 16)
                    for j in range(3):
                        sp.dma_start(w[:, :, j * D:(j + 1) * D], k_rows(v_d[j])).then_inc(w_in, 16)

                def warm():
                    with sp.Fori(0, WARM // 2) as i:
                        for s in range(2):
                            load(i * 2 + s, s, i * 2 + s + L - WARM, False, i)
                    move_ends(WARM)

                def sweep(k):
                    base = k * L + WARM
                    load(base, 0, 0, True, None)
                    load(base + 1, 1, 1, True, None)
                    with sp.Fori(0, L // 2 - 1) as i:
                        for s in range(2):
                            save(base + i * 2 + s, s, i * 2 + s)
                            load(base + i * 2 + s + 2, s, i * 2 + s + 2, True, None)
                    for s in range(2):
                        save(base + L - 2 + s, s, L - 2 + s)
                    move_ends(base + L)
                    for s in range(2):
                        sp.wait_ge(outed[s], (k * (L // 2) + L // 2) * 16 + HEAD)
                    sp.sem_inc(seen["sp"], 1)

                prepare()
                warm()
                sweeps(sp, "sp", sweep)

            @block.tensor
            def _(pe):

                def turn(src):
                    for j in range(KT):
                        mm = pe.transpose(psT[:, j * P:(j + 1) * P], src[:, j * P:(j + 1) * P], ident[:, :])
                    mm.then_inc(q["turned"], 1)

                def step(count, turns, s):
                    pe.wait_ge(q["hT_kept"], HEAD + turns + 1)
                    for dst, lo, hi, done in ((psA, 0, 512, "ig_made"), (psB, 512, GW, "o_made")):
                        for j in range(KT):
                            mm = pe.matmul(dst[:, 0:hi - lo], hT[:, s, j, :], w[:, j, lo:hi], start=(j == 0), stop=(j == KT - 1))
                        mm.then_inc(q[done], 1)
                    pe.wait_ge(q["h_ready"], HEAD + count + 1)
                    turn(h[:, s])

                def prepare():
                    pe.wait_ge(w_in, 64)

                def warm():
                    pe.wait_ge(q["started"], HEAD + 1)
                    turn(start[:, 0])
                    with pe.Fori(0, WARM // 2) as i:
                        for s in range(2):
                            step(i * 2 + s, i * 2 + s, s)

                def sweep(k):
                    pe.wait_ge(q["hT_kept"], k * (L + 1) + WARM + 1 + HEAD)
                    turn(start[:, 0])
                    with pe.Fori(0, L // 2) as i:
                        for s in range(2):
                            step(k * L + WARM + i * 2 + s, k * (L + 1) + WARM + 1 + i * 2 + s, s)
                    pe.wait_ge(q["gap_max"], HEAD + k + 1)
                    pe.transpose(psM[0:1, 0:P], most[:, :], ident[:, :]).then_inc(q["gap_turned"], 1)

                prepare()
                warm()
                sweeps(pe, "pe", sweep)

            @block.scalar
            def _(act):

                def keep_hT(turns, s):
                    act.wait_ge(q["turned"], HEAD + turns + 1)
                    nc.scalar.copy(hT[:, s], psT[:, 0:D].rearrange("p (k t) -> p k t", k=KT)).then_inc(q["hT_kept"], 1)

                def step(count, turns, s):
                    act.wait_ge(q["ig_added"], HEAD + count + 1)
                    nc.scalar.activation(gate[:, s, 0:D], z[:, s, 0:D], ACT.Sigmoid).then_inc(q["i_ready"], 1)
                    nc.scalar.activation(gate[:, s, D:2 * D], z[:, s, D:2 * D], ACT.Tanh).then_inc(q["g_ready"], 1)
                    act.wait_ge(q["o_added"], HEAD + count + 1)
                    nc.scalar.activation(gate[:, s, 2 * D:GW], z[:, s, 2 * D:GW], ACT.Sigmoid).then_inc(q["o_ready"], 1)
                    act.wait_ge(q["c_ready"], HEAD + count + 1)
                    nc.scalar.activation(tc[:, s], c[:, s], ACT.Tanh).then_inc(q["tanh_ready"], 1)
                    keep_hT(turns + 1, 1 - s)

                def warm():
                    keep_hT(0, 0)
                    with act.Fori(0, WARM // 2) as i:
                        for s in range(2):
                            step(i * 2 + s, i * 2 + s, s)

                def sweep(k):
                    keep_hT(k * (L + 1) + WARM + 1, 0)
                    with act.Fori(0, L // 2) as i:
                        for s in range(2):
                            step(k * L + WARM + i * 2 + s, k * (L + 1) + WARM + 1 + i * 2 + s, s)

                warm()
                sweeps(act, "act", sweep)

            @block.vector
            def _(dve):

                def step(count, r, s):
                    dve.wait_ge(xg_in[s], (r + 1) * 16 + HEAD)
                    dve.wait_ge(q["ig_made"], HEAD + count + 1)
                    nc.vector.tensor_tensor(z[:, s, 0:512], psA[:, :], xg[:, s, 0:512], ALU.add).then_inc(q["ig_added"], 1)
                    dve.wait_ge(q["o_made"], HEAD + count + 1)
                    nc.vector.tensor_tensor(z[:, s, 512:GW], psB[:, 0:GW - 512], xg[:, s, 512:GW], ALU.add).then_inc(q["o_added"], 1)
                    dve.wait_ge(q["g_ready"], HEAD + count + 1)
                    nc.vector.tensor_tensor(ig[:, s], gate[:, s, 0:D], gate[:, s, D:2 * D], ALU.mult).then_inc(q["ig_ready"], 1)
                    dve.wait_ge(q["hc_ready"], HEAD + count + 1)
                    dve.wait_ge(q["ig_ready"], HEAD + count + 1)
                    nc.vector.tensor_tensor(c[:, s], ig[:, s], hc[:, s], ALU.add).then_inc(q["c_ready"], 1)
                    dve.wait_ge(q["tanh_ready"], HEAD + count + 1)
                    nc.vector.tensor_tensor(h[:, s], gate[:, s, 2 * D:GW], tc[:, s], ALU.mult).then_inc(q["h_ready"], 1)

                def prepare():
                    nc.vector.memset(start[:, :, :], 0.0).then_inc(q["started"], 1)
                    nc.vector.memset(shifted[:, :, :], 0.0).then_inc(q["cleared"], 1)

                def warm():
                    with dve.Fori(0, WARM // 2) as i:
                        for s in range(2):
                            step(i * 2 + s, i, s)
                    dve.wait_ge(ends_in, HEAD + 64)
                    nc.vector.tensor_copy(start[:, :, :], shifted[:, :, :]).then_inc(q["started"], 1)
                    dve.wait_ge(q["started"], HEAD + 2)
                    nc.vector.memset(again[:, :], 1).then_inc(q["decided"], 1)

                def sweep(k):
                    with dve.Fori(0, L // 2) as i:
                        for s in range(2):
                            step(k * L + WARM + i * 2 + s, k * (L // 2) + i + WARM // 2, s)
                    dve.wait_ge(ends_in, k * 64 + 128 + HEAD)
                    nc.vector.tensor_tensor(gap[:, :], shifted[:, :, :].rearrange("p j d -> p (j d)"), start[:, :, :].rearrange("p j d -> p (j d)"),
                                            ALU.subtract).then_inc(q["gapped"], 1)
                    dve.wait_ge(q["gapped"], HEAD + k + 1)
                    nc.vector.tensor_reduce(most[:, :], gap[:, :], AX_X, ALU.max, apply_absolute_value=True).then_inc(q["gap_max"], 1)
                    nc.vector.tensor_copy(start[:, :, :], shifted[:, :, :]).then_inc(q["started"], 1)
                    dve.wait_ge(q["gap_turned"], HEAD + k + 1)
                    nc.vector.tensor_reduce(most1[:, :], psM[0:1, 0:P], AX_X, ALU.max).then_inc(q["gap_most"], 1)
                    dve.wait_ge(q["gap_most"], HEAD + k + 1)
                    nc.vector.tensor_scalar(again[:, :], most1[:, :], SAME, None, ALU.is_gt).then_inc(q["judged"], 1)
                    dve.wait_ge(q["judged"], HEAD + k + 1)
                    dve.sem_inc(seen["dve"], 1)

                prepare()
                warm()
                sweeps(dve, "dve", sweep)

            @block.gpsimd
            def _(pool):

                def product(hv, cv, s):
                    nc.gpsimd.tensor_tensor(hc[:, s], hv, cv, ALU.mult).then_inc(q["hc_ready"], 1)

                def warm():
                    pool.wait_ge(q["started"], HEAD + 1)
                    product(start[:, 0], start[:, 1], 0)
                    with pool.Fori(0, WARM // 2 - 1) as i:
                        for s in range(2):
                            pool.wait_ge(q["h_ready"], HEAD + i * 2 + s + 1)
                            product(h[:, s], c[:, s], 1 - s)
                    pool.wait_ge(q["h_ready"], HEAD + WARM - 1)
                    product(h[:, 0], c[:, 0], 1)

                def sweep(k):
                    def give(i, s):
                        pool.wait_ge(t_in[s], (k * (L // 2) + i + 1) * 16 + HEAD)
                        pool.wait_ge(outed[s], (k * (L // 2) + i) * 16 + HEAD)
                        nc.gpsimd.tensor_tensor(os[:, s], h[:, s], tin[:, s], ALU.add).then_inc(q["os_ready"], 1)

                    product(start[:, 0], start[:, 1], 0)
                    with pool.Fori(0, L // 2 - 1) as i:
                        for s in range(2):
                            pool.wait_ge(q["h_ready"], k * L + WARM + i * 2 + s + 1 + HEAD)
                            product(h[:, s], c[:, s], 1 - s)
                            give(i, s)
                    pool.wait_ge(q["h_ready"], k * L + WARM + L - 1 + HEAD)
                    product(h[:, 0], c[:, 0], 1)
                    give(L // 2 - 1, 0)
                    pool.wait_ge(q["h_ready"], k * L + WARM + L + HEAD)
                    give(L // 2 - 1, 1)

                warm()
                sweeps(pool, "pool", sweep)


def constants():
    ident = np.eye(P, dtype=np.float32)
    sel = np.zeros((P, 4, 32), np.float32)
    mask = np.zeros((P, H), np.float32)
    for j in range(4):
        for xx in range(2):
            for h in range(H):
                p = 32 * j + 8 * xx + h
                mask[p, h] = 1.0
                for q in range(4):
                    sel[p, q, 8 * q + 2 * j + xx] = 1.0
    return {"ident": ident, "sel": sel, "mask": mask}


_L0 = ["W_lk", "W_rk", "W_lv", "W_rv", "W_out", "ln_agg_g", "ln_agg_b", "W1", "b1", "W2", "b2", "ln2_g", "ln2_b"]
_L1 = ["bq", "bk", "bv"]
_GATES = ["i", "c", "o"]


def build(nc, aps, out, kind):
    att = nc.dram_tensor("att", (B, N, N, H * N), F32, kind=kind).ap()
    o_d = nc.dram_tensor("o", (B, N // 2, 2 * N, D), F32, kind=kind).ap()
    t_d = nc.dram_tensor("t", (B, T, D), F32, kind=kind).ap()
    xlT_d = nc.dram_tensor("xlT", (KT, P, B * T), F32, kind=kind).ap()
    t2_d = nc.dram_tensor("t2", (B, T, D), F32, kind=kind).ap()
    xg_d = nc.dram_tensor("xg", (B, T, 3 * D), F32, kind=kind).ap()
    x, ident = aps["x"], aps["ident"]
    w = {n: aps["L0_conv_" + n] for n in _L0}
    for b in range(B):
        scores_phase(nc, b, x, w["W_lk"], w["W_rk"], ident, att)
    for b in range(B):
        mix_phase(nc, b, x, w["W_lv"], w["W_rv"], ident, aps["sel"], aps["mask"], att, o_d)
    dense_phase(nc, x, o_d, w["W_out"], w["ln_agg_g"], w["ln_agg_b"], w["W1"], w["b1"], w["W2"], w["b2"], w["ln2_g"], w["ln2_b"], ident, t_d, xlT_d)
    for b in range(B):
        attention_phase(nc, b, t_d, xlT_d, aps["WqT"], aps["L1_attn_bq"], aps["WkT"], aps["L1_attn_bk"], aps["WvT"], aps["L1_attn_bv"], ident, t2_d)
    gates_phase(nc, t2_d, [aps["L1_ffn_U_" + g] for g in _GATES], [aps["L1_ffn_b_" + g] for g in _GATES], ident, xg_d)
    recurrent_phase(nc, xg_d, [aps["L1_ffn_V_" + g] for g in _GATES], ident, t2_d, out)


def kernel(**inputs):
    import numpy as _np
    import concourse.bacc as _bacc
    from concourse import mybir as _mybir
    from concourse.bass_utils import run_bass_kernel_spmd as _run

    given = {n: _np.ascontiguousarray(inputs[n]) for n in ["x"] + ["L0_conv_" + n for n in _L0] + ["L1_attn_" + n for n in _L1]
             + ["L1_ffn_" + m + "_" + g for m in ("U", "V", "b") for g in _GATES]}
    for n in ("q", "k", "v"):
        given[f"W{n}T"] = _np.ascontiguousarray(inputs[f"L1_attn_W{n}"].T)
    given.update(constants())
    nc = _bacc.Bacc("TRN2", target_bir_lowering=False, num_devices=1)
    arrays, aps = {}, {}
    for name, a in given.items():
        arrays[f"in_{name}"] = a
        aps[name] = nc.dram_tensor(f"in_{name}", a.shape, _mybir.dt.from_np(a.dtype), kind="ExternalInput").ap()
    out = nc.dram_tensor("out_0", (B, N, N, D), _mybir.dt.float32, kind="ExternalOutput").ap()
    build(nc, aps, out, "Internal")
    r = _run(nc, [arrays], core_ids=[0])
    return r.results[0]["out_0"]
```

```python
from contextlib import ExitStack

import numpy as np

import concourse.bass as bass
from concourse import mybir

F32 = mybir.dt.float32
I32 = mybir.dt.int32
F32R = mybir.dt.float32r
ALU = mybir.AluOpType
ACT = mybir.ActivationFunctionType
AX_X = mybir.AxisListType.X

P = 128
B, N, D = 2, 64, 256
H = 8
DK = D // H
G = 2
HG = H // G
T = N * N
KT = D // P
LN_EPS = 1e-5


class Phase:

    def __init__(self, nc, stack, name):
        self.nc, self.stack, self.name, self.sems = nc, stack, name, []
        stack.callback(self.clear)

    def clear(self):
        with self.nc.Block() as block:
            @block.sync
            def _(sp):
                for sem in self.sems:
                    sp.sem_clear(sem)

    def sb(self, name, shape, dtype=F32):
        return self.stack.enter_context(self.nc.sbuf_tensor(f"{self.name}_{name}", shape, dtype))

    def ps(self, name, shape):
        return self.stack.enter_context(self.nc.psum_tensor(f"{self.name}_{name}", shape, F32))

    def sem(self, name):
        self.sems.append(self.stack.enter_context(self.nc.semaphore(f"{self.name}_{name}")))
        return self.sems[-1]


HEAD = 32


def start_at_head(nc, sems, head=HEAD):
    with nc.Block() as block:
        @block.sync
        def _(sp):
            for sem in sems:
                sp.sem_inc(sem, head)


def k_rows(w):
    return w.rearrange("(k p) n -> p k n", p=P)


def scores_phase(nc, b, x, w_lk, w_rk, ident_d, att):
    with ExitStack() as stack:
        ph = Phase(nc, stack, f"sc{b}")
        ident = ph.sb("ident", [P, P])
        wlk = ph.sb("wlk", [P, KT, D])
        wrk = ph.sb("wrk", [P, KT, D])
        lkT = ph.sb("lkT", [P, G, T])
        rkT = ph.sb("rkT", [P, G, T])
        BLK = 512
        NBLK = T // BLK

        with ExitStack() as inner:
            pj = Phase(nc, inner, f"pj{b}")
            xin = pj.sb("xin", [P, 2, BLK // P, D])
            xT = pj.sb("xT", [P, 2, KT, BLK])
            psT = pj.ps("psT", [P, KT, BLK])
            psP = pj.ps("psP", [P, 2 * G, BLK])
            w_in = pj.sem("w_in")
            x_in = [pj.sem(f"x_in{s}") for s in range(2)]
            turned = pj.sem("turned")
            xT_done = pj.sem("xT_done")
            projected = pj.sem("projected")
            stored = pj.sem("stored")
            start_at_head(nc, [turned, xT_done, projected, stored])
            with nc.Block() as block:
                @block.sync
                def _(sp):
                    sp.dma_start(ident[:, :], ident_d).then_inc(w_in, 16)
                    sp.dma_start(wlk[:, :, :], k_rows(w_lk)).then_inc(w_in, 16)
                    sp.dma_start(wrk[:, :, :], k_rows(w_rk)).then_inc(w_in, 16)
                    xb = x[b].rearrange("x a d -> (x a) d")
                    with sp.Fori(0, NBLK // 2) as i:
                        for s in range(2):
                            n = i * 2 + s
                            sp.wait_ge(turned, HEAD + n - 1)
                            sp.dma_start(xin[:, s], xb[bass.ds(n * BLK, BLK), :].rearrange("(t p) d -> p t d", p=P)).then_inc(x_in[s], 16)

                @block.tensor
                def _(pe):
                    pe.wait_ge(w_in, 48)
                    with pe.Fori(0, NBLK // 2) as i:
                        for s in range(2):
                            n = i * 2 + s
                            pe.wait_ge(x_in[s], i * 16 + 16)
                            pe.wait_ge(xT_done, HEAD + n)
                            for k in range(KT):
                                for t in range(BLK // P):
                                    mm = pe.transpose(psT[:, k, t * P:(t + 1) * P], xin[:, s, t, k * P:(k + 1) * P], ident[:, :])
                            mm.then_inc(turned, 1)
                            pe.wait_ge(xT_done, HEAD + n + 1)
                            for j in range(2 * G):
                                w, g = (wlk, wrk)[j // G], j % G
                                pe.wait_ge(stored, HEAD + (n - 1) * (2 * G) + j + 1)
                                for k in range(KT):
                                    mm = pe.matmul(psP[:, j, :], w[:, k, g * P:(g + 1) * P], xT[:, s, k, :], start=(k == 0), stop=(k == KT - 1))
                                mm.then_inc(projected, 1)

                @block.scalar
                def _(act):
                    with act.Fori(0, NBLK // 2) as i:
                        for s in range(2):
                            n = i * 2 + s
                            act.wait_ge(turned, HEAD + n + 1)
                            act.wait_ge(projected, HEAD + (n - 1) * (2 * G))
                            nc.scalar.copy(xT[:, s], psT[:, :, :]).then_inc(xT_done, 1)

                @block.vector
                def _(dve):
                    with dve.Fori(0, NBLK // 2) as i:
                        for s in range(2):
                            n = i * 2 + s
                            for j in range(2 * G):
                                dst = (lkT, rkT)[j // G]
                                dve.wait_ge(projected, HEAD + n * (2 * G) + j + 1)
                                nc.vector.tensor_copy(dst[:, j % G, bass.ds(n * BLK, BLK)], psP[:, j, :]).then_inc(stored, 1)

        with ExitStack() as inner:
            sm = Phase(nc, inner, f"sm{b}")
            AB = 8
            NA = N // AB
            F = HG * N
            E = sm.sb("E", [P, N, F])
            lks = sm.sb("lks", [P, 2, G, AB, N])
            rks = sm.sb("rks", [P, 2, G, AB, N])
            part = sm.sb("part", [P, NA, F])
            top = sm.sb("top", [P, F])
            den = sm.sb("den", [P, F])
            rden = sm.sb("rden", [P, F])
            psS = sm.ps("psS", [P, 2, HG, AB * N])
            lk_cut = sm.sem("lk_cut")
            rk_cut = sm.sem("rk_cut")
            scored = sm.sem("scored")
            kept = sm.sem("kept")
            maxed = sm.sem("maxed")
            topped = sm.sem("topped")
            shifted = sm.sem("shifted")
            exped = sm.sem("exped")
            summed = sm.sem("summed")
            inverted = sm.sem("inverted")
            normed = sm.sem("normed")
            saved = sm.sem("saved")
            CH = 4
            CA = N // CH
            start_at_head(nc, [lk_cut, rk_cut, scored, kept, maxed])
            lk_v = lkT[:, :, :].rearrange("p g (x a) -> p g a x", a=N)
            rk_v = rkT[:, :, :].rearrange("p g (a y) -> p g a y", y=N)
            with nc.Block() as block:
                @block.gpsimd
                def _(pool):
                    with pool.Fori(0, NA // 2) as i:
                        for s in range(2):
                            n = i * 2 + s
                            pool.wait_ge(scored, HEAD + n - 1)
                            for g in range(G):
                                nc.gpsimd.tensor_copy(lks[:, s, g], lk_v[:, g, bass.ds(n * AB, AB), :]).then_inc(lk_cut, 1)

                @block.tensor
                def _(pe):
                    with pe.Fori(0, NA // 2) as i:
                        for s in range(2):
                            n = i * 2 + s
                            pe.wait_ge(lk_cut, HEAD + n * 2 + 2)
                            pe.wait_ge(rk_cut, HEAD + n * 2 + 2)
                            pe.wait_ge(kept, HEAD + n - 1)
                            for a in range(AB):
                                for g in range(G):
                                    for h in range(HG):
                                        r = slice(h * DK, (h + 1) * DK)
                                        mm = pe.matmul(psS[g * N:(g + 1) * N, s, h, a * N:(a + 1) * N], lks[r, s, g, a, :], rks[r, s, g, a, :],
                                                       start=True, stop=True, tile_position=(h * DK, g * N))
                            mm.then_inc(scored, 1)

                @block.scalar
                def _(act):
                    with act.Fori(0, NA // 2) as i:
                        for s in range(2):
                            n = i * 2 + s
                            act.wait_ge(scored, HEAD + n + 1)
                            nc.scalar.copy(E[:, bass.ds(n * AB, AB), :].rearrange("p a (h y) -> p h a y", h=HG),
                                           psS[:, s].rearrange("p h (a y) -> p h a y", a=AB)).then_inc(kept, 1)
                    for c in range(CH):
                        act.wait_ge(shifted, c + 1)
                        nc.scalar.activation(E[:, c * CA:(c + 1) * CA, :], E[:, c * CA:(c + 1) * CA, :], ACT.Exp,
                                             scale=float(DK) ** -0.5).then_inc(exped, 1)

                @block.vector
                def _(dve):
                    def cut(n, s):
                        dve.wait_ge(scored, HEAD + n - 1)
                        for g in range(G):
                            nc.vector.tensor_copy(rks[:, s, g], rk_v[:, g, bass.ds(n * AB, AB), :]).then_inc(rk_cut, 1)

                    def step_max(n):
                        dve.wait_ge(kept, HEAD + n + 1)
                        nc.vector.tensor_reduce(part[:, bass.ds(n, 1), :], E[:, bass.ds(n * AB, AB), :].rearrange("p a f -> p f a"),
                                                AX_X, ALU.max).then_inc(maxed, 1)

                    cut(0, 0)
                    with dve.Fori(0, NA // 2 - 1) as i:
                        cut(i * 2 + 1, 1)
                        step_max(i * 2)
                        cut(i * 2 + 2, 0)
                        step_max(i * 2 + 1)
                    cut(NA - 1, 1)
                    step_max(NA - 2)
                    step_max(NA - 1)
                    dve.wait_ge(maxed, HEAD + NA)
                    nc.vector.tensor_reduce(top[:, :], part[:, :, :].rearrange("p n f -> p f n"), AX_X, ALU.max).then_inc(topped, 1)
                    dve.wait_ge(topped, 1)
                    for c in range(CH):
                        nc.vector.tensor_tensor(E[:, c * CA:(c + 1) * CA, :], E[:, c * CA:(c + 1) * CA, :],
                                                top[:, :].unsqueeze(1).broadcast_to([P, CA, F]), ALU.subtract).then_inc(shifted, 1)
                    dve.wait_ge(exped, CH)
                    nc.vector.tensor_reduce(den[:, :], E[:, :, :].rearrange("p a f -> p f a"), AX_X, ALU.add).then_inc(summed, 1)
                    dve.wait_ge(summed, 1)
                    nc.vector.reciprocal(rden[:, :], den[:, :]).then_inc(inverted, 1)
                    dve.wait_ge(inverted, 1)
                    for c in range(CH):
                        nc.vector.tensor_tensor(E[:, c * CA:(c + 1) * CA, :], E[:, c * CA:(c + 1) * CA, :],
                                                rden[:, :].unsqueeze(1).broadcast_to([P, CA, F]), ALU.mult).then_inc(normed, 1)

                @block.sync
                def _(sp):
                    for c in range(CH):
                        sp.wait_ge(normed, c + 1)
                        for g in range(G):
                            sp.dma_start(att[b, :, c * CA:(c + 1) * CA, g * F:(g + 1) * F], E[g * N:(g + 1) * N, c * CA:(c + 1) * CA, :]).then_inc(saved, 16)
                    sp.wait_ge(saved, 16 * CH * G)


def mix_phase(nc, b, x, w_lv, w_rv, ident_d, sel_d, mask_d, att, o_d):
    with ExitStack() as stack:
        ph = Phase(nc, stack, f"mx{b}")
        ident = ph.sb("ident", [P, P])
        wlv = ph.sb("wlv", [P, KT, D])
        wrv = ph.sb("wrv", [P, KT, D])
        rv = ph.sb("rv", [P, N, D])
        xin = ph.sb("xin", [P, 2, D])
        xT = ph.sb("xT", [P, 2, KT, P])
        NXP = N // 2

        with ExitStack() as inner:
            rp = Phase(nc, inner, f"rp{b}")
            psT = rp.ps("psT", [P, 2, 512])
            psR = rp.ps("psR", [P, 2, 512])
            w_in = rp.sem("w_in")
            x_in = [rp.sem(f"x_in{s}") for s in range(2)]
            turned = rp.sem("turned")
            xT_done = rp.sem("xT_done")
            made = rp.sem("made")
            stored = rp.sem("stored")
            start_at_head(nc, [turned, xT_done, made, stored])
            with nc.Block() as block:
                @block.sync
                def _(sp):
                    sp.dma_start(ident[:, :], ident_d).then_inc(w_in, 16)
                    sp.dma_start(wrv[:, :, :], k_rows(w_rv)).then_inc(w_in, 16)
                    sp.dma_start(wlv[:, :, :], k_rows(w_lv)).then_inc(w_in, 16)
                    with sp.Fori(0, N // 2) as i:
                        for s in range(2):
                            n = i * 2 + s
                            sp.wait_ge(turned, HEAD + n - 1)
                            for c in range(2):
                                sp.dma_start(xin[c * N:(c + 1) * N, s, :], x[b, :, bass.ds(n, 1), :]).then_inc(x_in[s], 16)

                @block.tensor
                def _(pe):
                    def turn(n, s, i):
                        pe.wait_ge(x_in[s], i * 32 + 32)
                        pe.wait_ge(xT_done, HEAD + n - 1)
                        for k in range(KT):
                            mm = pe.transpose(psT[:, s, k * P:(k + 1) * P], xin[:, s, k * P:(k + 1) * P], ident[:, :])
                        mm.then_inc(turned, 1)

                    def make(n, s):
                        pe.wait_ge(xT_done, HEAD + n + 1)
                        pe.wait_ge(stored, HEAD + n - 1)
                        for k in range(KT):
                            mm = pe.matmul(psR[:, s, 0:D], xT[:, s, k, :], wrv[:, k, :], start=(k == 0), stop=(k == KT - 1))
                        mm.then_inc(made, 1)

                    pe.wait_ge(w_in, 48)
                    turn(0, 0, 0)
                    with pe.Fori(0, N // 2 - 1) as i:
                        turn(i * 2 + 1, 1, i)
                        make(i * 2, 0)
                        turn(i * 2 + 2, 0, i + 1)
                        make(i * 2 + 1, 1)
                    turn(N - 1, 1, N // 2 - 1)
                    make(N - 2, 0)
                    make(N - 1, 1)

                @block.scalar
                def _(act):
                    with act.Fori(0, N // 2) as i:
                        for s in range(2):
                            n = i * 2 + s
                            act.wait_ge(turned, HEAD + n + 1)
                            act.wait_ge(made, HEAD + n - 1)
                            nc.scalar.copy(xT[:, s], psT[:, s, 0:D].rearrange("p (k t) -> p k t", k=KT)).then_inc(xT_done, 1)

                @block.vector
                def _(dve):
                    with dve.Fori(0, N // 2) as i:
                        for s in range(2):
                            n = i * 2 + s
                            dve.wait_ge(made, HEAD + n + 1)
                            nc.vector.tensor_copy(rv[:, bass.ds(n, 1), :], psR[:, s, 0:D]).then_inc(stored, 1)

        with ExitStack() as inner:
            mp = Phase(nc, inner, f"mp{b}")
            YB = 8
            NYB = N // YB
            ZS = 4
            POOL_BLOCKS = (1, 4, 6)
            sel = mp.sb("sel", [P, 4, 32])
            mask = mp.sb("mask", [P, H])
            pair = mp.sb("pair", [P, 2, 2, H, N])
            lvs = mp.sb("lvs", [P, 2, D])
            Z = mp.sb("Z", [P, ZS, YB, D])
            cut = mp.sb("cut", [P, 2, 4, D])
            oS = mp.sb("oS", [P, 2, D])
            psT = mp.ps("psT", [P, 512])
            psL = mp.ps("psL", [P, 2, 512])
            psO = mp.ps("psO", [P, 2, 4, D])
            psN = mp.ps("psN", [P, 512])
            c_in = mp.sem("c_in")
            x_in = [mp.sem(f"x_in{s}") for s in range(2)]
            a_in = [mp.sem(f"a_in{s}") for s in range(2)]
            zeroed = mp.sem("zeroed")
            psO_clear = mp.sem("psO_clear")
            turned = mp.sem("turned")
            xT_done = mp.sem("xT_done")
            lv_made = mp.sem("lv_made")
            lv_kept = mp.sem("lv_kept")
            z_dve = mp.sem("z_dve")
            z_pool = mp.sem("z_pool")
            z_used = mp.sem("z_used")
            cut_done = mp.sem("cut_done")
            gathered = mp.sem("gathered")
            o_kept = mp.sem("o_kept")
            o_out = [mp.sem(f"o_out{s}") for s in range(2)]
            start_at_head(nc, [turned, xT_done, lv_made, lv_kept, z_dve, z_pool, z_used, cut_done, gathered, o_kept])
            dve_blocks = [k for k in range(NYB) if k not in POOL_BLOCKS]
            ND, NP = len(dve_blocks), len(POOL_BLOCKS)
            NQ = NYB // 2
            with nc.Block() as block:
                @block.sync
                def _(sp):
                    sp.dma_start(sel[:, :, :], sel_d).then_inc(c_in, 16)
                    sp.dma_start(mask[:, :], mask_d).then_inc(c_in, 16)
                    sp.wait_ge(zeroed, 2)

                    def load(n, s):
                        sp.wait_ge(turned, HEAD + n - 1)
                        sp.dma_start(xin[:, s, :], x[b, bass.ds(n * 2, 2)].rearrange("x a d -> (x a) d")).then_inc(x_in[s], 16)
                        sp.wait_ge(gathered, HEAD + (n - 1) * NQ)
                        for c in range(2):
                            sp.dma_start(pair[c * N:(c + 1) * N, s, c], att[b, bass.ds(n * 2 + c, 1)].rearrange("o a (h y) -> (o a) h y", y=N)).then_inc(a_in[s], 16)

                    def store(n, s):
                        sp.wait_ge(o_kept, HEAD + n + 1)
                        sp.dma_start(o_d[b, bass.ds(n, 1)].rearrange("o r d -> (o r) d"), oS[:, s, :]).then_inc(o_out[s], 16)

                    load(0, 0)
                    load(1, 1)
                    with sp.Fori(0, NXP // 2 - 1) as i:
                        for s in range(2):
                            store(i * 2 + s, s)
                            load(i * 2 + s + 2, s)
                    for s in range(2):
                        store(NXP - 2 + s, s)
                        sp.wait_ge(o_out[s], 16 * (NXP // 2))

                @block.tensor
                def _(pe):
                    def turn(n, s, r):
                        pe.wait_ge(x_in[s], r * 16 + 16)
                        pe.wait_ge(xT_done, HEAD + n)
                        for k in range(KT):
                            mm = pe.transpose(psT[:, k * P:(k + 1) * P], xin[:, s, k * P:(k + 1) * P], ident[:, :])
                        mm.then_inc(turned, 1)

                    def lv(n, s):
                        pe.wait_ge(xT_done, HEAD + n + 1)
                        pe.wait_ge(z_dve, HEAD + (n - 1) * ND)
                        for k in range(KT):
                            mm = pe.matmul(psL[:, s, 0:D], xT[:, s, k, :], wlv[:, k, :], start=(k == 0), stop=(k == KT - 1))
                        mm.then_inc(lv_made, 1)

                    def mix(n, s, c):
                        pe.wait_ge(cut_done, HEAD + n * NQ + c - 1)
                        for k in (2 * c, 2 * c + 1):
                            if k in POOL_BLOCKS:
                                pe.wait_ge(z_pool, HEAD + n * NP + POOL_BLOCKS.index(k) + 1)
                            else:
                                pe.wait_ge(z_dve, HEAD + n * ND + dve_blocks.index(k) + 1)
                            for y in range(YB):
                                j, q = y % 4, 2 * (k % 2) + y // 4
                                mm = pe.matmul(psO[32 * j:32 * j + 2 * H, c % 2, q, :], pair[:, s, :, :, k * YB + y], Z[:, k % ZS, y, :],
                                               start=True, stop=True, tile_position=(0, 32 * j))
                            mm.then_inc(z_used, 1)

                    def gather(n, c):
                        pe.wait_ge(cut_done, HEAD + n * NQ + c + 1)
                        if c == 0:
                            pe.wait_ge(o_kept, HEAD + n)
                        for q in range(4):
                            mm = pe.matmul(psN[32 * c:32 * c + 32, 0:D], sel[:, q, :], cut[:, c % 2, q, :], start=(q == 0), stop=(q == 3),
                                           tile_position=(0, 32 * c))
                        mm.then_inc(gathered, 1)

                    def step(n, s, r, first=False, last=False):
                        for c in range(NQ):
                            if c == 0:
                                pe.wait_ge(a_in[s], r * 32 + 32)
                            mix(n, s, c)
                            if c > 0:
                                gather(n, c - 1)
                            elif not first:
                                gather(n - 1, NQ - 1)
                            if c == 1 and not last:
                                turn(n + 1, 1 - s, r + s)
                            if c == 2 and not last:
                                lv(n + 1, 1 - s)
                        if last:
                            gather(n, NQ - 1)

                    pe.wait_ge(zeroed, 2)
                    pe.wait_ge(psO_clear, 1)
                    pe.wait_ge(c_in, 32)
                    turn(0, 0, 0)
                    lv(0, 0)
                    step(0, 0, 0, first=True)
                    step(1, 1, 0)
                    with pe.Fori(1, NXP // 2 - 1) as i:
                        for s in range(2):
                            step(i * 2 + s, s, i)
                    step(NXP - 2, 0, NXP // 2 - 1)
                    step(NXP - 1, 1, NXP // 2 - 1, last=True)

                @block.scalar
                def _(act):
                    def keep_xT(n, s):
                        act.wait_ge(turned, HEAD + n + 1)
                        nc.scalar.copy(xT[:, s], psT[:, 0:D].rearrange("p (k t) -> p k t", k=KT)).then_inc(xT_done, 1)

                    def keep_lv(n, s):
                        act.wait_ge(lv_made, HEAD + n + 1)
                        act.wait_ge(z_pool, HEAD + (n - 1) * NP)
                        nc.scalar.copy(lvs[:, s, :], psL[:, s, 0:D]).then_inc(lv_kept, 1)

                    def cut_heads(n, c):
                        act.wait_ge(z_used, HEAD + n * NYB + 2 * c + 2)
                        act.wait_ge(gathered, HEAD + n * NQ + c - 1)
                        for h in range(H):
                            ins = nc.scalar.activation(cut[:, c % 2, :, h * DK:(h + 1) * DK], psO[:, c % 2, :, h * DK:(h + 1) * DK], ACT.Copy,
                                                       scale=mask[:, h:h + 1])
                        ins.then_inc(cut_done, 1)

                    def keep_o(n, s, r):
                        act.wait_ge(gathered, HEAD + n * NQ + NQ)
                        if r is not None:
                            act.wait_ge(o_out[s], r * 16)
                        nc.scalar.copy(oS[:, s, :], psN[:, 0:D]).then_inc(o_kept, 1)

                    def step(n, s, r, first=False, last=False):
                        cut_heads(n, 0)
                        if not first:
                            keep_o(n - 1, 1 - s, r)
                        cut_heads(n, 1)
                        if not last:
                            keep_xT(n + 1, 1 - s)
                        cut_heads(n, 2)
                        if not last:
                            keep_lv(n + 1, 1 - s)
                        cut_heads(n, 3)

                    act.wait_ge(c_in, 32)
                    keep_xT(0, 0)
                    keep_lv(0, 0)
                    step(0, 0, None, first=True)
                    step(1, 1, None)
                    step(2, 0, None)
                    step(3, 1, 1)
                    with act.Fori(2, NXP // 2 - 1) as i:
                        step(i * 2, 0, i - 1)
                        step(i * 2 + 1, 1, i)
                    step(NXP - 2, 0, NXP // 2 - 2)
                    step(NXP - 1, 1, NXP // 2 - 1, last=True)
                    keep_o(NXP - 1, 1, NXP // 2 - 1)

                @block.vector
                def _(dve):
                    nc.vector.memset(psO[:, :, :, :], 0.0).then_inc(psO_clear, 1)
                    nc.vector.memset(pair[0:N, :, 1], 0.0).then_inc(zeroed, 1)
                    nc.vector.memset(pair[N:P, :, 0], 0.0).then_inc(zeroed, 1)
                    with dve.Fori(0, NXP // 2) as i:
                        for s in range(2):
                            n = i * 2 + s
                            dve.wait_ge(lv_kept, HEAD + n + 1)
                            for k in dve_blocks:
                                dve.wait_ge(z_used, HEAD + n * NYB + k + 1 - ZS)
                                nc.vector.tensor_tensor(Z[:, k % ZS], psL[:, s, 0:D].unsqueeze(1).broadcast_to([P, YB, D]), rv[:, k * YB:(k + 1) * YB, :],
                                                        ALU.mult).then_inc(z_dve, 1)

                @block.gpsimd
                def _(pool):
                    with pool.Fori(0, NXP // 2) as i:
                        for s in range(2):
                            n = i * 2 + s
                            pool.wait_ge(lv_kept, HEAD + n + 1)
                            for k in POOL_BLOCKS:
                                pool.wait_ge(z_used, HEAD + n * NYB + k + 1 - ZS)
                                nc.gpsimd.tensor_tensor(Z[:, k % ZS], lvs[:, s, :].unsqueeze(1).broadcast_to([P, YB, D]), rv[:, k * YB:(k + 1) * YB, :],
                                                        ALU.mult).then_inc(z_pool, 1)


def dense_phase(nc, x, o_d, w_out, g1, b1n, w1, b1, w2, b2, g2, b2n, ident_d, t_d, xlT_d):
    NT = B * T // P
    F1 = 2 * D
    MT = F1 // P
    with ExitStack() as stack:
        ph = Phase(nc, stack, "de")
        ident = ph.sb("ident", [P, P])
        wo = ph.sb("wo", [P, KT, D])
        wa = ph.sb("wa", [P, KT, F1])
        wb = ph.sb("wb", [P, MT, D])
        row = {name: ph.sb(name, [P, n]) for name, n in (("g1", D), ("b1n", D), ("b1", F1), ("b2", D), ("g2", D), ("b2n", D))}
        eps = ph.sb("eps", [P, 1])
        oin = ph.sb("oin", [P, 2, D])
        xres = ph.sb("xres", [P, 2, D])
        oT = ph.sb("oT", [P, 2, KT, P])
        hT = ph.sb("hT", [P, 2, KT, P])
        mT = ph.sb("mT", [P, 2, MT, P])
        xT = ph.sb("xT", [P, 2, KT, P])
        h0 = ph.sb("h0", [P, 2, D])
        hn = ph.sb("hn", [P, 2, D])
        hg = ph.sb("hg", [P, 2, D])
        hs = ph.sb("hs", [P, 2, D])
        hb2 = ph.sb("hb2", [P, NT, D])
        ma = ph.sb("ma", [P, 2, F1])
        m = ph.sb("m", [P, 2, F1])
        t0 = ph.sb("t0", [P, 2, D])
        tn = ph.sb("tn", [P, 2, D])
        tg = ph.sb("tg", [P, 2, D])
        ts = ph.sb("ts", [P, 2, D])
        xl = ph.sb("xl", [P, 2, D])
        stats = ph.sb("stats", [P, 3, 2, 6])
        mv = ph.sb("mv", [P, 3, 2, 2])
        std = ph.sb("std", [P, 3, 2, 1])
        rstd = ph.sb("rstd", [P, 3, 2, 1])
        ps_o, ps_h, ps_m, ps_x, ps_1, ps_2, ps_3 = (ph.ps(f"ps{j}", [P, 512]) for j in range(7))
        w_in = ph.sem("w_in")
        eps_set = ph.sem("eps_set")
        passed = ph.sem("passed")
        in_ = [ph.sem(f"in{s}") for s in range(2)]
        t_out = [ph.sem(f"t_out{s}") for s in range(2)]
        x_out = [ph.sem(f"x_out{s}") for s in range(2)]
        names = ("o_turned h_turned m_turned x_turned oT_kept hT_kept mT_kept xT_kept made1 made2 made3 "
                 "added1 biased relued added3 h_scaled h_done hb2_done t_scaled t_done").split()
        q = {n: ph.sem(n) for n in names}
        ln = [{n: ph.sem(f"{n}{j}") for n in ("stated", "aggregated", "rooted", "inverted", "normed")} for j in range(3)]
        start_at_head(nc, list(q.values()) + [v for d in ln for v in d.values()] + t_out + x_out)
        weights = [(ident[:, :], ident_d), (wo[:, :, :], k_rows(w_out)), (wa[:, :, :], k_rows(w1)), (wb[:, :, :], k_rows(w2))] + [
            (row[n][:, :], v.rearrange("(o n) -> o n", o=1).broadcast_to([P, row[n].shape[1]]))
            for n, v in (("g1", g1), ("b1n", b1n), ("b1", b1), ("b2", b2), ("g2", g2), ("b2n", b2n))]

        def iterations(eng, body):
            def fixed(i):
                body(i, i % 2, i // 2, lambda k: 0 <= i - 2 * k < NT)
            for i in range(8):
                fixed(i)
            with eng.Fori(4, NT // 2) as r:
                for s in range(2):
                    body(r * 2 + s, s, r, lambda k: True)
            for i in range(NT, NT + 8):
                fixed(i)

        with nc.Block() as block:
            @block.sync
            def _(sp):
                for dst, src in weights:
                    sp.dma_start(dst, src).then_inc(w_in, 16)

                def body(i, s, r, live):
                    if live(0):
                        sp.wait_ge(q["o_turned"], HEAD + i - 1)
                        sp.wait_ge(q["added1"], HEAD + i - 1)
                        ox = o_d.rearrange("b n (y x) d -> (b n) x y d", x=2)
                        for c in range(2):
                            sp.dma_start(oin[c * N:(c + 1) * N, s, :], ox[bass.ds(i, 1), c].rearrange("o y d -> (o y) d")).then_inc(in_[s], 16)
                        sp.dma_start(xres[:, s, :], x.rearrange("b x y d -> (b x y) d")[bass.ds(i * P, P), :]).then_inc(in_[s], 16)
                    if live(3):
                        n = i - 6
                        sp.wait_ge(q["t_done"], HEAD + n + 1)
                        sp.dma_start(t_d.rearrange("b t d -> (b t) d")[bass.ds(n * P, P), :], ts[:, s, :]).then_inc(t_out[s], 16)
                    if live(4):
                        n = i - 8
                        sp.wait_ge(q["xT_kept"], HEAD + n + 1)
                        sp.dma_start(xlT_d[:, :, bass.ds(n * P, P)].rearrange("k p t -> p k t"), xT[:, s]).then_inc(x_out[s], 16)

                iterations(sp, body)
                for s in range(2):
                    sp.wait_ge(t_out[s], HEAD + 16 * (NT // 2))
                    sp.wait_ge(x_out[s], HEAD + 16 * (NT // 2))

            @block.tensor
            def _(pe):
                def turn(dst, src, blocks, done):
                    for k in range(blocks):
                        mm = pe.transpose(dst[:, k * P:(k + 1) * P], src[:, k * P:(k + 1) * P], ident[:, :])
                    mm.then_inc(done, 1)

                def product(dst, lhsT, w, blocks, done):
                    for k in range(blocks):
                        mm = pe.matmul(dst, lhsT[:, k, :], w[:, k, :], start=(k == 0), stop=(k == blocks - 1))
                    mm.then_inc(done, 1)

                def body(i, s, r, live):
                    if live(0):
                        pe.wait_ge(in_[s], r * 48 + 48)
                        turn(ps_o, oin[:, s], KT, q["o_turned"])
                    if live(1):
                        pe.wait_ge(q["h_done"], HEAD + i - 2 + 1)
                        turn(ps_h, hs[:, s], KT, q["h_turned"])
                    if live(2):
                        pe.wait_ge(q["relued"], HEAD + i - 4 + 1)
                        turn(ps_m, m[:, s], MT, q["m_turned"])
                    if live(4):
                        pe.wait_ge(ln[2]["normed"], HEAD + i - 8 + 1)
                        pe.wait_ge(q["xT_kept"], HEAD + i - 8)
                        turn(ps_x, xl[:, s], KT, q["x_turned"])
                    if live(0):
                        pe.wait_ge(q["oT_kept"], HEAD + i + 1)
                        pe.wait_ge(q["added1"], HEAD + i)
                        product(ps_1[:, 0:D], oT[:, s], wo, KT, q["made1"])
                    if live(1):
                        pe.wait_ge(q["hT_kept"], HEAD + i - 2 + 1)
                        pe.wait_ge(q["biased"], HEAD + i - 2)
                        product(ps_2[:, :], hT[:, s], wa, KT, q["made2"])
                    if live(2):
                        pe.wait_ge(q["mT_kept"], HEAD + i - 4 + 1)
                        pe.wait_ge(q["added3"], HEAD + i - 4)
                        product(ps_3[:, 0:D], mT[:, s], wb, MT, q["made3"])

                pe.wait_ge(w_in, 16 * len(weights))
                iterations(pe, body)

            @block.scalar
            def _(act):
                def keep(dst, src, blocks, done):
                    nc.scalar.copy(dst, src[:, 0:blocks * P].rearrange("p (k t) -> p k t", k=blocks)).then_inc(done, 1)

                def root(j, n, s):
                    act.wait_ge(ln[j]["aggregated"], HEAD + n + 1)
                    nc.scalar.activation(std[:, j, s, :], mv[:, j, s, 1:2], ACT.Sqrt, bias=eps[:, :]).then_inc(ln[j]["rooted"], 1)

                def body(i, s, r, live):
                    if live(3):
                        root(2, i - 6, s)
                    if live(0):
                        act.wait_ge(q["o_turned"], HEAD + i + 1)
                        keep(oT[:, s], ps_o, KT, q["oT_kept"])
                    if live(1):
                        act.wait_ge(q["h_turned"], HEAD + i - 2 + 1)
                        keep(hT[:, s], ps_h, KT, q["hT_kept"])
                    if live(2):
                        act.wait_ge(q["m_turned"], HEAD + i - 4 + 1)
                        keep(mT[:, s], ps_m, MT, q["mT_kept"])
                    if live(4):
                        act.wait_ge(q["x_turned"], HEAD + i - 8 + 1)
                        act.wait_ge(x_out[s], HEAD + (r - 4) * 16)
                        keep(xT[:, s], ps_x, KT, q["xT_kept"])
                    if live(0):
                        root(0, i, s)
                    if live(1):
                        act.wait_ge(q["biased"], HEAD + i - 2 + 1)
                        nc.scalar.activation(m[:, s], ma[:, s], ACT.Relu).then_inc(q["relued"], 1)
                    if live(2):
                        root(1, i - 4, s)

                act.wait_ge(eps_set, 1)
                iterations(act, body)

            @block.vector
            def _(dve):
                def moments(j, n, s, src):
                    nc.vector.bn_stats(stats[:, j, s, :], src).then_inc(ln[j]["stated"], 1)
                    dve.wait_ge(ln[j]["stated"], HEAD + n + 1)
                    dve.sem_inc(passed, 1)
                    nc.vector.bn_aggr(mv[:, j, s, :], stats[:, j, s, :]).then_inc(ln[j]["aggregated"], 1)

                def normalise(j, n, s, dst, src):
                    dve.wait_ge(ln[j]["rooted"], HEAD + n + 1)
                    nc.vector.reciprocal(rstd[:, j, s, :], std[:, j, s, :]).then_inc(ln[j]["inverted"], 1)
                    dve.wait_ge(ln[j]["inverted"], HEAD + n + 1)
                    nc.vector.tensor_scalar(dst, src, mv[:, j, s, 0:1], rstd[:, j, s, :], ALU.subtract, ALU.mult).then_inc(ln[j]["normed"], 1)

                def body(i, s, r, live):
                    if live(3):
                        dve.wait_ge(q["t_done"], HEAD + i - 6 + 1)
                        moments(2, i - 6, s, ts[:, s])
                    if live(0):
                        dve.wait_ge(in_[s], r * 48 + 48)
                        dve.wait_ge(q["made1"], HEAD + i + 1)
                        nc.vector.tensor_tensor(h0[:, s], ps_1[:, 0:D], xres[:, s], ALU.add).then_inc(q["added1"], 1)
                        dve.wait_ge(q["added1"], HEAD + i + 1)
                        moments(0, i, s, h0[:, s])
                    if live(3):
                        dve.wait_ge(q["x_turned"], HEAD + i - 6 - 1)
                        normalise(2, i - 6, s, xl[:, s], ts[:, s])
                    if live(1):
                        dve.wait_ge(q["made2"], HEAD + i - 2 + 1)
                        dve.wait_ge(q["relued"], HEAD + i - 2 - 1)
                        nc.vector.tensor_tensor(ma[:, s], ps_2[:, :], row["b1"][:, :], ALU.add).then_inc(q["biased"], 1)
                    if live(0):
                        dve.wait_ge(q["h_scaled"], HEAD + i - 1)
                        normalise(0, i, s, hn[:, s], h0[:, s])
                    if live(2):
                        dve.wait_ge(q["made3"], HEAD + i - 4 + 1)
                        dve.wait_ge(q["hb2_done"], HEAD + i - 4 + 1)
                        nc.vector.tensor_tensor(t0[:, s], ps_3[:, 0:D], hb2[:, bass.ds(i - 4, 1), :].rearrange("p o d -> p (o d)"), ALU.add).then_inc(q["added3"], 1)
                        dve.wait_ge(q["added3"], HEAD + i - 4 + 1)
                        moments(1, i - 4, s, t0[:, s])
                        dve.wait_ge(q["t_scaled"], HEAD + i - 4 - 1)
                        normalise(1, i - 4, s, tn[:, s], t0[:, s])

                nc.vector.memset(eps[:, :], LN_EPS).then_inc(eps_set, 1)
                dve.wait_ge(w_in, 16 * len(weights))
                iterations(dve, body)

            @block.gpsimd
            def _(pool):
                def body(i, s, r, live):
                    if live(0):
                        pool.wait_ge(ln[0]["normed"], HEAD + i + 1)
                        nc.gpsimd.tensor_tensor(hg[:, s], hn[:, s], row["g1"][:, :], ALU.mult).then_inc(q["h_scaled"], 1)
                        pool.wait_ge(q["h_scaled"], HEAD + i + 1)
                        pool.wait_ge(q["h_turned"], HEAD + i - 1)
                        nc.gpsimd.tensor_tensor(hs[:, s], hg[:, s], row["b1n"][:, :], ALU.add).then_inc(q["h_done"], 1)
                        pool.wait_ge(q["h_done"], HEAD + i + 1)
                        nc.gpsimd.tensor_tensor(hb2[:, bass.ds(i, 1), :].rearrange("p o d -> p (o d)"), hs[:, s], row["b2"][:, :], ALU.add).then_inc(q["hb2_done"], 1)
                    if live(2):
                        n = i - 4
                        pool.wait_ge(ln[1]["normed"], HEAD + n + 1)
                        nc.gpsimd.tensor_tensor(tg[:, s], tn[:, s], row["g2"][:, :], ALU.mult).then_inc(q["t_scaled"], 1)
                        pool.wait_ge(q["t_scaled"], HEAD + n + 1)
                        pool.wait_ge(t_out[s], HEAD + (r - 2) * 16)
                        pool.wait_ge(ln[2]["normed"], HEAD + n - 1)
                        nc.gpsimd.tensor_tensor(ts[:, s], tg[:, s], row["b2n"][:, :], ALU.add).then_inc(q["t_done"], 1)

                pool.wait_ge(w_in, 16 * len(weights))
                iterations(pool, body)


def attention_phase(nc, b, t_d, xlT_d, wqT, bq, wkT, bk, wvT, bv, ident_d, t2_d):
    NT = T // P
    BLK = 512
    NBLK = T // BLK
    KB = BLK // P
    with ExitStack() as stack:
        ph = Phase(nc, stack, f"at{b}")
        ident = ph.sb("ident", [P, P])
        qT = ph.sb("qT", [P, KT, T])
        k_hi = ph.sb("k_hi", [P, KT, T], F32R)
        k_lo = ph.sb("k_lo", [P, KT, T], F32R)
        v_hi = ph.sb("v_hi", [P, T // P, D], F32R)
        v_lo = ph.sb("v_lo", [P, T // P, D], F32R)

        with ExitStack() as inner:
            pj = Phase(nc, inner, f"qk{b}")
            w = [pj.sb(n, [P, KT, D]) for n in ("wq", "wk", "wv")]
            bias = [pj.sb(n, [P, KT]) for n in ("bq", "bk")]
            bvr = pj.sb("bvr", [P, D])
            xs = pj.sb("xs", [P, 2, KT, BLK])
            v = pj.sb("v", [P, 2, 2, D])
            psP = pj.ps("psP", [P, 2 * KT, BLK])
            psV = pj.ps("psV", [P, KB, D])
            w_in = pj.sem("w_in")
            x_in = [pj.sem(f"x_in{s}") for s in range(2)]
            made = pj.sem("made")
            q_kept, k_hi_kept, v_hi_kept = (pj.sem(n) for n in ("q_kept", "k_hi_kept", "v_hi_kept"))
            k_lo_kept, v_biased = (pj.sem(n) for n in ("k_lo_kept", "v_biased"))
            passed = pj.sem("passed")
            v_lo_kept = pj.sem("v_lo_kept")
            start_at_head(nc, [made, q_kept, k_hi_kept, v_hi_kept, k_lo_kept, v_biased, v_lo_kept])
            loads = [(ident[:, :], ident_d), (w[0][:, :, :], k_rows(wqT)), (w[1][:, :, :], k_rows(wkT)), (w[2][:, :, :], k_rows(wvT)),
                     (bias[0][:, :], bq.rearrange("(k p) -> p k", p=P)), (bias[1][:, :], bk.rearrange("(k p) -> p k", p=P)),
                     (bvr[:, :], bv.rearrange("(o n) -> o n", o=1).broadcast_to([P, D]))]
            with nc.Block() as block:
                @block.sync
                def _(sp):
                    with nc.allow_non_contiguous_dma("two biases of 256 numbers, one to a partition"):
                        for dst, src in loads:
                            sp.dma_start(dst, src).then_inc(w_in, 16)
                    with sp.Fori(0, NBLK // 2) as r:
                        for s in range(2):
                            n = r * 2 + s
                            sp.wait_ge(made, HEAD + (n - 1) * 6)
                            sp.dma_start(xs[:, s], xlT_d[:, :, bass.ds(n * BLK + b * T, BLK)].rearrange("k p t -> p k t")).then_inc(x_in[s], 16)

                @block.tensor
                def _(pe):
                    pe.wait_ge(w_in, 16 * len(loads))
                    with pe.Fori(0, NBLK // 2) as r:
                        for s in range(2):
                            n = r * 2 + s
                            pe.wait_ge(x_in[s], r * 16 + 16)
                            for j in range(2 * KT):
                                pe.wait_ge((q_kept, k_lo_kept)[j // KT], HEAD + (n - 1) * KT + j % KT + 1)
                                for k in range(KT):
                                    mm = pe.matmul(psP[:, j, :], w[j // KT][:, k, (j % KT) * P:(j % KT + 1) * P], xs[:, s, k, :], start=(k == 0), stop=(k == KT - 1))
                                mm.then_inc(made, 1)
                            for u in range(2):
                                pe.wait_ge(v_biased, HEAD + (n - 1) * 2 + u + 1)
                                for t in (2 * u, 2 * u + 1):
                                    for k in range(KT):
                                        mm = pe.matmul(psV[:, t, :], xs[:, s, k, t * P:(t + 1) * P], w[2][:, k, :], start=(k == 0), stop=(k == KT - 1))
                                mm.then_inc(made, 1)

                @block.scalar
                def _(act):
                    act.wait_ge(w_in, 16 * len(loads))
                    with act.Fori(0, NBLK // 2) as r:
                        for s in range(2):
                            n = r * 2 + s
                            for j in range(2 * KT):
                                act.wait_ge(made, HEAD + n * 6 + j + 1)
                                nc.scalar.activation((qT, k_hi)[j // KT][:, j % KT, bass.ds(n * BLK, BLK)], psP[:, j, :], ACT.Identity,
                                                     bias=bias[j // KT][:, j % KT:j % KT + 1]).then_inc((q_kept, k_hi_kept)[j // KT], 1)
                            for u in range(2):
                                act.wait_ge(v_biased, HEAD + n * 2 + u + 1)
                                nc.scalar.copy(v_hi[:, bass.ds(n * KB + 2 * u, 2), :], v[:, u]).then_inc(v_hi_kept, 1)

                @block.gpsimd
                def _(pool):
                    with pool.Fori(0, NBLK // 2) as r:
                        for s in range(2):
                            n = r * 2 + s
                            for u in range(2):
                                part = bass.ds(n * KB + 2 * u, 2)
                                pool.wait_ge(v_hi_kept, HEAD + n * 2 + u + 1)
                                pool.sem_inc(passed, 1)
                                nc.gpsimd.tensor_tensor(v_lo[:, part, :], v[:, u], v_hi[:, part, :], ALU.subtract).then_inc(v_lo_kept, 1)

                @block.vector
                def _(dve):
                    dve.wait_ge(w_in, 16 * len(loads))
                    with dve.Fori(0, NBLK // 2) as r:
                        for s in range(2):
                            n = r * 2 + s
                            for k in range(KT):
                                part = bass.ds(n * BLK, BLK)
                                dve.wait_ge(k_hi_kept, HEAD + n * KT + k + 1)
                                nc.vector.scalar_tensor_tensor(out=k_lo[:, k, part], in0=psP[:, KT + k, :], scalar=bias[1][:, k:k + 1], in1=k_hi[:, k, part],
                                                               op0=ALU.add, op1=ALU.subtract).then_inc(k_lo_kept, 1)
                            for u in range(2):
                                dve.wait_ge(made, HEAD + n * 6 + 4 + u + 1)
                                dve.wait_ge(v_lo_kept, HEAD + (n - 1) * 2 + u + 1)
                                nc.vector.tensor_tensor(v[:, u], psV[:, 2 * u:2 * u + 2, :],
                                                        bvr[:, :].unsqueeze(1).broadcast_to([P, 2, D]), ALU.add).then_inc(v_biased, 1)

        with ExitStack() as inner:
            ap = Phase(nc, inner, f"sv{b}")
            SCALE = float(D) ** -0.5
            q_hi = ap.sb("q_hi", [P, 2, KT, P], F32R)
            q_lo = ap.sb("q_lo", [P, 2, KT, P], F32R)
            S = ap.sb("S", [P, 2, NBLK, BLK])
            mx = ap.sb("mx", [P, 2, NBLK])
            top = ap.sb("top", [P, 2, 1])
            shift = ap.sb("shift", [P, 2, 1])
            part = ap.sb("part", [P, 2, NBLK])
            den = ap.sb("den", [P, 2, 1])
            rden = ap.sb("rden", [P, 2, 1])
            p_hi = ap.sb("p_hi", [P, 2, KB, P], F32R)
            p_lo = ap.sb("p_lo", [P, 2, KB, P], F32R)
            t = ap.sb("t", [P, 2, D])
            psS = ap.ps("psS", [P, 4, BLK])
            psT = ap.ps("psT", [P, 2, BLK])
            psO = ap.ps("psO", [P, 2, 512])
            t_in = [ap.sem(f"t_in{s}") for s in range(2)]
            t2_out = [ap.sem(f"t2_out{s}") for s in range(2)]
            q_hi_cut = ap.sem("q_hi_cut")
            passed = ap.sem("passed")
            q_cut = ap.sem("q_cut")
            scored = ap.sem("scored")
            kept = ap.sem("kept")
            maxed = ap.sem("maxed")
            topped = ap.sem("topped")
            shifted = ap.sem("shifted")
            exped = ap.sem("exped")
            turned = ap.sem("turned")
            hi_kept = ap.sem("hi_kept")
            pT_kept = ap.sem("pT_kept")
            weighed = ap.sem("weighed")
            summed = ap.sem("summed")
            inverted = ap.sem("inverted")
            added = ap.sem("added")
            start_at_head(nc, [q_hi_cut, hi_kept, q_cut, scored, kept, maxed, topped, shifted, exped, turned, pT_kept, weighed, summed, inverted, added] + t2_out)
            C = NBLK

            def tiles(eng, body):
                body(0, 0, 0, True)
                body(1, 1, 0, True)
                with eng.Fori(1, NT // 2 - 1) as r:
                    for s in range(2):
                        body(r * 2 + s, s, r, True)
                body(NT - 2, 0, NT // 2 - 1, True)
                body(NT - 1, 1, NT // 2 - 1, False)

            with nc.Block() as block:
                @block.sync
                def _(sp):
                    def load(n, s, r):
                        sp.wait_ge(t2_out[s], HEAD + r * 16)
                        sp.dma_start(t[:, s, :], t_d[b, bass.ds(n * P, P), :]).then_inc(t_in[s], 16)

                    def save(n, s):
                        sp.wait_ge(added, HEAD + n + 1)
                        sp.dma_start(t2_d[b, bass.ds(n * P, P), :], t[:, s, :]).then_inc(t2_out[s], 16)

                    for s in range(2):
                        load(s, s, 0)
                    with sp.Fori(0, NT // 2 - 1) as r:
                        for s in range(2):
                            save(r * 2 + s, s)
                            load(r * 2 + s + 2, s, r + 1)
                    for s in range(2):
                        save(NT - 2 + s, s)
                    for s in range(2):
                        sp.wait_ge(t2_out[s], HEAD + 16 * (NT // 2))

                @block.gpsimd
                def _(pool):
                    with pool.Fori(0, NT // 2) as r:
                        for s in range(2):
                            n = r * 2 + s
                            pool.wait_ge(scored, HEAD + (n - 1) * C)
                            nc.gpsimd.tensor_copy(q_hi[:, s], qT[:, :, bass.ds(n * P, P)]).then_inc(q_hi_cut, 1)
                            pool.wait_ge(q_hi_cut, HEAD + n + 1)
                            pool.sem_inc(passed, 1)
                            nc.gpsimd.tensor_tensor(q_lo[:, s], qT[:, :, bass.ds(n * P, P)], q_hi[:, s], ALU.subtract).then_inc(q_cut, 1)

                @block.tensor
                def _(pe):
                    def score(n, s, c):
                        if c == 0:
                            pe.wait_ge(q_cut, HEAD + n + 1)
                        pe.wait_ge(kept, HEAD + n * C + c - 3)
                        terms = [(a, b, k) for k in range(KT) for a, b in ((q_hi, k_hi), (q_hi, k_lo), (q_lo, k_hi))]
                        for i, (a, b, k) in enumerate(terms):
                            mm = pe.matmul(psS[:, c % 4, :], a[:, s, k, :], b[:, k, c * BLK:(c + 1) * BLK], start=(i == 0), stop=(i == len(terms) - 1))
                        mm.then_inc(scored, 1)

                    def turn(n, s, c):
                        pe.wait_ge(exped, HEAD + n * C + c + 1)
                        pe.wait_ge(pT_kept, HEAD + n * C + c - 1)
                        for t in range(KB):
                            mm = pe.transpose(psT[:, c % 2, t * P:(t + 1) * P], S[:, s, c, t * P:(t + 1) * P], ident[:, :])
                        mm.then_inc(turned, 1)

                    def weigh(n, s, c):
                        pe.wait_ge(pT_kept, HEAD + n * C + c + 1)
                        if c == 0:
                            pe.wait_ge(added, HEAD + n - 1)
                        terms = [(a, b, t) for t in range(KB) for a, b in ((p_hi, v_hi), (p_hi, v_lo), (p_lo, v_hi))]
                        for i, (a, b, t) in enumerate(terms):
                            mm = pe.matmul(psO[:, s, 0:D], a[:, c % 2, t, :], b[:, c * KB + t, :],
                                           start=(c == 0 and i == 0), stop=(c == C - 1 and i == len(terms) - 1))
                        mm.then_inc(weighed, 1)

                    def body(n, s, r, ahead):
                        for step in range(C + 4):
                            if ahead and step < C:
                                score(n + 1, 1 - s, step)
                            if 3 <= step < C + 3:
                                turn(n, s, step - 3)
                            if 4 <= step:
                                weigh(n, s, step - 4)

                    for c in range(C):
                        score(0, 0, c)
                    tiles(pe, body)

                @block.scalar
                def _(act):
                    def keep(n, s, c):
                        act.wait_ge(scored, HEAD + n * C + c + 1)
                        nc.scalar.copy(S[:, s, c, :], psS[:, c % 4, :]).then_inc(kept, 1)

                    def exponent(n, s, c):
                        if c == 0:
                            act.wait_ge(shifted, HEAD + n + 1)
                        nc.scalar.activation(S[:, s, c, :], S[:, s, c, :], ACT.Exp, bias=shift[:, s, :], scale=SCALE,
                                             accum_out=part[:, s, c:c + 1]).then_inc(exped, 1)

                    def keep_hi(n, s, c):
                        act.wait_ge(turned, HEAD + n * C + c + 1)
                        act.wait_ge(weighed, HEAD + n * C + c - 1)
                        nc.scalar.copy(p_hi[:, c % 2], psT[:, c % 2, :].rearrange("p (t q) -> p t q", t=KB)).then_inc(hi_kept, 1)

                    def body(n, s, r, ahead):
                        exponent(n, s, 0)
                        for step in range(C + 3):
                            if step + 1 < C:
                                exponent(n, s, step + 1)
                            if ahead and step < C:
                                keep(n + 1, 1 - s, step)
                            if step >= 3:
                                keep_hi(n, s, step - 3)

                    for c in range(C):
                        keep(0, 0, c)
                    tiles(act, body)

                @block.vector
                def _(dve):
                    def most(n, s, c):
                        dve.wait_ge(kept, HEAD + n * C + c + 1)
                        nc.vector.tensor_reduce(mx[:, s, c:c + 1], S[:, s, c, :], AX_X, ALU.max).then_inc(maxed, 1)

                    def bias(n, s):
                        dve.wait_ge(maxed, HEAD + n * C + C)
                        nc.vector.tensor_reduce(top[:, s, :], mx[:, s, :], AX_X, ALU.max).then_inc(topped, 1)
                        dve.wait_ge(topped, HEAD + n + 1)
                        nc.vector.tensor_scalar(shift[:, s, :], top[:, s, :], -SCALE, None, ALU.mult).then_inc(shifted, 1)

                    def keep_pT(n, s, c):
                        dve.wait_ge(hi_kept, HEAD + n * C + c + 1)
                        nc.vector.tensor_tensor(p_lo[:, c % 2], psT[:, c % 2, :].rearrange("p (t q) -> p t q", t=KB), p_hi[:, c % 2],
                                                ALU.subtract).then_inc(pT_kept, 1)

                    def finish(n, s, r):
                        nc.vector.tensor_reduce(den[:, s, :], part[:, s, :], AX_X, ALU.add).then_inc(summed, 1)
                        dve.wait_ge(summed, HEAD + n + 1)
                        nc.vector.reciprocal(rden[:, s, :], den[:, s, :]).then_inc(inverted, 1)
                        dve.wait_ge(weighed, HEAD + n * C + C)
                        dve.wait_ge(inverted, HEAD + n + 1)
                        dve.wait_ge(t_in[s], r * 16 + 16)
                        nc.vector.scalar_tensor_tensor(out=t[:, s, :], in0=psO[:, s, 0:D], scalar=rden[:, s, :], in1=t[:, s, :],
                                                       op0=ALU.mult, op1=ALU.add).then_inc(added, 1)

                    def body(n, s, r, ahead):
                        for step in range(C + 3):
                            if ahead and step < C:
                                most(n + 1, 1 - s, step)
                                if step == C - 1:
                                    bias(n + 1, 1 - s)
                            if step >= 3:
                                keep_pT(n, s, step - 3)
                        finish(n, s, r)

                    for c in range(C):
                        most(0, 0, c)
                    bias(0, 0)
                    tiles(dve, body)


def gates_phase(nc, t2_d, u, bg, ident_d, xg_d):
    NT = B * T // P
    GW = 3 * D
    with ExitStack() as stack:
        ph = Phase(nc, stack, "ga")
        ident = ph.sb("ident", [P, P])
        w = ph.sb("w", [P, KT, GW])
        bias = ph.sb("bias", [P, GW])
        eps = ph.sb("eps", [P, 1])
        tin = ph.sb("tin", [P, 2, D])
        xl = ph.sb("xl", [P, 2, D])
        xT = ph.sb("xT", [P, 2, KT, P])
        xg = ph.sb("xg", [P, 2, GW])
        stats = ph.sb("stats", [P, 2, 6])
        mv = ph.sb("mv", [P, 2, 2])
        std = ph.sb("std", [P, 2, 1])
        rstd = ph.sb("rstd", [P, 2, 1])
        psT = ph.ps("psT", [P, 2, 512])
        psG = ph.ps("psG", [P, 2, 1024])
        w_in, eps_set, passed = ph.sem("w_in"), ph.sem("eps_set"), ph.sem("passed")
        t_in = [ph.sem(f"t_in{s}") for s in range(2)]
        g_out = [ph.sem(f"g_out{s}") for s in range(2)]
        stated, aggregated, rooted, inverted, normed, turned, xT_kept, made, biased = (
            ph.sem(n) for n in "stated aggregated rooted inverted normed turned xT_kept made biased".split())
        start_at_head(nc, [stated, aggregated, rooted, inverted, normed, turned, xT_kept, made, biased] + g_out)
        loads = [(ident[:, :], ident_d)] + [(w[:, :, j * D:(j + 1) * D], k_rows(u[j])) for j in range(3)] + [
            (bias[:, j * D:(j + 1) * D], bg[j].rearrange("(o n) -> o n", o=1).broadcast_to([P, D])) for j in range(3)]

        def iterations(eng, body):
            for i in range(4):
                body(i, i % 2, i // 2, lambda k, i=i: i - 2 * k >= 0)
            with eng.Fori(2, NT // 2) as r:
                for s in range(2):
                    body(r * 2 + s, s, r, lambda k: True)
            for i in range(NT, NT + 4):
                body(i, i % 2, i // 2, lambda k, i=i: i - 2 * k < NT)

        with nc.Block() as block:
            @block.sync
            def _(sp):
                for dst, src in loads:
                    sp.dma_start(dst, src).then_inc(w_in, 16)

                def body(i, s, r, live):
                    if live(0):
                        sp.wait_ge(normed, HEAD + i - 1)
                        sp.dma_start(tin[:, s, :], t2_d.rearrange("b t d -> (b t) d")[bass.ds(i * P, P), :]).then_inc(t_in[s], 16)
                    if live(2):
                        n = i - 4
                        sp.wait_ge(biased, HEAD + n + 1)
                        sp.dma_start(xg_d.rearrange("b t d -> (b t) d")[bass.ds(n * P, P), :], xg[:, s, :]).then_inc(g_out[s], 16)
                iterations(sp, body)
                for s in range(2):
                    sp.wait_ge(g_out[s], HEAD + 16 * (NT // 2))

            @block.tensor
            def _(pe):
                def body(i, s, r, live):
                    if live(1):
                        n = i - 2
                        pe.wait_ge(normed, HEAD + n + 1)
                        pe.wait_ge(xT_kept, HEAD + n - 1)
                        for k in range(KT):
                            mm = pe.transpose(psT[:, s, k * P:(k + 1) * P], xl[:, s, k * P:(k + 1) * P], ident[:, :])
                        mm.then_inc(turned, 1)
                    if live(2):
                        n = i - 4
                        pe.wait_ge(xT_kept, HEAD + n + 1)
                        pe.wait_ge(biased, HEAD + n - 1)
                        for lo, hi in ((0, 512), (512, GW)):
                            for k in range(KT):
                                mm = pe.matmul(psG[:, s, lo:hi], xT[:, s, k, :], w[:, k, lo:hi], start=(k == 0), stop=(k == KT - 1))
                        mm.then_inc(made, 1)
                pe.wait_ge(w_in, 16 * len(loads))
                iterations(pe, body)

            @block.scalar
            def _(act):
                def body(i, s, r, live):
                    if live(0):
                        act.wait_ge(aggregated, HEAD + i + 1)
                        nc.scalar.activation(std[:, s, :], mv[:, s, 1:2], ACT.Sqrt, bias=eps[:, :]).then_inc(rooted, 1)
                    if live(1):
                        n = i - 2
                        act.wait_ge(turned, HEAD + n + 1)
                        act.wait_ge(made, HEAD + n - 1)
                        nc.scalar.copy(xT[:, s], psT[:, s, 0:D].rearrange("p (k t) -> p k t", k=KT)).then_inc(xT_kept, 1)
                act.wait_ge(eps_set, 1)
                iterations(act, body)

            @block.vector
            def _(dve):
                def body(i, s, r, live):
                    if live(0):
                        dve.wait_ge(t_in[s], r * 16 + 16)
                        nc.vector.bn_stats(stats[:, s, :], tin[:, s]).then_inc(stated, 1)
                        dve.wait_ge(stated, HEAD + i + 1)
                        dve.sem_inc(passed, 1)
                        nc.vector.bn_aggr(mv[:, s, :], stats[:, s, :]).then_inc(aggregated, 1)
                    if live(2):
                        n = i - 4
                        dve.wait_ge(made, HEAD + n + 1)
                        dve.wait_ge(g_out[s], HEAD + (r - 2) * 16)
                        nc.vector.tensor_tensor(xg[:, s, :], psG[:, s, 0:GW], bias[:, :], ALU.add).then_inc(biased, 1)
                    if live(0):
                        dve.wait_ge(rooted, HEAD + i + 1)
                        nc.vector.reciprocal(rstd[:, s, :], std[:, s, :]).then_inc(inverted, 1)
                        dve.wait_ge(inverted, HEAD + i + 1)
                        dve.wait_ge(turned, HEAD + i - 1)
                        nc.vector.tensor_scalar(xl[:, s, :], tin[:, s, :], mv[:, s, 0:1], rstd[:, s, :], ALU.subtract, ALU.mult).then_inc(normed, 1)
                nc.vector.memset(eps[:, :], LN_EPS).then_inc(eps_set, 1)
                dve.wait_ge(w_in, 16 * len(loads))
                iterations(dve, body)


def recurrent_phase(nc, xg_d, v_d, ident_d, t2_d, out):
    L = T // P
    SAME = 2.0 ** -18
    GW = 3 * D
    TURNS = (L + 1, L)
    with ExitStack() as stack:
        ph = Phase(nc, stack, "re")
        ident = ph.sb("ident", [P, P])
        w = ph.sb("w", [P, KT, GW])
        w_hi = ph.sb("w_hi", [P, KT, GW], F32R)
        w_lo = ph.sb("w_lo", [P, KT, GW], F32R)
        h_hi = ph.sb("h_hi", [P, B, KT, P], F32R)
        h_lo = ph.sb("h_lo", [P, B, KT, P], F32R)
        h = ph.sb("h", [P, B, D])
        c = ph.sb("c", [P, B, D])
        hc = ph.sb("hc", [P, B, D])
        ig = ph.sb("ig", [P, B, D])
        tc = ph.sb("tc", [P, B, D])
        z = ph.sb("z", [P, B, GW])
        gate = ph.sb("gate", [P, B, GW])
        xg = ph.sb("xg", [P, B, 2, GW])
        tin = ph.sb("tin", [P, B, 2, D])
        os = ph.sb("os", [P, B, 2, D])
        start = ph.sb("start", [P, 2, B, D])
        moved = ph.sb("moved", [P, 2, B, D])
        gap = ph.sb("gap", [P, 2 * B * D])
        most = ph.sb("most", [P, 1])
        most1 = ph.sb("most1", [1, 1])
        again = ph.sb("again", [1, 1], I32)
        number = ph.sb("number", [1, 1], I32)
        psA = [ph.ps(f"psA{g}", [P, 512]) for g in range(B)]
        psB = [ph.ps(f"psB{g}", [P, 512]) for g in range(B)]
        psT = [ph.ps(f"psT{g}", [P, 512]) for g in range(B)]
        psM = ph.ps("psM", [P, 512])
        sem = ph.sem
        w_in = sem("w_in")
        xg_in = [[sem(f"xg_in{g}{s}") for s in range(2)] for g in range(B)]
        t_in = [[sem(f"t_in{g}{s}") for s in range(2)] for g in range(B)]
        outed = [[sem(f"outed{g}{s}") for s in range(2)] for g in range(B)]
        ends_in = sem("ends_in")
        per_group = ("ig_made o_made turned hi_ready hT_ready ig_added o_added i_ready g_ready o_ready ig_ready c_ready "
                     "tanh_ready h_ready hc_ready os_ready").split()
        q = [{n: sem(f"{n}{g}") for n in per_group} for g in range(B)]
        w_hi_ready, w_lo_ready, zeroed, started, gapped, gap_max, gap_turned, gap_most, judged, decided = (
            sem(n) for n in "w_hi_ready w_lo_ready zeroed started gapped gap_max gap_turned gap_most judged decided".split())
        seen = {e: sem(f"seen_{e}") for e in ("sp", "pe", "act", "dve", "pool")}
        start_at_head(nc, [d["os_ready"] for d in q], HEAD + L)
        start_at_head(nc, [v for l in t_in + outed for v in l], HEAD + L // 2 * 16)
        start_at_head(nc, [v for d in q for n, v in d.items() if n != "os_ready"] + [v for l in xg_in for v in l]
                      + [ends_in, zeroed, started, gapped, gap_max, gap_turned, gap_most, judged, decided])

        rows = lambda a: a.rearrange("b (n s) d -> b n s d", s=L)
        x_rows, t_rows, out_rows = rows(xg_d), rows(t2_d), rows(out.rearrange("b x y d -> b (x y) d"))

        def at(v, step):
            return v[:, bass.ds(step, 1), :].rearrange("n o d -> n (o d)")

        def runs(eng, name, run):
            run(0, False)
            eng.wait_ge(decided, HEAD + 1)
            with eng.While(lambda: eng.value_load(again[0:1, 0:1], min_val=0, max_val=1) > 0):
                k = eng.value_load(number[0:1, 0:1], min_val=1, max_val=P + 1)
                run(k, True)
                if name != "dve":
                    eng.wait_ge(decided, k + 1 + HEAD)
                    eng.sem_inc(seen[name], 1)

        def steps(eng, body, first=0):
            with eng.Fori(first, L // 2) as r:
                for s in range(2):
                    body(r * 2 + s, s, r)

        with nc.Block() as block:
            @block.sync
            def _(sp):
                def load(k, g, n, s, full):
                    sp.wait_ge(q[g]["o_added"], k * L + n - 1 + HEAD)
                    sp.dma_start(xg[:, g, s, :], at(x_rows[g], n)).then_inc(xg_in[g][s], 16)
                    if full:
                        sp.wait_ge(q[g]["os_ready"], k * L + n - 1 + HEAD)
                        sp.dma_start(tin[:, g, s, :], at(t_rows[g], n)).then_inc(t_in[g][s], 16)

                def save(k, g, n, s):
                    sp.wait_ge(q[g]["os_ready"], k * L + n + 1 + HEAD)
                    sp.dma_start(at(out_rows[g], n), os[:, g, s, :]).then_inc(outed[g][s], 16)

                def run(k, full):
                    for s in range(2):
                        for g in range(B):
                            load(k, g, s, s, full)
                    with sp.Fori(0, L // 2 - 1) as r:
                        for s in range(2):
                            for g in range(B):
                                if full:
                                    save(k, g, r * 2 + s, s)
                                load(k, g, r * 2 + s + 2, s, full)
                    if full:
                        for s in range(2):
                            for g in range(B):
                                save(k, g, L - 2 + s, s)
                    for g in range(B):
                        sp.wait_ge(q[g]["h_ready"], k * (L + 1) + L + 1 + HEAD)
                        for j, buf in enumerate((h, c)):
                            sp.dma_start(moved[1:P, j, g, :], buf[0:P - 1, g, :]).then_inc(ends_in, 16)
                    if full:
                        for g in range(B):
                            for s in range(2):
                                sp.wait_ge(outed[g][s], (k + 1) * (L // 2) * 16 + HEAD)
                                sp.sem_inc(seen["sp"], 1)

                sp.dma_start(ident[:, :], ident_d).then_inc(w_in, 16)
                for j in range(3):
                    sp.dma_start(w[:, :, j * D:(j + 1) * D], k_rows(v_d[j])).then_inc(w_in, 16)
                sp.wait_ge(zeroed, HEAD + 2)
                runs(sp, "sp", run)

            @block.tensor
            def _(pe):
                def turn(g):
                    for j in range(KT):
                        mm = pe.transpose(psT[g][:, j * P:(j + 1) * P], h[:, g, j * P:(j + 1) * P], ident[:, :])
                    mm.then_inc(q[g]["turned"], 1)

                def product(g, dst, lo, hi, done):
                    terms = [(a, b, j) for j in range(KT) for a, b in ((h_hi, w_hi), (h_hi, w_lo), (h_lo, w_hi))]
                    for i, (a, b, j) in enumerate(terms):
                        mm = pe.matmul(dst[:, 0:hi - lo], a[:, g, j, :], b[:, j, lo:hi], start=(i == 0), stop=(i == len(terms) - 1))
                    mm.then_inc(q[g][done], 1)

                def run(k, full):
                    def step(n, s, r):
                        for g in range(B):
                            o = 1 - g
                            pe.wait_ge(q[g]["hT_ready"], k * TURNS[g] + n + 1 + HEAD)
                            product(g, psA[g], 0, 512, "ig_made")
                            pe.wait_ge(q[o]["h_ready"], k * (L + 1) + n + (1, 2)[g] + HEAD)
                            turn(o)
                            product(g, psB[g], 512, GW, "o_made")

                    pe.wait_ge(q[0]["h_ready"], k * (L + 1) + 1 + HEAD)
                    turn(0)
                    steps(pe, step)
                    if full:
                        pe.wait_ge(gap_max, HEAD + k)
                        pe.transpose(psM[0:1, 0:P], most[:, :], ident[:, :]).then_inc(gap_turned, 1)

                pe.wait_ge(w_in, 64)
                pe.wait_ge(w_lo_ready, 1)
                runs(pe, "pe", run)

            @block.scalar
            def _(act):
                def run(k, full):
                    def tanh_c(g, n):
                        act.wait_ge(q[g]["c_ready"], k * (L + 1) + n + 2 + HEAD)
                        nc.scalar.activation(tc[:, g], c[:, g], ACT.Tanh).then_inc(q[g]["tanh_ready"], 1)

                    def keep_hi(g, n):
                        act.wait_ge(q[g]["turned"], k * TURNS[g] + n + 1 + HEAD)
                        nc.scalar.copy(h_hi[:, g], psT[g][:, 0:D].rearrange("p (k t) -> p k t", k=KT)).then_inc(q[g]["hi_ready"], 1)

                    def step(n, s, r, first=False):
                        for g in range(B):
                            o = 1 - g
                            if not (first and g == 0):
                                tanh_c(o, n - 1 + g)
                            keep_hi(o, n + g)
                            act.wait_ge(q[g]["ig_added"], k * L + n + 1 + HEAD)
                            nc.scalar.activation(gate[:, g, 0:D], z[:, g, 0:D], ACT.Sigmoid).then_inc(q[g]["i_ready"], 1)
                            nc.scalar.activation(gate[:, g, D:2 * D], z[:, g, D:2 * D], ACT.Tanh).then_inc(q[g]["g_ready"], 1)
                            act.wait_ge(q[g]["o_added"], k * L + n + 1 + HEAD)
                            nc.scalar.activation(gate[:, g, 2 * D:GW], z[:, g, 2 * D:GW], ACT.Sigmoid).then_inc(q[g]["o_ready"], 1)

                    keep_hi(0, 0)
                    step(0, 0, 0, first=True)
                    step(1, 1, 0)
                    steps(act, step, 1)
                    tanh_c(1, L - 1)

                runs(act, "act", run)

            @block.vector
            def _(dve):
                def run(k, full):
                    def cell(g, n):
                        dve.wait_ge(q[g]["hc_ready"], k * (L + 1) + n + 1 + HEAD)
                        dve.wait_ge(q[g]["ig_ready"], k * L + n + 1 + HEAD)
                        nc.vector.tensor_tensor(c[:, g], ig[:, g], hc[:, g], ALU.add).then_inc(q[g]["c_ready"], 1)
                        if full:
                            dve.wait_ge(q[g]["os_ready"], k * L + n + HEAD)
                        dve.wait_ge(q[g]["tanh_ready"], k * L + n + 1 + HEAD)
                        nc.vector.tensor_tensor(h[:, g], gate[:, g, 2 * D:GW], tc[:, g], ALU.mult).then_inc(q[g]["h_ready"], 1)

                    def keep_lo(g, n):
                        dve.wait_ge(q[g]["hi_ready"], k * TURNS[g] + n + 1 + HEAD)
                        nc.vector.tensor_tensor(h_lo[:, g], psT[g][:, 0:D].rearrange("p (k t) -> p k t", k=KT), h_hi[:, g],
                                                ALU.subtract).then_inc(q[g]["hT_ready"], 1)

                    def step(n, s, r, first=False):
                        for g in range(B):
                            o = 1 - g
                            if not (first and g == 0):
                                cell(o, n - 1 + g)
                            dve.wait_ge(xg_in[g][s], (k * (L // 2) + r + 1) * 16 + HEAD)
                            dve.wait_ge(q[g]["ig_made"], k * L + n + 1 + HEAD)
                            nc.vector.tensor_tensor(z[:, g, 0:512], psA[g][:, :], xg[:, g, s, 0:512], ALU.add).then_inc(q[g]["ig_added"], 1)
                            keep_lo(o, n + g)
                            dve.wait_ge(q[g]["o_made"], k * L + n + 1 + HEAD)
                            nc.vector.tensor_tensor(z[:, g, 512:GW], psB[g][:, 0:GW - 512], xg[:, g, s, 512:GW], ALU.add).then_inc(q[g]["o_added"], 1)
                            dve.wait_ge(q[g]["g_ready"], k * L + n + 1 + HEAD)
                            nc.vector.tensor_tensor(ig[:, g], gate[:, g, 0:D], gate[:, g, D:2 * D], ALU.mult).then_inc(q[g]["ig_ready"], 1)

                    for g in range(B):
                        dve.wait_ge(q[g]["hc_ready"], k * (L + 1) + HEAD)
                        dve.wait_ge(q[g]["os_ready"], k * L + HEAD)
                        nc.vector.tensor_copy(c[:, g], start[:, 1, g]).then_inc(q[g]["c_ready"], 1)
                        nc.vector.tensor_copy(h[:, g], start[:, 0, g]).then_inc(q[g]["h_ready"], 1)
                    keep_lo(0, 0)
                    step(0, 0, 0, first=True)
                    step(1, 1, 0)
                    steps(dve, step, 1)
                    cell(1, L - 1)

                    dve.wait_ge(ends_in, k * 64 + 64 + HEAD)
                    if full:
                        flat = "p j g d -> p (j g d)"
                        nc.vector.tensor_tensor(gap[:, :], moved[:, :, :, :].rearrange(flat), start[:, :, :, :].rearrange(flat),
                                                ALU.subtract).then_inc(gapped, 1)
                        dve.wait_ge(gapped, HEAD + k)
                        nc.vector.tensor_reduce(most[:, :], gap[:, :], AX_X, ALU.max, apply_absolute_value=True).then_inc(gap_max, 1)
                        dve.wait_ge(gap_max, HEAD + k)
                    nc.vector.tensor_copy(start[:, :, :, :], moved[:, :, :, :]).then_inc(started, 1)
                    if full:
                        dve.wait_ge(gap_turned, HEAD + k)
                        nc.vector.tensor_reduce(most1[:, :], psM[0:1, 0:P], AX_X, ALU.max).then_inc(gap_most, 1)
                        dve.wait_ge(gap_most, HEAD + k)
                        nc.vector.tensor_scalar(again[:, :], most1[:, :], SAME, None, ALU.is_gt)
                    else:
                        nc.vector.memset(again[:, :], 1)
                    dve.wait_ge(started, k + 2 + HEAD)
                    nc.vector.tensor_scalar(number[:, :], number[:, :], 1, None, ALU.add).then_inc(judged, 1)
                    dve.wait_ge(judged, k + 1 + HEAD)
                    dve.sem_inc(decided, 1)

                nc.vector.memset(start[:, :, :, :], 0.0).then_inc(started, 1)
                nc.vector.memset(number[:, :], 0).then_inc(zeroed, 1)
                nc.vector.memset(moved[:, :, :, :], 0.0).then_inc(zeroed, 1)
                dve.wait_ge(w_in, 64)
                nc.vector.tensor_copy(w_hi[:, :, :], w[:, :, :]).then_inc(w_hi_ready, 1)
                dve.wait_ge(w_hi_ready, 1)
                nc.vector.tensor_tensor(w_lo[:, :, :], w[:, :, :], w_hi[:, :, :], ALU.subtract).then_inc(w_lo_ready, 1)
                runs(dve, "dve", run)

            @block.gpsimd
            def _(pool):
                def run(k, full):
                    def product(g, n):
                        pool.wait_ge(q[g]["h_ready"], k * (L + 1) + n + 1 + HEAD)
                        nc.gpsimd.tensor_tensor(hc[:, g], h[:, g], c[:, g], ALU.mult).then_inc(q[g]["hc_ready"], 1)

                    def step(n, s, r):
                        for g in range(B):
                            product(g, n + 1)
                            if full:
                                pool.wait_ge(t_in[g][s], (k * (L // 2) + r + 1) * 16 + HEAD)
                                pool.wait_ge(outed[g][s], (k * (L // 2) + r) * 16 + HEAD)
                                nc.gpsimd.tensor_tensor(os[:, g, s], h[:, g], tin[:, g, s], ALU.add).then_inc(q[g]["os_ready"], 1)

                    for g in range(B):
                        product(g, 0)
                    steps(pool, step)

                runs(pool, "pool", run)


def constants():
    ident = np.eye(P, dtype=np.float32)
    sel = np.zeros((P, 4, 32), np.float32)
    mask = np.zeros((P, H), np.float32)
    for j in range(4):
        for xx in range(2):
            for h in range(H):
                p = 32 * j + 8 * xx + h
                mask[p, h] = 1.0
                for q in range(4):
                    sel[p, q, 8 * q + 2 * j + xx] = 1.0
    return {"ident": ident, "sel": sel, "mask": mask}


_L0 = ["W_lk", "W_rk", "W_lv", "W_rv", "W_out", "ln_agg_g", "ln_agg_b", "W1", "b1", "W2", "b2", "ln2_g", "ln2_b"]
_L1 = ["bq", "bk", "bv"]
_GATES = ["i", "c", "o"]


def build(nc, aps, out, kind):
    att = nc.dram_tensor("att", (B, N, N, H * N), F32, kind=kind).ap()
    o_d = nc.dram_tensor("o", (B, N // 2, 2 * N, D), F32, kind=kind).ap()
    t_d = nc.dram_tensor("t", (B, T, D), F32, kind=kind).ap()
    xlT_d = nc.dram_tensor("xlT", (KT, P, B * T), F32, kind=kind).ap()
    t2_d = nc.dram_tensor("t2", (B, T, D), F32, kind=kind).ap()
    xg_d = nc.dram_tensor("xg", (B, T, 3 * D), F32, kind=kind).ap()
    x, ident = aps["x"], aps["ident"]
    w = {n: aps["L0_conv_" + n] for n in _L0}
    for b in range(B):
        scores_phase(nc, b, x, w["W_lk"], w["W_rk"], ident, att)
    for b in range(B):
        mix_phase(nc, b, x, w["W_lv"], w["W_rv"], ident, aps["sel"], aps["mask"], att, o_d)
    dense_phase(nc, x, o_d, w["W_out"], w["ln_agg_g"], w["ln_agg_b"], w["W1"], w["b1"], w["W2"], w["b2"], w["ln2_g"], w["ln2_b"], ident, t_d, xlT_d)
    for b in range(B):
        attention_phase(nc, b, t_d, xlT_d, aps["WqT"], aps["L1_attn_bq"], aps["WkT"], aps["L1_attn_bk"], aps["WvT"], aps["L1_attn_bv"], ident, t2_d)
    gates_phase(nc, t2_d, [aps["L1_ffn_U_" + g] for g in _GATES], [aps["L1_ffn_b_" + g] for g in _GATES], ident, xg_d)
    recurrent_phase(nc, xg_d, [aps["L1_ffn_V_" + g] for g in _GATES], ident, t2_d, out)


def kernel(**inputs):
    import numpy as _np
    import concourse.bacc as _bacc
    from concourse import mybir as _mybir
    from concourse.bass_utils import run_bass_kernel_spmd as _run

    given = {n: _np.ascontiguousarray(inputs[n]) for n in ["x"] + ["L0_conv_" + n for n in _L0] + ["L1_attn_" + n for n in _L1]
             + ["L1_ffn_" + m + "_" + g for m in ("U", "V", "b") for g in _GATES]}
    for n in ("q", "k", "v"):
        given[f"W{n}T"] = _np.ascontiguousarray(inputs[f"L1_attn_W{n}"].T)
    given.update(constants())
    nc = _bacc.Bacc("TRN2", target_bir_lowering=False, num_devices=1)
    arrays, aps = {}, {}
    for name, a in given.items():
        arrays[f"in_{name}"] = a
        aps[name] = nc.dram_tensor(f"in_{name}", a.shape, _mybir.dt.from_np(a.dtype), kind="ExternalInput").ap()
    out = nc.dram_tensor("out_0", (B, N, N, D), _mybir.dt.float32, kind="ExternalOutput").ap()
    build(nc, aps, out, "Internal")
    r = _run(nc, [arrays], core_ids=[0])
    return r.results[0]["out_0"]
```

```python
from contextlib import ExitStack

import numpy as np

import concourse.bass as bass
from concourse import mybir

F32 = mybir.dt.float32
I32 = mybir.dt.int32
F32R = mybir.dt.float32r
ALU = mybir.AluOpType
ACT = mybir.ActivationFunctionType
AX_X = mybir.AxisListType.X

P = 128
B, N, D = 2, 64, 256
H = 8
DK = D // H
G = 2
HG = H // G
T = N * N
KT = D // P
LN_EPS = 1e-5


class Phase:

    def __init__(self, nc, stack, name):
        self.nc, self.stack, self.name, self.sems = nc, stack, name, []
        stack.callback(self.clear)

    def clear(self):
        with self.nc.Block() as block:
            @block.sync
            def _(sp):
                for sem in self.sems:
                    sp.sem_clear(sem)

    def sb(self, name, shape, dtype=F32):
        return self.stack.enter_context(self.nc.sbuf_tensor(f"{self.name}_{name}", shape, dtype))

    def ps(self, name, shape):
        return self.stack.enter_context(self.nc.psum_tensor(f"{self.name}_{name}", shape, F32))

    def sem(self, name):
        self.sems.append(self.stack.enter_context(self.nc.semaphore(f"{self.name}_{name}")))
        return self.sems[-1]


HEAD = 32


def start_at_head(nc, sems, head=HEAD):
    with nc.Block() as block:
        @block.sync
        def _(sp):
            for sem in sems:
                sp.sem_inc(sem, head)


def k_rows(w):
    return w.rearrange("(k p) n -> p k n", p=P)


def scores_phase(nc, b, x, w_lk, w_rk, ident_d, att):
    with ExitStack() as stack:
        ph = Phase(nc, stack, f"sc{b}")
        ident = ph.sb("ident", [P, P])
        wlk = ph.sb("wlk", [P, KT, D])
        wrk = ph.sb("wrk", [P, KT, D])
        lkT = ph.sb("lkT", [P, G, T])
        rkT = ph.sb("rkT", [P, G, T])
        BLK = 512
        NBLK = T // BLK

        with ExitStack() as inner:
            pj = Phase(nc, inner, f"pj{b}")
            xin = pj.sb("xin", [P, 2, BLK // P, D])
            xT = pj.sb("xT", [P, 2, KT, BLK])
            psT = pj.ps("psT", [P, KT, BLK])
            psP = pj.ps("psP", [P, 2 * G, BLK])
            w_in = pj.sem("w_in")
            x_in = [pj.sem(f"x_in{s}") for s in range(2)]
            turned = pj.sem("turned")
            xT_done = pj.sem("xT_done")
            projected = pj.sem("projected")
            stored = pj.sem("stored")
            start_at_head(nc, [turned, xT_done, projected, stored])
            with nc.Block() as block:
                @block.sync
                def _(sp):
                    sp.dma_start(ident[:, :], ident_d).then_inc(w_in, 16)
                    sp.dma_start(wlk[:, :, :], k_rows(w_lk)).then_inc(w_in, 16)
                    sp.dma_start(wrk[:, :, :], k_rows(w_rk)).then_inc(w_in, 16)
                    xb = x[b].rearrange("x a d -> (x a) d")
                    with sp.Fori(0, NBLK // 2) as i:
                        for s in range(2):
                            n = i * 2 + s
                            sp.wait_ge(turned, HEAD + n - 1)
                            sp.dma_start(xin[:, s], xb[bass.ds(n * BLK, BLK), :].rearrange("(t p) d -> p t d", p=P)).then_inc(x_in[s], 16)

                @block.tensor
                def _(pe):
                    pe.wait_ge(w_in, 48)
                    with pe.Fori(0, NBLK // 2) as i:
                        for s in range(2):
                            n = i * 2 + s
                            pe.wait_ge(x_in[s], i * 16 + 16)
                            pe.wait_ge(xT_done, HEAD + n)
                            for k in range(KT):
                                for t in range(BLK // P):
                                    mm = pe.transpose(psT[:, k, t * P:(t + 1) * P], xin[:, s, t, k * P:(k + 1) * P], ident[:, :])
                            mm.then_inc(turned, 1)
                            pe.wait_ge(xT_done, HEAD + n + 1)
                            for j in range(2 * G):
                                w, g = (wlk, wrk)[j // G], j % G
                                pe.wait_ge(stored, HEAD + (n - 1) * (2 * G) + j + 1)
                                for k in range(KT):
                                    mm = pe.matmul(psP[:, j, :], w[:, k, g * P:(g + 1) * P], xT[:, s, k, :], start=(k == 0), stop=(k == KT - 1))
                                mm.then_inc(projected, 1)

                @block.scalar
                def _(act):
                    with act.Fori(0, NBLK // 2) as i:
                        for s in range(2):
                            n = i * 2 + s
                            act.wait_ge(turned, HEAD + n + 1)
                            act.wait_ge(projected, HEAD + (n - 1) * (2 * G))
                            nc.scalar.copy(xT[:, s], psT[:, :, :]).then_inc(xT_done, 1)

                @block.vector
                def _(dve):
                    with dve.Fori(0, NBLK // 2) as i:
                        for s in range(2):
                            n = i * 2 + s
                            for j in range(2 * G):
                                dst = (lkT, rkT)[j // G]
                                dve.wait_ge(projected, HEAD + n * (2 * G) + j + 1)
                                nc.vector.tensor_copy(dst[:, j % G, bass.ds(n * BLK, BLK)], psP[:, j, :]).then_inc(stored, 1)

        with ExitStack() as inner:
            sm = Phase(nc, inner, f"sm{b}")
            AB = 8
            NA = N // AB
            F = HG * N
            E = sm.sb("E", [P, N, F])
            lks = sm.sb("lks", [P, 2, G, AB, N])
            rks = sm.sb("rks", [P, 2, G, AB, N])
            part = sm.sb("part", [P, NA, F])
            top = sm.sb("top", [P, F])
            den = sm.sb("den", [P, F])
            rden = sm.sb("rden", [P, F])
            psS = sm.ps("psS", [P, 2, HG, AB * N])
            lk_cut = sm.sem("lk_cut")
            rk_cut = sm.sem("rk_cut")
            scored = sm.sem("scored")
            kept = sm.sem("kept")
            maxed = sm.sem("maxed")
            topped = sm.sem("topped")
            shifted = sm.sem("shifted")
            exped = sm.sem("exped")
            summed = sm.sem("summed")
            inverted = sm.sem("inverted")
            normed = sm.sem("normed")
            saved = sm.sem("saved")
            CH = 4
            CA = N // CH
            start_at_head(nc, [lk_cut, rk_cut, scored, kept, maxed])
            lk_v = lkT[:, :, :].rearrange("p g (x a) -> p g a x", a=N)
            rk_v = rkT[:, :, :].rearrange("p g (a y) -> p g a y", y=N)
            with nc.Block() as block:
                @block.gpsimd
                def _(pool):
                    with pool.Fori(0, NA // 2) as i:
                        for s in range(2):
                            n = i * 2 + s
                            pool.wait_ge(scored, HEAD + n - 1)
                            for g in range(G):
                                nc.gpsimd.tensor_copy(lks[:, s, g], lk_v[:, g, bass.ds(n * AB, AB), :]).then_inc(lk_cut, 1)

                @block.tensor
                def _(pe):
                    with pe.Fori(0, NA // 2) as i:
                        for s in range(2):
                            n = i * 2 + s
                            pe.wait_ge(lk_cut, HEAD + n * 2 + 2)
                            pe.wait_ge(rk_cut, HEAD + n * 2 + 2)
                            pe.wait_ge(kept, HEAD + n - 1)
                            for a in range(AB):
                                for g in range(G):
                                    for h in range(HG):
                                        r = slice(h * DK, (h + 1) * DK)
                                        mm = pe.matmul(psS[g * N:(g + 1) * N, s, h, a * N:(a + 1) * N], lks[r, s, g, a, :], rks[r, s, g, a, :],
                                                       start=True, stop=True, tile_position=(h * DK, g * N))
                            mm.then_inc(scored, 1)

                @block.scalar
                def _(act):
                    with act.Fori(0, NA // 2) as i:
                        for s in range(2):
                            n = i * 2 + s
                            act.wait_ge(scored, HEAD + n + 1)
                            nc.scalar.copy(E[:, bass.ds(n * AB, AB), :].rearrange("p a (h y) -> p h a y", h=HG),
                                           psS[:, s].rearrange("p h (a y) -> p h a y", a=AB)).then_inc(kept, 1)
                    for c in range(CH):
                        act.wait_ge(shifted, c + 1)
                        nc.scalar.activation(E[:, c * CA:(c + 1) * CA, :], E[:, c * CA:(c + 1) * CA, :], ACT.Exp,
                                             scale=float(DK) ** -0.5).then_inc(exped, 1)

                @block.vector
                def _(dve):
                    def cut(n, s):
                        dve.wait_ge(scored, HEAD + n - 1)
                        for g in range(G):
                            nc.vector.tensor_copy(rks[:, s, g], rk_v[:, g, bass.ds(n * AB, AB), :]).then_inc(rk_cut, 1)

                    def step_max(n):
                        dve.wait_ge(kept, HEAD + n + 1)
                        nc.vector.tensor_reduce(part[:, bass.ds(n, 1), :], E[:, bass.ds(n * AB, AB), :].rearrange("p a f -> p f a"),
                                                AX_X, ALU.max).then_inc(maxed, 1)

                    cut(0, 0)
                    with dve.Fori(0, NA // 2 - 1) as i:
                        cut(i * 2 + 1, 1)
                        step_max(i * 2)
                        cut(i * 2 + 2, 0)
                        step_max(i * 2 + 1)
                    cut(NA - 1, 1)
                    step_max(NA - 2)
                    step_max(NA - 1)
                    dve.wait_ge(maxed, HEAD + NA)
                    nc.vector.tensor_reduce(top[:, :], part[:, :, :].rearrange("p n f -> p f n"), AX_X, ALU.max).then_inc(topped, 1)
                    dve.wait_ge(topped, 1)
                    for c in range(CH):
                        nc.vector.tensor_tensor(E[:, c * CA:(c + 1) * CA, :], E[:, c * CA:(c + 1) * CA, :],
                                                top[:, :].unsqueeze(1).broadcast_to([P, CA, F]), ALU.subtract).then_inc(shifted, 1)
                    dve.wait_ge(exped, CH)
                    nc.vector.tensor_reduce(den[:, :], E[:, :, :].rearrange("p a f -> p f a"), AX_X, ALU.add).then_inc(summed, 1)
                    dve.wait_ge(summed, 1)
                    nc.vector.reciprocal(rden[:, :], den[:, :]).then_inc(inverted, 1)
                    dve.wait_ge(inverted, 1)
                    for c in range(CH):
                        nc.vector.tensor_tensor(E[:, c * CA:(c + 1) * CA, :], E[:, c * CA:(c + 1) * CA, :],
                                                rden[:, :].unsqueeze(1).broadcast_to([P, CA, F]), ALU.mult).then_inc(normed, 1)

                @block.sync
                def _(sp):
                    for c in range(CH):
                        sp.wait_ge(normed, c + 1)
                        for g in range(G):
                            sp.dma_start(att[b, :, c * CA:(c + 1) * CA, g * F:(g + 1) * F], E[g * N:(g + 1) * N, c * CA:(c + 1) * CA, :]).then_inc(saved, 16)
                    sp.wait_ge(saved, 16 * CH * G)


def mix_phase(nc, b, x, w_lv, w_rv, ident_d, sel_d, mask_d, att, o_d):
    with ExitStack() as stack:
        ph = Phase(nc, stack, f"mx{b}")
        ident = ph.sb("ident", [P, P])
        wlv = ph.sb("wlv", [P, KT, D])
        wrv = ph.sb("wrv", [P, KT, D])
        rv = ph.sb("rv", [P, N, D])
        xin = ph.sb("xin", [P, 2, D])
        xT = ph.sb("xT", [P, 2, KT, P])
        NXP = N // 2

        with ExitStack() as inner:
            rp = Phase(nc, inner, f"rp{b}")
            psT = rp.ps("psT", [P, 2, 512])
            psR = rp.ps("psR", [P, 2, 512])
            w_in = rp.sem("w_in")
            x_in = [rp.sem(f"x_in{s}") for s in range(2)]
            turned = rp.sem("turned")
            xT_done = rp.sem("xT_done")
            made = rp.sem("made")
            stored = rp.sem("stored")
            start_at_head(nc, [turned, xT_done, made, stored])
            with nc.Block() as block:
                @block.sync
                def _(sp):
                    sp.dma_start(ident[:, :], ident_d).then_inc(w_in, 16)
                    sp.dma_start(wrv[:, :, :], k_rows(w_rv)).then_inc(w_in, 16)
                    sp.dma_start(wlv[:, :, :], k_rows(w_lv)).then_inc(w_in, 16)
                    with sp.Fori(0, N // 2) as i:
                        for s in range(2):
                            n = i * 2 + s
                            sp.wait_ge(turned, HEAD + n - 1)
                            for c in range(2):
                                sp.dma_start(xin[c * N:(c + 1) * N, s, :], x[b, :, bass.ds(n, 1), :]).then_inc(x_in[s], 16)

                @block.tensor
                def _(pe):
                    def turn(n, s, i):
                        pe.wait_ge(x_in[s], i * 32 + 32)
                        pe.wait_ge(xT_done, HEAD + n - 1)
                        for k in range(KT):
                            mm = pe.transpose(psT[:, s, k * P:(k + 1) * P], xin[:, s, k * P:(k + 1) * P], ident[:, :])
                        mm.then_inc(turned, 1)

                    def make(n, s):
                        pe.wait_ge(xT_done, HEAD + n + 1)
                        pe.wait_ge(stored, HEAD + n - 1)
                        for k in range(KT):
                            mm = pe.matmul(psR[:, s, 0:D], xT[:, s, k, :], wrv[:, k, :], start=(k == 0), stop=(k == KT - 1))
                        mm.then_inc(made, 1)

                    pe.wait_ge(w_in, 48)
                    turn(0, 0, 0)
                    with pe.Fori(0, N // 2 - 1) as i:
                        turn(i * 2 + 1, 1, i)
                        make(i * 2, 0)
                        turn(i * 2 + 2, 0, i + 1)
                        make(i * 2 + 1, 1)
                    turn(N - 1, 1, N // 2 - 1)
                    make(N - 2, 0)
                    make(N - 1, 1)

                @block.scalar
                def _(act):
                    with act.Fori(0, N // 2) as i:
                        for s in range(2):
                            n = i * 2 + s
                            act.wait_ge(turned, HEAD + n + 1)
                            act.wait_ge(made, HEAD + n - 1)
                            nc.scalar.copy(xT[:, s], psT[:, s, 0:D].rearrange("p (k t) -> p k t", k=KT)).then_inc(xT_done, 1)

                @block.vector
                def _(dve):
                    with dve.Fori(0, N // 2) as i:
                        for s in range(2):
                            n = i * 2 + s
                            dve.wait_ge(made, HEAD + n + 1)
                            nc.vector.tensor_copy(rv[:, bass.ds(n, 1), :], psR[:, s, 0:D]).then_inc(stored, 1)

        with ExitStack() as inner:
            mp = Phase(nc, inner, f"mp{b}")
            YB = 8
            NYB = N // YB
            POOL_BLOCKS = ((1, 4, 6), (1, 5))
            sel = mp.sb("sel", [P, 4, 32])
            mask = mp.sb("mask", [P, H])
            pair = mp.sb("pair", [P, 2, 2, H, N])
            lvs = mp.sb("lvs", [P, 2, D])
            Z = mp.sb("Z", [P, NYB, YB, D])
            cut = mp.sb("cut", [P, 2, 4, D])
            oS = mp.sb("oS", [P, 2, D])
            psT = mp.ps("psT", [P, 512])
            psL = mp.ps("psL", [P, 2, 512])
            psO = mp.ps("psO", [P, 2, 4, D])
            psN = mp.ps("psN", [P, 512])
            c_in = mp.sem("c_in")
            x_in = [mp.sem(f"x_in{s}") for s in range(2)]
            a_in = [mp.sem(f"a_in{s}") for s in range(2)]
            zeroed = mp.sem("zeroed")
            psO_clear = mp.sem("psO_clear")
            turned = mp.sem("turned")
            xT_done = mp.sem("xT_done")
            lv_made = mp.sem("lv_made")
            lv_kept = mp.sem("lv_kept")
            z_dve = mp.sem("z_dve")
            z_pool = mp.sem("z_pool")
            z_used = mp.sem("z_used")
            cut_done = mp.sem("cut_done")
            gathered = mp.sem("gathered")
            o_kept = mp.sem("o_kept")
            o_out = [mp.sem(f"o_out{s}") for s in range(2)]
            start_at_head(nc, [turned, xT_done, lv_made, lv_kept, z_dve, z_pool, z_used, cut_done, gathered, o_kept])
            DVE_BLOCKS = [[k for k in range(NYB) if k not in own] for own in POOL_BLOCKS]

            def before(blocks, r, s):
                return r * (len(blocks[0]) + len(blocks[1])) + s * len(blocks[0])

            NQ = NYB // 2
            with nc.Block() as block:
                @block.sync
                def _(sp):
                    sp.dma_start(sel[:, :, :], sel_d).then_inc(c_in, 16)
                    sp.dma_start(mask[:, :], mask_d).then_inc(c_in, 16)
                    sp.wait_ge(zeroed, 2)

                    def load(n, s):
                        sp.wait_ge(turned, HEAD + n - 1)
                        sp.dma_start(xin[:, s, :], x[b, bass.ds(n * 2, 2)].rearrange("x a d -> (x a) d")).then_inc(x_in[s], 16)
                        sp.wait_ge(z_used, HEAD + (n - 1) * NYB)
                        for c in range(2):
                            sp.dma_start(pair[c * N:(c + 1) * N, s, c], att[b, bass.ds(n * 2 + c, 1)].rearrange("o a (h y) -> (o a) h y", y=N)).then_inc(a_in[s], 16)

                    load(0, 0)
                    load(1, 1)
                    with sp.Fori(1, NXP // 2) as i:
                        for s in range(2):
                            load(i * 2 + s, s)
                    for s in range(2):
                        sp.wait_ge(o_out[s], 16 * (NXP // 2))

                @block.tensor
                def _(pe):
                    def turn(n, s, r):
                        pe.wait_ge(x_in[s], r * 16 + 16)
                        pe.wait_ge(xT_done, HEAD + n)
                        for k in range(KT):
                            mm = pe.transpose(psT[:, k * P:(k + 1) * P], xin[:, s, k * P:(k + 1) * P], ident[:, :])
                        mm.then_inc(turned, 1)

                    def lv(n, s, read):
                        pe.wait_ge(xT_done, HEAD + n + 1)
                        pe.wait_ge(z_dve, HEAD + read)
                        for k in range(KT):
                            mm = pe.matmul(psL[:, s, 0:D], xT[:, s, k, :], wlv[:, k, :], start=(k == 0), stop=(k == KT - 1))
                        mm.then_inc(lv_made, 1)

                    def mix(n, s, r, c):
                        pe.wait_ge(cut_done, HEAD + n * NQ + c - 1)
                        for k in (2 * c, 2 * c + 1):
                            if k in POOL_BLOCKS[s]:
                                pe.wait_ge(z_pool, before(POOL_BLOCKS, r, s) + POOL_BLOCKS[s].index(k) + 1 + HEAD)
                            else:
                                pe.wait_ge(z_dve, before(DVE_BLOCKS, r, s) + DVE_BLOCKS[s].index(k) + 1 + HEAD)
                            for y in range(YB):
                                j, q = y % 4, 2 * (k % 2) + y // 4
                                mm = pe.matmul(psO[32 * j:32 * j + 2 * H, c % 2, q, :], pair[:, s, :, :, k * YB + y], Z[:, k, y, :],
                                               start=True, stop=True, tile_position=(0, 32 * j))
                            mm.then_inc(z_used, 1)

                    def gather(n, c):
                        pe.wait_ge(cut_done, HEAD + n * NQ + c + 1)
                        if c == 0:
                            pe.wait_ge(o_kept, HEAD + n)
                        for q in range(4):
                            mm = pe.matmul(psN[32 * c:32 * c + 32, 0:D], sel[:, q, :], cut[:, c % 2, q, :], start=(q == 0), stop=(q == 3),
                                           tile_position=(0, 32 * c))
                        mm.then_inc(gathered, 1)

                    def step(n, s, r, first=False, last=False):
                        for c in range(NQ):
                            if c == 0:
                                pe.wait_ge(a_in[s], r * 32 + 32)
                            mix(n, s, r, c)
                            if c > 1:
                                gather(n, c - 2)
                            elif not first:
                                gather(n - 1, NQ - 2 + c)
                            if c == 0 and not last:
                                turn(n + 1, 1 - s, r + s)
                            if c == 1 and not last:
                                lv(n + 1, 1 - s, before(DVE_BLOCKS, r, s))
                        if last:
                            gather(n, NQ - 2)
                            gather(n, NQ - 1)

                    pe.wait_ge(zeroed, 2)
                    pe.wait_ge(psO_clear, 1)
                    pe.wait_ge(c_in, 32)
                    turn(0, 0, 0)
                    lv(0, 0, 0)
                    step(0, 0, 0, first=True)
                    step(1, 1, 0)
                    with pe.Fori(1, NXP // 2 - 1) as i:
                        for s in range(2):
                            step(i * 2 + s, s, i)
                    step(NXP - 2, 0, NXP // 2 - 1)
                    step(NXP - 1, 1, NXP // 2 - 1, last=True)

                @block.scalar
                def _(act):
                    def keep_xT(n, s):
                        act.wait_ge(turned, HEAD + n + 1)
                        nc.scalar.copy(xT[:, s], psT[:, 0:D].rearrange("p (k t) -> p k t", k=KT)).then_inc(xT_done, 1)

                    def keep_lv(n, s, read):
                        act.wait_ge(lv_made, HEAD + n + 1)
                        act.wait_ge(z_pool, HEAD + read)
                        nc.scalar.copy(lvs[:, s, :], psL[:, s, 0:D]).then_inc(lv_kept, 1)

                    def cut_heads(n, c):
                        act.wait_ge(z_used, HEAD + n * NYB + 2 * c + 2)
                        act.wait_ge(gathered, HEAD + n * NQ + c - 1)
                        for h in range(H):
                            ins = nc.scalar.activation(cut[:, c % 2, :, h * DK:(h + 1) * DK], psO[:, c % 2, :, h * DK:(h + 1) * DK], ACT.Copy,
                                                       scale=mask[:, h:h + 1])
                        ins.then_inc(cut_done, 1)

                    def keep_o(n, s, r):
                        act.wait_ge(gathered, HEAD + n * NQ + NQ)
                        if r is not None:
                            act.wait_ge(o_out[s], r * 16)
                        nc.scalar.copy(oS[:, s, :], psN[:, 0:D]).then_inc(o_kept, 1)
                        act.wait_ge(o_kept, HEAD + n + 1)
                        act.dma_start(o_d[b, bass.ds(n, 1)].rearrange("o r d -> (o r) d"), oS[:, s, :]).then_inc(o_out[s], 16)

                    def step(n, s, r, first=False, opening=False, last=False):
                        cut_heads(n, 0)
                        if not last:
                            keep_xT(n + 1, 1 - s)
                        cut_heads(n, 1)
                        if not last:
                            keep_lv(n + 1, 1 - s, before(POOL_BLOCKS, r, s))
                        if not first:
                            keep_o(n - 1, 1 - s, None if opening else r + s - 1)
                        cut_heads(n, 2)
                        cut_heads(n, 3)

                    act.wait_ge(c_in, 32)
                    keep_xT(0, 0)
                    keep_lv(0, 0, 0)
                    step(0, 0, 0, first=True)
                    step(1, 1, 0, opening=True)
                    step(2, 0, 1, opening=True)
                    step(3, 1, 1)
                    with act.Fori(2, NXP // 2 - 1) as i:
                        for s in range(2):
                            step(i * 2 + s, s, i)
                    step(NXP - 2, 0, NXP // 2 - 1)
                    step(NXP - 1, 1, NXP // 2 - 1, last=True)
                    keep_o(NXP - 1, 1, NXP // 2 - 1)

                @block.vector
                def _(dve):
                    nc.vector.memset(psO[:, :, :, :], 0.0).then_inc(psO_clear, 1)
                    nc.vector.memset(pair[0:N, :, 1], 0.0).then_inc(zeroed, 1)
                    nc.vector.memset(pair[N:P, :, 0], 0.0).then_inc(zeroed, 1)
                    with dve.Fori(0, NXP // 2) as i:
                        for s in range(2):
                            n = i * 2 + s
                            dve.wait_ge(lv_kept, HEAD + n + 1)
                            for k in DVE_BLOCKS[s]:
                                dve.wait_ge(z_used, HEAD + (n - 1) * NYB + k + 1)
                                nc.vector.tensor_tensor(Z[:, k], psL[:, s, 0:D].unsqueeze(1).broadcast_to([P, YB, D]), rv[:, k * YB:(k + 1) * YB, :],
                                                        ALU.mult).then_inc(z_dve, 1)

                @block.gpsimd
                def _(pool):
                    with pool.Fori(0, NXP // 2) as i:
                        for s in range(2):
                            n = i * 2 + s
                            pool.wait_ge(lv_kept, HEAD + n + 1)
                            for k in POOL_BLOCKS[s]:
                                pool.wait_ge(z_used, HEAD + (n - 1) * NYB + k + 1)
                                nc.gpsimd.tensor_tensor(Z[:, k], lvs[:, s, :].unsqueeze(1).broadcast_to([P, YB, D]), rv[:, k * YB:(k + 1) * YB, :],
                                                        ALU.mult).then_inc(z_pool, 1)


def dense_phase(nc, x, o_d, w_out, g1, b1n, w1, b1, w2, b2, g2, b2n, ident_d, t_d, xlT_d):
    U = 2
    NT = B * T // P // U
    F1 = 2 * D
    MT = F1 // P
    with ExitStack() as stack:
        ph = Phase(nc, stack, "de")
        ident = ph.sb("ident", [P, P])
        wo = ph.sb("wo", [P, KT, D])
        wa = ph.sb("wa", [P, KT, F1])
        wb = ph.sb("wb", [P, MT, D])
        row = {name: ph.sb(name, [P, n]) for name, n in (("g1", D), ("b1n", D), ("b1", F1), ("b2", D), ("g2", D), ("b2n", D))}
        eps = ph.sb("eps", [P, 1])
        oin = ph.sb("oin", [P, 2, U, D])
        xres = ph.sb("xres", [P, 2, U, D])
        oT = ph.sb("oT", [P, 2, KT, U * P])
        hT = ph.sb("hT", [P, 2, KT, U * P])
        mT = ph.sb("mT", [P, 2, MT, U * P])
        xT = ph.sb("xT", [P, 2, KT, U * P])
        h0 = ph.sb("h0", [P, 2, U, D])
        hn = ph.sb("hn", [P, 2, U, D])
        hg = ph.sb("hg", [P, 2, U, D])
        hs = ph.sb("hs", [P, 2, U, D])
        hb2 = ph.sb("hb2", [P, NT, U, D])
        ma = ph.sb("ma", [P, 2, U, F1])
        m = ph.sb("m", [P, 2, U, F1])
        t0 = ph.sb("t0", [P, 2, U, D])
        tn = ph.sb("tn", [P, 2, U, D])
        tg = ph.sb("tg", [P, 2, U, D])
        ts = ph.sb("ts", [P, 2, U, D])
        xl = ph.sb("xl", [P, 2, U, D])
        stats = ph.sb("stats", [P, 3, 2, U, 6])
        mv = ph.sb("mv", [P, 3, 2, U, 2])
        std = ph.sb("std", [P, 3, 2, U, 1])
        rstd = ph.sb("rstd", [P, 3, 2, U, 1])
        ps_o, ps_h, ps_x, ps_1 = (ph.ps(f"ps_{n}", [P, U * D]) for n in "ohx1")
        ps_3 = ps_1
        ps_m, ps_2 = (ph.ps(f"ps_{n}", [P, U * F1]) for n in "m2")
        w_in = ph.sem("w_in")
        eps_set = ph.sem("eps_set")
        passed = ph.sem("passed")
        in_ = [ph.sem(f"in{s}") for s in range(2)]
        t_out = [ph.sem(f"t_out{s}") for s in range(2)]
        x_out = [ph.sem(f"x_out{s}") for s in range(2)]
        names = ("o_turned h_turned m_turned x_turned oT_kept hT_kept mT_kept xT_kept made1 made2 made3 "
                 "added1 biased relued added3 h_scaled h_done hb2_done t_scaled t_done").split()
        q = {n: ph.sem(n) for n in names}
        ln = [{n: ph.sem(f"{n}{j}") for n in ("stated", "aggregated", "rooted", "inverted", "normed")} for j in range(3)]
        start_at_head(nc, list(q.values()) + [v for d in ln for v in d.values()] + t_out + x_out)
        weights = [(ident[:, :], ident_d), (wo[:, :, :], k_rows(w_out)), (wa[:, :, :], k_rows(w1)), (wb[:, :, :], k_rows(w2))] + [
            (row[n][:, :], v.rearrange("(o n) -> o n", o=1).broadcast_to([P, row[n].shape[1]]))
            for n, v in (("g1", g1), ("b1n", b1n), ("b1", b1), ("b2", b2), ("g2", g2), ("b2n", b2n))]

        def iterations(eng, body):
            def fixed(i):
                body(i, i % 2, i // 2, lambda k: 0 <= i - 2 * k < NT)
            for i in range(8):
                fixed(i)
            with eng.Fori(4, NT // 2) as r:
                for s in range(2):
                    body(r * 2 + s, s, r, lambda k: True)
            for i in range(NT, NT + 8):
                fixed(i)

        def tiles(v):
            return v[:, :].rearrange("p (u d) -> p u d", u=U)

        def both(name):
            return row[name][:, :].unsqueeze(1).broadcast_to([P, U, row[name].shape[1]])

        def tile_rows(v, n):
            return v[bass.ds(n * (U * P), U * P), :].rearrange("(u p) d -> p u d", p=P)

        with nc.Block() as block:
            @block.sync
            def _(sp):
                for dst, src in weights:
                    sp.dma_start(dst, src).then_inc(w_in, 16)

                def body(i, s, r, live):
                    if live(0):
                        sp.wait_ge(q["o_turned"], HEAD + i - 1)
                        sp.wait_ge(q["added1"], HEAD + i - 1)
                        ox = o_d.rearrange("b n (y x) d -> (b n) x y d", x=2)
                        for c in range(2):
                            sp.dma_start(oin[c * N:(c + 1) * N, s], ox[bass.ds(i * U, U), c].rearrange("u y d -> y u d")).then_inc(in_[s], 16)
                        sp.dma_start(xres[:, s], tile_rows(x.rearrange("b x y d -> (b x y) d"), i)).then_inc(in_[s], 16)
                    if live(3):
                        n = i - 6
                        sp.wait_ge(q["t_done"], HEAD + n + 1)
                        sp.dma_start(tile_rows(t_d.rearrange("b t d -> (b t) d"), n), ts[:, s]).then_inc(t_out[s], 16)
                    if live(4):
                        n = i - 8
                        sp.wait_ge(q["xT_kept"], HEAD + n + 1)
                        sp.dma_start(xlT_d[:, :, bass.ds(n * (U * P), U * P)].rearrange("k p t -> p k t"), xT[:, s]).then_inc(x_out[s], 16)

                iterations(sp, body)
                for s in range(2):
                    sp.wait_ge(t_out[s], HEAD + 16 * (NT // 2))
                    sp.wait_ge(x_out[s], HEAD + 16 * (NT // 2))

            @block.tensor
            def _(pe):
                def turn(dst, src, blocks, done):
                    for k in range(blocks):
                        for u in range(U):
                            mm = pe.transpose(dst[:, (k * U + u) * P:(k * U + u + 1) * P], src[:, u, k * P:(k + 1) * P], ident[:, :])
                    mm.then_inc(done, 1)

                def product(dst, lhsT, w, blocks, done):
                    width = w.shape[2]
                    for u in range(U):
                        for k in range(blocks):
                            mm = pe.matmul(dst[:, u * width:(u + 1) * width], lhsT[:, k, u * P:(u + 1) * P], w[:, k, :], start=(k == 0), stop=(k == blocks - 1))
                    mm.then_inc(done, 1)

                def body(i, s, r, live):
                    if live(0):
                        pe.wait_ge(in_[s], r * 48 + 48)
                        turn(ps_o, oin[:, s], KT, q["o_turned"])
                    if live(1):
                        pe.wait_ge(q["h_done"], HEAD + i - 2 + 1)
                        turn(ps_h, hs[:, s], KT, q["h_turned"])
                    if live(2):
                        pe.wait_ge(q["relued"], HEAD + i - 4 + 1)
                        turn(ps_m, m[:, s], MT, q["m_turned"])
                    if live(4):
                        pe.wait_ge(ln[2]["normed"], HEAD + i - 8 + 1)
                        pe.wait_ge(q["xT_kept"], HEAD + i - 8)
                        turn(ps_x, xl[:, s], KT, q["x_turned"])
                    if live(0):
                        pe.wait_ge(q["oT_kept"], HEAD + i + 1)
                        if live(2.5):
                            pe.wait_ge(q["added3"], HEAD + i - 4)
                        product(ps_1, oT[:, s], wo, KT, q["made1"])
                    if live(1):
                        pe.wait_ge(q["hT_kept"], HEAD + i - 2 + 1)
                        pe.wait_ge(q["biased"], HEAD + i - 2)
                        product(ps_2, hT[:, s], wa, KT, q["made2"])
                    if live(2):
                        pe.wait_ge(q["mT_kept"], HEAD + i - 4 + 1)
                        pe.wait_ge(q["added3"], HEAD + i - 4)
                        if live(0):
                            pe.wait_ge(q["added1"], HEAD + i + 1)
                        product(ps_3, mT[:, s], wb, MT, q["made3"])

                pe.wait_ge(w_in, 16 * len(weights))
                iterations(pe, body)

            @block.scalar
            def _(act):
                def keep(dst, src, blocks, done):
                    nc.scalar.copy(dst, src[:, :].rearrange("p (k t) -> p k t", k=blocks)).then_inc(done, 1)

                def root(j, n, s):
                    act.wait_ge(ln[j]["aggregated"], HEAD + n + 1)
                    nc.scalar.activation(std[:, j, s], mv[:, j, s, :, 1:2], ACT.Sqrt, bias=eps[:, :]).then_inc(ln[j]["rooted"], 1)

                def body(i, s, r, live):
                    if live(0):
                        act.wait_ge(q["o_turned"], HEAD + i + 1)
                        keep(oT[:, s], ps_o, KT, q["oT_kept"])
                    if live(1):
                        act.wait_ge(q["h_turned"], HEAD + i - 2 + 1)
                        keep(hT[:, s], ps_h, KT, q["hT_kept"])
                    if live(2.5):
                        root(1, i - 5, 1 - s)
                    if live(2):
                        act.wait_ge(q["m_turned"], HEAD + i - 4 + 1)
                        keep(mT[:, s], ps_m, MT, q["mT_kept"])
                    if live(4):
                        act.wait_ge(q["x_turned"], HEAD + i - 8 + 1)
                        act.wait_ge(x_out[s], HEAD + (r - 4) * 16)
                        keep(xT[:, s], ps_x, KT, q["xT_kept"])
                    if live(0):
                        root(0, i, s)
                    if live(3):
                        root(2, i - 6, s)
                    if live(1):
                        act.wait_ge(q["biased"], HEAD + i - 2 + 1)
                        nc.scalar.activation(m[:, s], ma[:, s], ACT.Relu).then_inc(q["relued"], 1)

                act.wait_ge(eps_set, 1)
                iterations(act, body)

            @block.vector
            def _(dve):
                def moments(j, n, s, src):
                    for u in range(U):
                        ins = nc.vector.bn_stats(stats[:, j, s, u, :], src[:, u])
                    ins.then_inc(ln[j]["stated"], 1)
                    dve.wait_ge(ln[j]["stated"], HEAD + n + 1)
                    dve.sem_inc(passed, 1)
                    for u in range(U):
                        ins = nc.vector.bn_aggr(mv[:, j, s, u, :], stats[:, j, s, u, :])
                    ins.then_inc(ln[j]["aggregated"], 1)

                def normalise(j, n, s, dst, src):
                    dve.wait_ge(ln[j]["rooted"], HEAD + n + 1)
                    nc.vector.reciprocal(rstd[:, j, s], std[:, j, s]).then_inc(ln[j]["inverted"], 1)
                    dve.wait_ge(ln[j]["inverted"], HEAD + n + 1)
                    for u in range(U):
                        ins = nc.vector.tensor_scalar(dst[:, u], src[:, u], mv[:, j, s, u, 0:1], rstd[:, j, s, u, :], ALU.subtract, ALU.mult)
                    ins.then_inc(ln[j]["normed"], 1)

                def body(i, s, r, live):
                    if live(0):
                        dve.wait_ge(in_[s], r * 48 + 48)
                        dve.wait_ge(q["made1"], HEAD + i + 1)
                        nc.vector.tensor_tensor(h0[:, s], tiles(ps_1), xres[:, s], ALU.add).then_inc(q["added1"], 1)
                        dve.wait_ge(q["added1"], HEAD + i + 1)
                        moments(0, i, s, h0[:, s])
                    if live(2.5):
                        dve.wait_ge(q["t_scaled"], HEAD + i - 5 - 1)
                        normalise(1, i - 5, 1 - s, tn[:, 1 - s], t0[:, 1 - s])
                    if live(3):
                        dve.wait_ge(q["t_done"], HEAD + i - 6 + 1)
                        moments(2, i - 6, s, ts[:, s])
                    if live(1):
                        dve.wait_ge(q["made2"], HEAD + i - 2 + 1)
                        dve.wait_ge(q["relued"], HEAD + i - 2 - 1)
                        nc.vector.tensor_tensor(ma[:, s], tiles(ps_2), both("b1"), ALU.add).then_inc(q["biased"], 1)
                    if live(0):
                        dve.wait_ge(q["h_scaled"], HEAD + i - 1)
                        normalise(0, i, s, hn[:, s], h0[:, s])
                    if live(3):
                        dve.wait_ge(q["x_turned"], HEAD + i - 6 - 1)
                        normalise(2, i - 6, s, xl[:, s], ts[:, s])
                    if live(2):
                        dve.wait_ge(q["made3"], HEAD + i - 4 + 1)
                        dve.wait_ge(q["hb2_done"], HEAD + i - 4 + 1)
                        nc.vector.tensor_tensor(t0[:, s], tiles(ps_3), hb2[:, bass.ds(i - 4, 1)].rearrange("p o u d -> p (o u) d"), ALU.add).then_inc(q["added3"], 1)
                        dve.wait_ge(q["added3"], HEAD + i - 4 + 1)
                        moments(1, i - 4, s, t0[:, s])

                nc.vector.memset(eps[:, :], LN_EPS).then_inc(eps_set, 1)
                dve.wait_ge(w_in, 16 * len(weights))
                iterations(dve, body)

            @block.gpsimd
            def _(pool):
                def body(i, s, r, live):
                    if live(2.5):
                        n, o = i - 5, 1 - s
                        pool.wait_ge(ln[1]["normed"], HEAD + n + 1)
                        nc.gpsimd.tensor_tensor(tg[:, o], tn[:, o], both("g2"), ALU.mult).then_inc(q["t_scaled"], 1)
                        pool.wait_ge(q["t_scaled"], HEAD + n + 1)
                        pool.wait_ge(t_out[o], HEAD + (r + s - 3) * 16)
                        pool.wait_ge(ln[2]["normed"], HEAD + n - 1)
                        nc.gpsimd.tensor_tensor(ts[:, o], tg[:, o], both("b2n"), ALU.add).then_inc(q["t_done"], 1)
                    if live(0):
                        pool.wait_ge(ln[0]["normed"], HEAD + i + 1)
                        nc.gpsimd.tensor_tensor(hg[:, s], hn[:, s], both("g1"), ALU.mult).then_inc(q["h_scaled"], 1)
                        pool.wait_ge(q["h_scaled"], HEAD + i + 1)
                        pool.wait_ge(q["h_turned"], HEAD + i - 1)
                        nc.gpsimd.tensor_tensor(hs[:, s], hg[:, s], both("b1n"), ALU.add).then_inc(q["h_done"], 1)
                        pool.wait_ge(q["h_done"], HEAD + i + 1)
                        nc.gpsimd.tensor_tensor(hb2[:, bass.ds(i, 1)].rearrange("p o u d -> p (o u) d"), hs[:, s], both("b2"), ALU.add).then_inc(q["hb2_done"], 1)
                iterations(pool, body)


def attention_phase(nc, b, t_d, xlT_d, wqT, bq, wkT, bk, wvT, bv, ident_d, t2_d):
    NT = T // P
    BLK = 512
    NBLK = T // BLK
    KB = BLK // P
    with ExitStack() as stack:
        ph = Phase(nc, stack, f"at{b}")
        ident = ph.sb("ident", [P, P])
        qT = ph.sb("qT", [P, KT, T])
        k_hi = ph.sb("k_hi", [P, KT, T], F32R)
        k_lo = ph.sb("k_lo", [P, KT, T], F32R)
        v_hi = ph.sb("v_hi", [P, T // P, D], F32R)
        v_lo = ph.sb("v_lo", [P, T // P, D], F32R)

        with ExitStack() as inner:
            pj = Phase(nc, inner, f"qk{b}")
            w = [pj.sb(n, [P, KT, D]) for n in ("wq", "wk", "wv")]
            bias = [pj.sb(n, [P, KT]) for n in ("bq", "bk")]
            bvr = pj.sb("bvr", [P, D])
            xs = pj.sb("xs", [P, 2, KT, BLK])
            v = pj.sb("v", [P, 2, 2, D])
            psP = pj.ps("psP", [P, 2 * KT, BLK])
            psV = pj.ps("psV", [P, KB, D])
            w_in = pj.sem("w_in")
            x_in = [pj.sem(f"x_in{s}") for s in range(2)]
            made = pj.sem("made")
            q_kept, k_hi_kept, v_hi_kept = (pj.sem(n) for n in ("q_kept", "k_hi_kept", "v_hi_kept"))
            k_lo_kept, v_biased = (pj.sem(n) for n in ("k_lo_kept", "v_biased"))
            passed = pj.sem("passed")
            v_lo_kept = pj.sem("v_lo_kept")
            start_at_head(nc, [made, q_kept, k_hi_kept, v_hi_kept, k_lo_kept, v_biased, v_lo_kept])
            loads = [(ident[:, :], ident_d), (w[0][:, :, :], k_rows(wqT)), (w[1][:, :, :], k_rows(wkT)), (w[2][:, :, :], k_rows(wvT)),
                     (bias[0][:, :], bq.rearrange("(k p) -> p k", p=P)), (bias[1][:, :], bk.rearrange("(k p) -> p k", p=P)),
                     (bvr[:, :], bv.rearrange("(o n) -> o n", o=1).broadcast_to([P, D]))]
            with nc.Block() as block:
                @block.sync
                def _(sp):
                    with nc.allow_non_contiguous_dma("two biases of 256 numbers, one to a partition"):
                        for dst, src in loads:
                            sp.dma_start(dst, src).then_inc(w_in, 16)
                    with sp.Fori(0, NBLK // 2) as r:
                        for s in range(2):
                            n = r * 2 + s
                            sp.wait_ge(made, HEAD + (n - 1) * 6)
                            sp.dma_start(xs[:, s], xlT_d[:, :, bass.ds(n * BLK + b * T, BLK)].rearrange("k p t -> p k t")).then_inc(x_in[s], 16)

                @block.tensor
                def _(pe):
                    pe.wait_ge(w_in, 16 * len(loads))
                    with pe.Fori(0, NBLK // 2) as r:
                        for s in range(2):
                            n = r * 2 + s
                            pe.wait_ge(x_in[s], r * 16 + 16)
                            for j in range(2 * KT):
                                pe.wait_ge((q_kept, k_lo_kept)[j // KT], HEAD + (n - 1) * KT + j % KT + 1)
                                for k in range(KT):
                                    mm = pe.matmul(psP[:, j, :], w[j // KT][:, k, (j % KT) * P:(j % KT + 1) * P], xs[:, s, k, :], start=(k == 0), stop=(k == KT - 1))
                                mm.then_inc(made, 1)
                            for u in range(2):
                                pe.wait_ge(v_biased, HEAD + (n - 1) * 2 + u + 1)
                                for t in (2 * u, 2 * u + 1):
                                    for k in range(KT):
                                        mm = pe.matmul(psV[:, t, :], xs[:, s, k, t * P:(t + 1) * P], w[2][:, k, :], start=(k == 0), stop=(k == KT - 1))
                                mm.then_inc(made, 1)

                @block.scalar
                def _(act):
                    act.wait_ge(w_in, 16 * len(loads))
                    with act.Fori(0, NBLK // 2) as r:
                        for s in range(2):
                            n = r * 2 + s
                            for j in range(2 * KT):
                                act.wait_ge(made, HEAD + n * 6 + j + 1)
                                nc.scalar.activation((qT, k_hi)[j // KT][:, j % KT, bass.ds(n * BLK, BLK)], psP[:, j, :], ACT.Identity,
                                                     bias=bias[j // KT][:, j % KT:j % KT + 1]).then_inc((q_kept, k_hi_kept)[j // KT], 1)
                            for u in range(2):
                                act.wait_ge(v_biased, HEAD + n * 2 + u + 1)
                                nc.scalar.copy(v_hi[:, bass.ds(n * KB + 2 * u, 2), :], v[:, u]).then_inc(v_hi_kept, 1)

                @block.gpsimd
                def _(pool):
                    with pool.Fori(0, NBLK // 2) as r:
                        for s in range(2):
                            n = r * 2 + s
                            for u in range(2):
                                part = bass.ds(n * KB + 2 * u, 2)
                                pool.wait_ge(v_hi_kept, HEAD + n * 2 + u + 1)
                                pool.sem_inc(passed, 1)
                                nc.gpsimd.tensor_tensor(v_lo[:, part, :], v[:, u], v_hi[:, part, :], ALU.subtract).then_inc(v_lo_kept, 1)

                @block.vector
                def _(dve):
                    dve.wait_ge(w_in, 16 * len(loads))
                    with dve.Fori(0, NBLK // 2) as r:
                        for s in range(2):
                            n = r * 2 + s
                            for k in range(KT):
                                part = bass.ds(n * BLK, BLK)
                                dve.wait_ge(k_hi_kept, HEAD + n * KT + k + 1)
                                nc.vector.scalar_tensor_tensor(out=k_lo[:, k, part], in0=psP[:, KT + k, :], scalar=bias[1][:, k:k + 1], in1=k_hi[:, k, part],
                                                               op0=ALU.add, op1=ALU.subtract).then_inc(k_lo_kept, 1)
                            for u in range(2):
                                dve.wait_ge(made, HEAD + n * 6 + 4 + u + 1)
                                dve.wait_ge(v_lo_kept, HEAD + (n - 1) * 2 + u + 1)
                                nc.vector.tensor_tensor(v[:, u], psV[:, 2 * u:2 * u + 2, :],
                                                        bvr[:, :].unsqueeze(1).broadcast_to([P, 2, D]), ALU.add).then_inc(v_biased, 1)

        with ExitStack() as inner:
            ap = Phase(nc, inner, f"sv{b}")
            SCALE = float(D) ** -0.5
            q_hi = ap.sb("q_hi", [P, 2, KT, P], F32R)
            q_lo = ap.sb("q_lo", [P, 2, KT, P], F32R)
            S = ap.sb("S", [P, 2, NBLK, BLK])
            mx = ap.sb("mx", [P, 2, NBLK])
            top = ap.sb("top", [P, 2, 1])
            shift = ap.sb("shift", [P, 2, 1])
            part = ap.sb("part", [P, 2, NBLK])
            den = ap.sb("den", [P, 2, 1])
            rden = ap.sb("rden", [P, 2, 1])
            p_hi = ap.sb("p_hi", [P, 2, KB, P], F32R)
            p_lo = ap.sb("p_lo", [P, 2, KB, P], F32R)
            t = ap.sb("t", [P, 2, D])
            psS = ap.ps("psS", [P, 4, BLK])
            psT = ap.ps("psT", [P, 2, BLK])
            psO = ap.ps("psO", [P, 2, 512])
            t_in = [ap.sem(f"t_in{s}") for s in range(2)]
            t2_out = [ap.sem(f"t2_out{s}") for s in range(2)]
            q_hi_cut = ap.sem("q_hi_cut")
            passed = ap.sem("passed")
            q_cut = ap.sem("q_cut")
            scored = ap.sem("scored")
            kept = ap.sem("kept")
            maxed = ap.sem("maxed")
            topped = ap.sem("topped")
            shifted = ap.sem("shifted")
            exped = ap.sem("exped")
            turned = ap.sem("turned")
            hi_kept = ap.sem("hi_kept")
            pT_kept = ap.sem("pT_kept")
            weighed = ap.sem("weighed")
            summed = ap.sem("summed")
            inverted = ap.sem("inverted")
            added = ap.sem("added")
            start_at_head(nc, [q_hi_cut, hi_kept, q_cut, scored, kept, maxed, topped, shifted, exped, turned, pT_kept, weighed, summed, inverted, added] + t2_out)
            C = NBLK

            def tiles(eng, body):
                body(0, 0, 0, True)
                body(1, 1, 0, True)
                with eng.Fori(1, NT // 2 - 1) as r:
                    for s in range(2):
                        body(r * 2 + s, s, r, True)
                body(NT - 2, 0, NT // 2 - 1, True)
                body(NT - 1, 1, NT // 2 - 1, False)

            with nc.Block() as block:
                @block.sync
                def _(sp):
                    def load(n, s, r):
                        sp.wait_ge(t2_out[s], HEAD + r * 16)
                        sp.dma_start(t[:, s, :], t_d[b, bass.ds(n * P, P), :]).then_inc(t_in[s], 16)

                    def save(n, s):
                        sp.wait_ge(added, HEAD + n + 1)
                        sp.dma_start(t2_d[b, bass.ds(n * P, P), :], t[:, s, :]).then_inc(t2_out[s], 16)

                    for s in range(2):
                        load(s, s, 0)
                    with sp.Fori(0, NT // 2 - 1) as r:
                        for s in range(2):
                            save(r * 2 + s, s)
                            load(r * 2 + s + 2, s, r + 1)
                    for s in range(2):
                        save(NT - 2 + s, s)
                    for s in range(2):
                        sp.wait_ge(t2_out[s], HEAD + 16 * (NT // 2))

                @block.gpsimd
                def _(pool):
                    with pool.Fori(0, NT // 2) as r:
                        for s in range(2):
                            n = r * 2 + s
                            pool.wait_ge(scored, HEAD + (n - 1) * C)
                            nc.gpsimd.tensor_copy(q_hi[:, s], qT[:, :, bass.ds(n * P, P)]).then_inc(q_hi_cut, 1)
                            pool.wait_ge(q_hi_cut, HEAD + n + 1)
                            pool.sem_inc(passed, 1)
                            nc.gpsimd.tensor_tensor(q_lo[:, s], qT[:, :, bass.ds(n * P, P)], q_hi[:, s], ALU.subtract).then_inc(q_cut, 1)

                @block.tensor
                def _(pe):
                    def score(n, s, c):
                        if c == 0:
                            pe.wait_ge(q_cut, HEAD + n + 1)
                        pe.wait_ge(kept, HEAD + n * C + c - 3)
                        terms = [(a, b, k) for k in range(KT) for a, b in ((q_hi, k_hi), (q_hi, k_lo), (q_lo, k_hi))]
                        for i, (a, b, k) in enumerate(terms):
                            mm = pe.matmul(psS[:, c % 4, :], a[:, s, k, :], b[:, k, c * BLK:(c + 1) * BLK], start=(i == 0), stop=(i == len(terms) - 1))
                        mm.then_inc(scored, 1)

                    def turn(n, s, c):
                        pe.wait_ge(exped, HEAD + n * C + c + 1)
                        pe.wait_ge(pT_kept, HEAD + n * C + c - 1)
                        for t in range(KB):
                            mm = pe.transpose(psT[:, c % 2, t * P:(t + 1) * P], S[:, s, c, t * P:(t + 1) * P], ident[:, :])
                        mm.then_inc(turned, 1)

                    def weigh(n, s, c):
                        pe.wait_ge(pT_kept, HEAD + n * C + c + 1)
                        if c == 0:
                            pe.wait_ge(added, HEAD + n - 1)
                        terms = [(a, b, t) for t in range(KB) for a, b in ((p_hi, v_hi), (p_hi, v_lo), (p_lo, v_hi))]
                        for i, (a, b, t) in enumerate(terms):
                            mm = pe.matmul(psO[:, s, 0:D], a[:, c % 2, t, :], b[:, c * KB + t, :],
                                           start=(c == 0 and i == 0), stop=(c == C - 1 and i == len(terms) - 1))
                        mm.then_inc(weighed, 1)

                    def body(n, s, r, ahead):
                        for step in range(C + 4):
                            if ahead and step < C:
                                score(n + 1, 1 - s, step)
                            if 3 <= step < C + 3:
                                turn(n, s, step - 3)
                            if 4 <= step:
                                weigh(n, s, step - 4)

                    for c in range(C):
                        score(0, 0, c)
                    tiles(pe, body)

                @block.scalar
                def _(act):
                    def keep(n, s, c):
                        act.wait_ge(scored, HEAD + n * C + c + 1)
                        nc.scalar.copy(S[:, s, c, :], psS[:, c % 4, :]).then_inc(kept, 1)

                    def exponent(n, s, c):
                        if c == 0:
                            act.wait_ge(shifted, HEAD + n + 1)
                        nc.scalar.activation(S[:, s, c, :], S[:, s, c, :], ACT.Exp, bias=shift[:, s, :], scale=SCALE,
                                             accum_out=part[:, s, c:c + 1]).then_inc(exped, 1)

                    def keep_hi(n, s, c):
                        act.wait_ge(turned, HEAD + n * C + c + 1)
                        act.wait_ge(weighed, HEAD + n * C + c - 1)
                        nc.scalar.copy(p_hi[:, c % 2], psT[:, c % 2, :].rearrange("p (t q) -> p t q", t=KB)).then_inc(hi_kept, 1)

                    def body(n, s, r, ahead):
                        exponent(n, s, 0)
                        for step in range(C + 3):
                            if step + 1 < C:
                                exponent(n, s, step + 1)
                            if ahead and step < C:
                                keep(n + 1, 1 - s, step)
                            if step >= 3:
                                keep_hi(n, s, step - 3)

                    for c in range(C):
                        keep(0, 0, c)
                    tiles(act, body)

                @block.vector
                def _(dve):
                    def most(n, s, c):
                        dve.wait_ge(kept, HEAD + n * C + c + 1)
                        nc.vector.tensor_reduce(mx[:, s, c:c + 1], S[:, s, c, :], AX_X, ALU.max).then_inc(maxed, 1)

                    def bias(n, s):
                        dve.wait_ge(maxed, HEAD + n * C + C)
                        nc.vector.tensor_reduce(top[:, s, :], mx[:, s, :], AX_X, ALU.max).then_inc(topped, 1)
                        dve.wait_ge(topped, HEAD + n + 1)
                        nc.vector.tensor_scalar(shift[:, s, :], top[:, s, :], -SCALE, None, ALU.mult).then_inc(shifted, 1)

                    def keep_pT(n, s, c):
                        dve.wait_ge(hi_kept, HEAD + n * C + c + 1)
                        nc.vector.tensor_tensor(p_lo[:, c % 2], psT[:, c % 2, :].rearrange("p (t q) -> p t q", t=KB), p_hi[:, c % 2],
                                                ALU.subtract).then_inc(pT_kept, 1)

                    def finish(n, s, r):
                        nc.vector.tensor_reduce(den[:, s, :], part[:, s, :], AX_X, ALU.add).then_inc(summed, 1)
                        dve.wait_ge(summed, HEAD + n + 1)
                        nc.vector.reciprocal(rden[:, s, :], den[:, s, :]).then_inc(inverted, 1)
                        dve.wait_ge(weighed, HEAD + n * C + C)
                        dve.wait_ge(inverted, HEAD + n + 1)
                        dve.wait_ge(t_in[s], r * 16 + 16)
                        nc.vector.scalar_tensor_tensor(out=t[:, s, :], in0=psO[:, s, 0:D], scalar=rden[:, s, :], in1=t[:, s, :],
                                                       op0=ALU.mult, op1=ALU.add).then_inc(added, 1)

                    def body(n, s, r, ahead):
                        for step in range(C + 3):
                            if ahead and step < C:
                                most(n + 1, 1 - s, step)
                                if step == C - 1:
                                    bias(n + 1, 1 - s)
                            if step >= 3:
                                keep_pT(n, s, step - 3)
                        finish(n, s, r)

                    for c in range(C):
                        most(0, 0, c)
                    bias(0, 0)
                    tiles(dve, body)


def gates_phase(nc, t2_d, u, bg, ident_d, xg_d):
    U = 2
    NT = B * T // P // U
    GW = 3 * D
    with ExitStack() as stack:
        ph = Phase(nc, stack, "ga")
        ident = ph.sb("ident", [P, P])
        w = ph.sb("w", [P, KT, GW])
        bias = ph.sb("bias", [P, GW])
        eps = ph.sb("eps", [P, 1])
        tin = ph.sb("tin", [P, 2, U, D])
        xl = ph.sb("xl", [P, 2, U, D])
        xT = ph.sb("xT", [P, 2, KT, U * P])
        xg = ph.sb("xg", [P, 2, U, GW])
        stats = ph.sb("stats", [P, 2, U, 6])
        mv = ph.sb("mv", [P, 2, U, 2])
        std = ph.sb("std", [P, 2, U, 1])
        rstd = ph.sb("rstd", [P, 2, U, 1])
        psT = ph.ps("psT", [P, 2, 512])
        psG = ph.ps("psG", [P, U, 1024])
        w_in, eps_set, passed = ph.sem("w_in"), ph.sem("eps_set"), ph.sem("passed")
        t_in = [ph.sem(f"t_in{s}") for s in range(2)]
        g_out = [ph.sem(f"g_out{s}") for s in range(2)]
        stated, aggregated, rooted, inverted, normed, turned, xT_kept, made, biased = (
            ph.sem(n) for n in "stated aggregated rooted inverted normed turned xT_kept made biased".split())
        start_at_head(nc, [stated, aggregated, rooted, inverted, normed, turned, xT_kept, made, biased] + g_out)
        loads = [(ident[:, :], ident_d)] + [(w[:, :, j * D:(j + 1) * D], k_rows(u[j])) for j in range(3)] + [
            (bias[:, j * D:(j + 1) * D], bg[j].rearrange("(o n) -> o n", o=1).broadcast_to([P, D])) for j in range(3)]

        def iterations(eng, body):
            for i in range(4):
                body(i, i % 2, i // 2, lambda k, i=i: i - 2 * k >= 0)
            with eng.Fori(2, NT // 2) as r:
                for s in range(2):
                    body(r * 2 + s, s, r, lambda k: True)
            for i in range(NT, NT + 4):
                body(i, i % 2, i // 2, lambda k, i=i: i - 2 * k < NT)

        def tile_rows(v, n):
            return v.rearrange("b t d -> (b t) d")[bass.ds(n * (U * P), U * P), :].rearrange("(u p) d -> p u d", p=P)

        with nc.Block() as block:
            @block.sync
            def _(sp):
                for dst, src in loads:
                    sp.dma_start(dst, src).then_inc(w_in, 16)

                def body(i, s, r, live):
                    if live(0):
                        sp.wait_ge(normed, HEAD + i - 1)
                        sp.dma_start(tin[:, s], tile_rows(t2_d, i)).then_inc(t_in[s], 16)
                    if live(2):
                        n = i - 4
                        sp.wait_ge(biased, HEAD + (n + 1) * U)
                        sp.dma_start(tile_rows(xg_d, n), xg[:, s]).then_inc(g_out[s], 16)
                iterations(sp, body)
                for s in range(2):
                    sp.wait_ge(g_out[s], HEAD + 16 * (NT // 2))

            @block.tensor
            def _(pe):
                def body(i, s, r, live):
                    if live(1):
                        n = i - 2
                        pe.wait_ge(normed, HEAD + n + 1)
                        pe.wait_ge(xT_kept, HEAD + n - 1)
                        for k in range(KT):
                            for u in range(U):
                                mm = pe.transpose(psT[:, s, (k * U + u) * P:(k * U + u + 1) * P], xl[:, s, u, k * P:(k + 1) * P], ident[:, :])
                        mm.then_inc(turned, 1)
                    if live(2):
                        n = i - 4
                        pe.wait_ge(xT_kept, HEAD + n + 1)
                        for u in range(U):
                            pe.wait_ge(biased, HEAD + (n - 1) * U + u + 1)
                            for lo, hi in ((0, 512), (512, GW)):
                                for k in range(KT):
                                    mm = pe.matmul(psG[:, u, lo:hi], xT[:, s, k, u * P:(u + 1) * P], w[:, k, lo:hi], start=(k == 0), stop=(k == KT - 1))
                            mm.then_inc(made, 1)
                pe.wait_ge(w_in, 16 * len(loads))
                iterations(pe, body)

            @block.scalar
            def _(act):
                def body(i, s, r, live):
                    if live(0):
                        act.wait_ge(aggregated, HEAD + i + 1)
                        nc.scalar.activation(std[:, s], mv[:, s, :, 1:2], ACT.Sqrt, bias=eps[:, :]).then_inc(rooted, 1)
                    if live(1):
                        n = i - 2
                        act.wait_ge(turned, HEAD + n + 1)
                        act.wait_ge(made, HEAD + (n - 1) * U)
                        nc.scalar.copy(xT[:, s], psT[:, s, :].rearrange("p (k t) -> p k t", k=KT)).then_inc(xT_kept, 1)
                act.wait_ge(eps_set, 1)
                iterations(act, body)

            @block.vector
            def _(dve):
                def body(i, s, r, live):
                    if live(0):
                        dve.wait_ge(t_in[s], r * 16 + 16)
                        for u in range(U):
                            ins = nc.vector.bn_stats(stats[:, s, u, :], tin[:, s, u])
                        ins.then_inc(stated, 1)
                        dve.wait_ge(stated, HEAD + i + 1)
                        dve.sem_inc(passed, 1)
                        for u in range(U):
                            ins = nc.vector.bn_aggr(mv[:, s, u, :], stats[:, s, u, :])
                        ins.then_inc(aggregated, 1)
                    if live(2):
                        n = i - 4
                        dve.wait_ge(g_out[s], HEAD + (r - 2) * 16)
                        for u in range(U):
                            dve.wait_ge(made, HEAD + n * U + u + 1)
                            nc.vector.tensor_tensor(xg[:, s, u, :], psG[:, u, 0:GW], bias[:, :], ALU.add).then_inc(biased, 1)
                    if live(0):
                        dve.wait_ge(rooted, HEAD + i + 1)
                        nc.vector.reciprocal(rstd[:, s], std[:, s]).then_inc(inverted, 1)
                        dve.wait_ge(inverted, HEAD + i + 1)
                        dve.wait_ge(turned, HEAD + i - 1)
                        for u in range(U):
                            ins = nc.vector.tensor_scalar(xl[:, s, u, :], tin[:, s, u, :], mv[:, s, u, 0:1], rstd[:, s, u, :], ALU.subtract, ALU.mult)
                        ins.then_inc(normed, 1)
                nc.vector.memset(eps[:, :], LN_EPS).then_inc(eps_set, 1)
                dve.wait_ge(w_in, 16 * len(loads))
                iterations(dve, body)


def recurrent_phase(nc, xg_d, v_d, ident_d, t2_d, out):
    L = T // P
    SAME = 2.0 ** -18
    GW = 3 * D
    TURNS = (L + 1, L)
    with ExitStack() as stack:
        ph = Phase(nc, stack, "re")
        ident = ph.sb("ident", [P, P])
        w = ph.sb("w", [P, KT, GW])
        w_hi = ph.sb("w_hi", [P, KT, GW], F32R)
        w_lo = ph.sb("w_lo", [P, KT, GW], F32R)
        h_hi = ph.sb("h_hi", [P, B, KT, P], F32R)
        h_lo = ph.sb("h_lo", [P, B, KT, P], F32R)
        h = ph.sb("h", [P, B, D])
        c = ph.sb("c", [P, B, D])
        hc = ph.sb("hc", [P, B, D])
        ig = ph.sb("ig", [P, B, D])
        tc = ph.sb("tc", [P, B, D])
        z = ph.sb("z", [P, B, GW])
        gate = ph.sb("gate", [P, B, GW])
        xg = ph.sb("xg", [P, B, 2, GW])
        tin = ph.sb("tin", [P, B, 2, D])
        os = ph.sb("os", [P, B, 2, D])
        start = ph.sb("start", [P, 2, B, D])
        moved = ph.sb("moved", [P, 2, B, D])
        gap = ph.sb("gap", [P, 2 * B * D])
        most = ph.sb("most", [P, 1])
        most1 = ph.sb("most1", [1, 1])
        again = ph.sb("again", [1, 1], I32)
        number = ph.sb("number", [1, 1], I32)
        psA = [ph.ps(f"psA{g}", [P, 512]) for g in range(B)]
        psB = [ph.ps(f"psB{g}", [P, 512]) for g in range(B)]
        psT = [ph.ps(f"psT{g}", [P, 512]) for g in range(B)]
        psM = ph.ps("psM", [P, 512])
        sem = ph.sem
        w_in = sem("w_in")
        xg_in = [[sem(f"xg_in{g}{s}") for s in range(2)] for g in range(B)]
        t_in = [[sem(f"t_in{g}{s}") for s in range(2)] for g in range(B)]
        outed = [[sem(f"outed{g}{s}") for s in range(2)] for g in range(B)]
        ends_in = sem("ends_in")
        per_group = ("ig_made o_made turned hi_ready hT_ready ig_added o_added i_ready g_ready o_ready ig_ready c_ready "
                     "tanh_ready h_ready hc_ready os_ready").split()
        q = [{n: sem(f"{n}{g}") for n in per_group} for g in range(B)]
        w_hi_ready, w_lo_ready, zeroed, started, gapped, gap_max, gap_turned, gap_most, judged, decided = (
            sem(n) for n in "w_hi_ready w_lo_ready zeroed started gapped gap_max gap_turned gap_most judged decided".split())
        seen = {e: sem(f"seen_{e}") for e in ("sp", "pe", "act", "dve", "pool")}
        start_at_head(nc, [d["os_ready"] for d in q], HEAD + L)
        start_at_head(nc, [v for l in t_in + outed for v in l], HEAD + L // 2 * 16)
        start_at_head(nc, [v for d in q for n, v in d.items() if n != "os_ready"] + [v for l in xg_in for v in l]
                      + [ends_in, zeroed, started, gapped, gap_max, gap_turned, gap_most, judged, decided])

        rows = lambda a: a.rearrange("b (n s) d -> b n s d", s=L)
        x_rows, t_rows, out_rows = rows(xg_d), rows(t2_d), rows(out.rearrange("b x y d -> b (x y) d"))

        def at(v, step):
            return v[:, bass.ds(step, 1), :].rearrange("n o d -> n (o d)")

        def runs(eng, name, run):
            run(0, False)
            eng.wait_ge(decided, HEAD + 1)
            with eng.While(lambda: eng.value_load(again[0:1, 0:1], min_val=0, max_val=1) > 0):
                k = eng.value_load(number[0:1, 0:1], min_val=1, max_val=P + 1)
                run(k, True)
                if name != "dve":
                    eng.wait_ge(decided, k + 1 + HEAD)
                    eng.sem_inc(seen[name], 1)

        def steps(eng, body, first=0):
            with eng.Fori(first, L // 2) as r:
                for s in range(2):
                    body(r * 2 + s, s, r)

        with nc.Block() as block:
            @block.sync
            def _(sp):
                def load(k, g, n, s, full):
                    sp.wait_ge(q[g]["o_added"], k * L + n - 1 + HEAD)
                    sp.dma_start(xg[:, g, s, :], at(x_rows[g], n)).then_inc(xg_in[g][s], 16)
                    if full:
                        sp.wait_ge(q[g]["os_ready"], k * L + n - 1 + HEAD)
                        sp.dma_start(tin[:, g, s, :], at(t_rows[g], n)).then_inc(t_in[g][s], 16)

                def save(k, g, n, s):
                    sp.wait_ge(q[g]["os_ready"], k * L + n + 1 + HEAD)
                    sp.dma_start(at(out_rows[g], n), os[:, g, s, :]).then_inc(outed[g][s], 16)

                def run(k, full):
                    for s in range(2):
                        for g in range(B):
                            load(k, g, s, s, full)
                    with sp.Fori(0, L // 2 - 1) as r:
                        for s in range(2):
                            for g in range(B):
                                if full:
                                    save(k, g, r * 2 + s, s)
                                load(k, g, r * 2 + s + 2, s, full)
                    if full:
                        for s in range(2):
                            for g in range(B):
                                save(k, g, L - 2 + s, s)
                    for g in range(B):
                        sp.wait_ge(q[g]["h_ready"], k * (L + 1) + L + 1 + HEAD)
                        for j, buf in enumerate((h, c)):
                            sp.dma_start(moved[1:P, j, g, :], buf[0:P - 1, g, :]).then_inc(ends_in, 16)
                    if full:
                        for g in range(B):
                            for s in range(2):
                                sp.wait_ge(outed[g][s], (k + 1) * (L // 2) * 16 + HEAD)
                                sp.sem_inc(seen["sp"], 1)

                sp.dma_start(ident[:, :], ident_d).then_inc(w_in, 16)
                for j in range(3):
                    sp.dma_start(w[:, :, j * D:(j + 1) * D], k_rows(v_d[j])).then_inc(w_in, 16)
                sp.wait_ge(zeroed, HEAD + 2)
                runs(sp, "sp", run)

            @block.tensor
            def _(pe):
                def turn(g):
                    for j in range(KT):
                        mm = pe.transpose(psT[g][:, j * P:(j + 1) * P], h[:, g, j * P:(j + 1) * P], ident[:, :])
                    mm.then_inc(q[g]["turned"], 1)

                def product(g, dst, lo, hi, done):
                    terms = [(a, b, j) for j in range(KT) for a, b in ((h_hi, w_hi), (h_hi, w_lo), (h_lo, w_hi))]
                    for i, (a, b, j) in enumerate(terms):
                        mm = pe.matmul(dst[:, 0:hi - lo], a[:, g, j, :], b[:, j, lo:hi], start=(i == 0), stop=(i == len(terms) - 1))
                    mm.then_inc(q[g][done], 1)

                def run(k, full):
                    def step(n, s, r):
                        for g in range(B):
                            o = 1 - g
                            pe.wait_ge(q[g]["hT_ready"], k * TURNS[g] + n + 1 + HEAD)
                            product(g, psA[g], 0, 512, "ig_made")
                            pe.wait_ge(q[o]["h_ready"], k * (L + 1) + n + (1, 2)[g] + HEAD)
                            turn(o)
                            product(g, psB[g], 512, GW, "o_made")

                    pe.wait_ge(q[0]["h_ready"], k * (L + 1) + 1 + HEAD)
                    turn(0)
                    steps(pe, step)
                    if full:
                        pe.wait_ge(gap_max, HEAD + k)
                        pe.transpose(psM[0:1, 0:P], most[:, :], ident[:, :]).then_inc(gap_turned, 1)

                pe.wait_ge(w_in, 64)
                pe.wait_ge(w_lo_ready, 1)
                runs(pe, "pe", run)

            @block.scalar
            def _(act):
                def run(k, full):
                    def tanh_c(g, n):
                        act.wait_ge(q[g]["c_ready"], k * (L + 1) + n + 2 + HEAD)
                        nc.scalar.activation(tc[:, g], c[:, g], ACT.Tanh).then_inc(q[g]["tanh_ready"], 1)

                    def keep_hi(g, n):
                        act.wait_ge(q[g]["turned"], k * TURNS[g] + n + 1 + HEAD)
                        nc.scalar.copy(h_hi[:, g], psT[g][:, 0:D].rearrange("p (k t) -> p k t", k=KT)).then_inc(q[g]["hi_ready"], 1)

                    def step(n, s, r, first=False):
                        for g in range(B):
                            o = 1 - g
                            if not (first and g == 0):
                                tanh_c(o, n - 1 + g)
                            keep_hi(o, n + g)
                            act.wait_ge(q[g]["ig_added"], k * L + n + 1 + HEAD)
                            nc.scalar.activation(gate[:, g, 0:D], z[:, g, 0:D], ACT.Sigmoid).then_inc(q[g]["i_ready"], 1)
                            nc.scalar.activation(gate[:, g, D:2 * D], z[:, g, D:2 * D], ACT.Tanh).then_inc(q[g]["g_ready"], 1)
                            act.wait_ge(q[g]["o_added"], k * L + n + 1 + HEAD)
                            nc.scalar.activation(gate[:, g, 2 * D:GW], z[:, g, 2 * D:GW], ACT.Sigmoid).then_inc(q[g]["o_ready"], 1)

                    keep_hi(0, 0)
                    step(0, 0, 0, first=True)
                    step(1, 1, 0)
                    steps(act, step, 1)
                    tanh_c(1, L - 1)

                runs(act, "act", run)

            @block.vector
            def _(dve):
                def run(k, full):
                    def cell(g, n):
                        dve.wait_ge(q[g]["hc_ready"], k * (L + 1) + n + 1 + HEAD)
                        dve.wait_ge(q[g]["ig_ready"], k * L + n + 1 + HEAD)
                        nc.vector.tensor_tensor(c[:, g], ig[:, g], hc[:, g], ALU.add).then_inc(q[g]["c_ready"], 1)
                        if full:
                            dve.wait_ge(q[g]["os_ready"], k * L + n + HEAD)
                        dve.wait_ge(q[g]["tanh_ready"], k * L + n + 1 + HEAD)
                        nc.vector.tensor_tensor(h[:, g], gate[:, g, 2 * D:GW], tc[:, g], ALU.mult).then_inc(q[g]["h_ready"], 1)

                    def keep_lo(g, n):
                        dve.wait_ge(q[g]["hi_ready"], k * TURNS[g] + n + 1 + HEAD)
                        nc.vector.tensor_tensor(h_lo[:, g], psT[g][:, 0:D].rearrange("p (k t) -> p k t", k=KT), h_hi[:, g],
                                                ALU.subtract).then_inc(q[g]["hT_ready"], 1)

                    def step(n, s, r, first=False):
                        for g in range(B):
                            o = 1 - g
                            if not (first and g == 0):
                                cell(o, n - 1 + g)
                            dve.wait_ge(xg_in[g][s], (k * (L // 2) + r + 1) * 16 + HEAD)
                            dve.wait_ge(q[g]["ig_made"], k * L + n + 1 + HEAD)
                            nc.vector.tensor_tensor(z[:, g, 0:512], psA[g][:, :], xg[:, g, s, 0:512], ALU.add).then_inc(q[g]["ig_added"], 1)
                            keep_lo(o, n + g)
                            dve.wait_ge(q[g]["o_made"], k * L + n + 1 + HEAD)
                            nc.vector.tensor_tensor(z[:, g, 512:GW], psB[g][:, 0:GW - 512], xg[:, g, s, 512:GW], ALU.add).then_inc(q[g]["o_added"], 1)
                            dve.wait_ge(q[g]["g_ready"], k * L + n + 1 + HEAD)
                            nc.vector.tensor_tensor(ig[:, g], gate[:, g, 0:D], gate[:, g, D:2 * D], ALU.mult).then_inc(q[g]["ig_ready"], 1)

                    for g in range(B):
                        dve.wait_ge(q[g]["hc_ready"], k * (L + 1) + HEAD)
                        dve.wait_ge(q[g]["os_ready"], k * L + HEAD)
                        nc.vector.tensor_copy(c[:, g], start[:, 1, g]).then_inc(q[g]["c_ready"], 1)
                        nc.vector.tensor_copy(h[:, g], start[:, 0, g]).then_inc(q[g]["h_ready"], 1)
                    keep_lo(0, 0)
                    step(0, 0, 0, first=True)
                    step(1, 1, 0)
                    steps(dve, step, 1)
                    cell(1, L - 1)

                    dve.wait_ge(ends_in, k * 64 + 64 + HEAD)
                    if full:
                        flat = "p j g d -> p (j g d)"
                        nc.vector.tensor_tensor(gap[:, :], moved[:, :, :, :].rearrange(flat), start[:, :, :, :].rearrange(flat),
                                                ALU.subtract).then_inc(gapped, 1)
                        dve.wait_ge(gapped, HEAD + k)
                        nc.vector.tensor_reduce(most[:, :], gap[:, :], AX_X, ALU.max, apply_absolute_value=True).then_inc(gap_max, 1)
                        dve.wait_ge(gap_max, HEAD + k)
                    nc.vector.tensor_copy(start[:, :, :, :], moved[:, :, :, :]).then_inc(started, 1)
                    if full:
                        dve.wait_ge(gap_turned, HEAD + k)
                        nc.vector.tensor_reduce(most1[:, :], psM[0:1, 0:P], AX_X, ALU.max).then_inc(gap_most, 1)
                        dve.wait_ge(gap_most, HEAD + k)
                        nc.vector.tensor_scalar(again[:, :], most1[:, :], SAME, None, ALU.is_gt)
                    else:
                        nc.vector.memset(again[:, :], 1)
                    dve.wait_ge(started, k + 2 + HEAD)
                    nc.vector.tensor_scalar(number[:, :], number[:, :], 1, None, ALU.add).then_inc(judged, 1)
                    dve.wait_ge(judged, k + 1 + HEAD)
                    dve.sem_inc(decided, 1)

                nc.vector.memset(start[:, :, :, :], 0.0).then_inc(started, 1)
                nc.vector.memset(number[:, :], 0).then_inc(zeroed, 1)
                nc.vector.memset(moved[:, :, :, :], 0.0).then_inc(zeroed, 1)
                dve.wait_ge(w_in, 64)
                nc.vector.tensor_copy(w_hi[:, :, :], w[:, :, :]).then_inc(w_hi_ready, 1)
                dve.wait_ge(w_hi_ready, 1)
                nc.vector.tensor_tensor(w_lo[:, :, :], w[:, :, :], w_hi[:, :, :], ALU.subtract).then_inc(w_lo_ready, 1)
                runs(dve, "dve", run)

            @block.gpsimd
            def _(pool):
                def run(k, full):
                    def product(g, n):
                        pool.wait_ge(q[g]["h_ready"], k * (L + 1) + n + 1 + HEAD)
                        nc.gpsimd.tensor_tensor(hc[:, g], h[:, g], c[:, g], ALU.mult).then_inc(q[g]["hc_ready"], 1)

                    def step(n, s, r):
                        for g in range(B):
                            product(g, n + 1)
                            if full:
                                pool.wait_ge(t_in[g][s], (k * (L // 2) + r + 1) * 16 + HEAD)
                                pool.wait_ge(outed[g][s], (k * (L // 2) + r) * 16 + HEAD)
                                nc.gpsimd.tensor_tensor(os[:, g, s], h[:, g], tin[:, g, s], ALU.add).then_inc(q[g]["os_ready"], 1)

                    for g in range(B):
                        product(g, 0)
                    steps(pool, step)

                runs(pool, "pool", run)


def constants():
    ident = np.eye(P, dtype=np.float32)
    sel = np.zeros((P, 4, 32), np.float32)
    mask = np.zeros((P, H), np.float32)
    for j in range(4):
        for xx in range(2):
            for h in range(H):
                p = 32 * j + 8 * xx + h
                mask[p, h] = 1.0
                for q in range(4):
                    sel[p, q, 8 * q + 2 * j + xx] = 1.0
    return {"ident": ident, "sel": sel, "mask": mask}


_L0 = ["W_lk", "W_rk", "W_lv", "W_rv", "W_out", "ln_agg_g", "ln_agg_b", "W1", "b1", "W2", "b2", "ln2_g", "ln2_b"]
_L1 = ["bq", "bk", "bv"]
_GATES = ["i", "c", "o"]


def build(nc, aps, out, kind):
    att = nc.dram_tensor("att", (B, N, N, H * N), F32, kind=kind).ap()
    o_d = nc.dram_tensor("o", (B, N // 2, 2 * N, D), F32, kind=kind).ap()
    t_d = nc.dram_tensor("t", (B, T, D), F32, kind=kind).ap()
    xlT_d = nc.dram_tensor("xlT", (KT, P, B * T), F32, kind=kind).ap()
    t2_d = nc.dram_tensor("t2", (B, T, D), F32, kind=kind).ap()
    xg_d = nc.dram_tensor("xg", (B, T, 3 * D), F32, kind=kind).ap()
    x, ident = aps["x"], aps["ident"]
    w = {n: aps["L0_conv_" + n] for n in _L0}
    for b in range(B):
        scores_phase(nc, b, x, w["W_lk"], w["W_rk"], ident, att)
    for b in range(B):
        mix_phase(nc, b, x, w["W_lv"], w["W_rv"], ident, aps["sel"], aps["mask"], att, o_d)
    dense_phase(nc, x, o_d, w["W_out"], w["ln_agg_g"], w["ln_agg_b"], w["W1"], w["b1"], w["W2"], w["b2"], w["ln2_g"], w["ln2_b"], ident, t_d, xlT_d)
    for b in range(B):
        attention_phase(nc, b, t_d, xlT_d, aps["WqT"], aps["L1_attn_bq"], aps["WkT"], aps["L1_attn_bk"], aps["WvT"], aps["L1_attn_bv"], ident, t2_d)
    gates_phase(nc, t2_d, [aps["L1_ffn_U_" + g] for g in _GATES], [aps["L1_ffn_b_" + g] for g in _GATES], ident, xg_d)
    recurrent_phase(nc, xg_d, [aps["L1_ffn_V_" + g] for g in _GATES], ident, t2_d, out)


def kernel(**inputs):
    import numpy as _np
    import concourse.bacc as _bacc
    from concourse import mybir as _mybir
    from concourse.bass_utils import run_bass_kernel_spmd as _run

    given = {n: _np.ascontiguousarray(inputs[n]) for n in ["x"] + ["L0_conv_" + n for n in _L0] + ["L1_attn_" + n for n in _L1]
             + ["L1_ffn_" + m + "_" + g for m in ("U", "V", "b") for g in _GATES]}
    for n in ("q", "k", "v"):
        given[f"W{n}T"] = _np.ascontiguousarray(inputs[f"L1_attn_W{n}"].T)
    given.update(constants())
    nc = _bacc.Bacc("TRN2", target_bir_lowering=False, num_devices=1)
    arrays, aps = {}, {}
    for name, a in given.items():
        arrays[f"in_{name}"] = a
        aps[name] = nc.dram_tensor(f"in_{name}", a.shape, _mybir.dt.from_np(a.dtype), kind="ExternalInput").ap()
    out = nc.dram_tensor("out_0", (B, N, N, D), _mybir.dt.float32, kind="ExternalOutput").ap()
    build(nc, aps, out, "Internal")
    r = _run(nc, [arrays], core_ids=[0])
    return r.results[0]["out_0"]
```
